# Optimizing a Trainium2 kernel written in Bass

```python
import numpy as np
import jax
import jax.numpy as jnp

def _softmax(x, axis=-1):
    return jax.nn.softmax(x, axis=axis)

def _gelu(x):
    return jax.nn.gelu(x, approximate=True)

def _silu(x):
    return jax.nn.silu(x)

def _sigmoid(x):
    return jax.nn.sigmoid(x)

def _layernorm(x, axis=-1, eps=1e-05):
    m = jnp.mean(x, axis=axis, keepdims=True)
    v = jnp.var(x, axis=axis, keepdims=True)
    return (x - m) / jnp.sqrt(v + eps)

def _scatter_add(tgt, idx, src, axis=0):
    return tgt.at[idx].add(src)

def _segment_sum(src, seg, n):
    return jax.ops.segment_sum(src, seg, n)
kernel_name = 'mk_macaron_d1_jaxref_r8_ea2aed'

def setup_inputs(seed: int=0):
    np.random.seed(seed)
    _w = jnp.asarray

    def _L0_attn_setup():
        import jax, jax.numpy as jnp
        import numpy as np
        from jax.scipy.linalg import solve_triangular
        H = 4
        CHUNK = 64
        NORM_EPS = 1e-05

        def _l2norm(x):
            return x / jnp.clip(jnp.linalg.norm(x, axis=-1, keepdims=True), 1e-12)

        def _deltanet_forward(hidden_states, conv_w, Wq, Wk, Wv, Wb, Wg, norm_w, Wo):
            B, L, D = hidden_states.shape
            Kc = conv_w.shape[1]
            dqh = Wq.shape[1] // H
            dvh = Wv.shape[1] // H
            xp = jnp.pad(hidden_states, ((0, 0), (Kc - 1, 0), (0, 0)))
            h = sum((conv_w[:, i] * xp[:, i:i + L, :] for i in range(Kc)))
            h = jax.nn.silu(h)
            q = (h @ Wq).reshape(B, L, H, dqh).transpose(0, 2, 1, 3)
            k = (h @ Wk).reshape(B, L, H, dqh).transpose(0, 2, 1, 3)
            v = (h @ Wv).reshape(B, L, H, dvh).transpose(0, 2, 1, 3)
            q = _l2norm(q)
            k = _l2norm(k)
            beta = jax.nn.sigmoid(h @ Wb).transpose(0, 2, 1)
            qm = q.reshape(B * H, L, dqh)
            km = k.reshape(B * H, L, dqh)
            vm = v.reshape(B * H, L, dvh)
            bm = beta.reshape(B * H, L)
            Nc = L // CHUNK
            eye = jnp.eye(CHUNK, dtype=q.dtype)

            def per_head(qh, kh, vh, bh):
                qs = qh.reshape(Nc, CHUNK, dqh)
                ks_ = kh.reshape(Nc, CHUNK, dqh)
                vs = vh.reshape(Nc, CHUNK, dvh)
                bs = bh.reshape(Nc, CHUNK)

                def step(S, xs):
                    qc, kc, vc, bc = xs
                    kb = kc * bc[:, None]
                    A = jnp.tril(kb @ kc.T, -1)
                    U = solve_triangular(eye + A, vc * bc[:, None] - kb @ S, lower=True)
                    o = qc @ S + jnp.tril(qc @ kc.T) @ U
                    return (S + kc.T @ U, o)
                S0 = jnp.zeros((dqh, dvh), qh.dtype)
                _, o = jax.lax.scan(step, S0, (qs, ks_, vs, bs))
                return o.reshape(L, dvh)
            o = jax.vmap(per_head)(qm, km, vm, bm)
            o = o.reshape(B, H, L, dvh).transpose(0, 2, 1, 3)
            g = (h @ Wg).reshape(B, L, H, dvh)
            rms = o * jax.lax.rsqrt(jnp.mean(o * o, axis=-1, keepdims=True) + NORM_EPS)
            out = rms * norm_w * (g * jax.nn.sigmoid(g))
            return out.reshape(B, L, H * dvh) @ Wo
        key = jax.random.key(seed)
        ks = jax.random.split(key, 9)
        B, L, D = (4, 512, 128)
        dk, dv = (64, 128)
        s = 0.02
        return {'hidden_states': jax.random.normal(ks[0], (B, L, D), jnp.float32), 'conv_w': jax.random.normal(ks[1], (D, 4), jnp.float32) * 0.2, 'Wq': jax.random.normal(ks[2], (D, dk), jnp.float32) * s, 'Wk': jax.random.normal(ks[3], (D, dk), jnp.float32) * s, 'Wv': jax.random.normal(ks[4], (D, dv), jnp.float32) * s, 'Wb': jax.random.normal(ks[5], (D, H), jnp.float32) * s, 'Wg': jax.random.normal(ks[6], (D, dv), jnp.float32) * s, 'norm_w': jnp.ones((dv // H,), jnp.float32), 'Wo': jax.random.normal(ks[7], (dv, D), jnp.float32) * s}
    _L0_attn_in = _L0_attn_setup()

    def _L0_ffn_setup():
        import jax, jax.numpy as jnp
        import numpy as np
        B, T, DIM = (2, 256, 128)
        H, DH, E, K = (16, 64, 8, 2)
        key = jax.random.key(seed)
        ks = jax.random.split(key, 7)
        s = 0.02
        return {'x': jax.random.normal(ks[0], (B, T, DIM), jnp.float32), 'Wq': jax.random.normal(ks[1], (H, DH, DIM), jnp.float32) * s, 'Wk': jax.random.normal(ks[2], (H, DH, DIM), jnp.float32) * s, 'Wv': jax.random.normal(ks[3], (E, DH, DIM), jnp.float32) * s, 'Ws': jax.random.normal(ks[4], (H, E, DIM), jnp.float32) * s, 'Wd': jax.random.normal(ks[5], (H, E, DIM), jnp.float32) * s, 'Wo': jax.random.normal(ks[6], (E, DIM, DH), jnp.float32) * s}
    _L0_ffn_in = _L0_ffn_setup()
    _d = {'L0_attn_hidden_states': _L0_attn_in['hidden_states'], 'L0_attn_conv_w': _L0_attn_in['conv_w'], 'L0_attn_Wq': _L0_attn_in['Wq'], 'L0_attn_Wk': _L0_attn_in['Wk'], 'L0_attn_Wv': _L0_attn_in['Wv'], 'L0_attn_Wb': _L0_attn_in['Wb'], 'L0_attn_Wg': _L0_attn_in['Wg'], 'L0_attn_norm_w': _L0_attn_in['norm_w'], 'L0_attn_Wo': _L0_attn_in['Wo'], 'L0_ffn_Wq': _L0_ffn_in['Wq'], 'L0_ffn_Wk': _L0_ffn_in['Wk'], 'L0_ffn_Wv': _L0_ffn_in['Wv'], 'L0_ffn_Ws': _L0_ffn_in['Ws'], 'L0_ffn_Wd': _L0_ffn_in['Wd'], 'L0_ffn_Wo': _L0_ffn_in['Wo']}
    _x0 = _d['L0_attn_hidden_states']
    _d['L0_attn_hidden_states'] = jax.random.normal(jax.random.fold_in(jax.random.key(seed), 1), (8, 256, 128), dtype=_x0.dtype)
    del _x0
    return _d

def reference(L0_attn_hidden_states, L0_attn_conv_w, L0_attn_Wq, L0_attn_Wk, L0_attn_Wv, L0_attn_Wb, L0_attn_Wg, L0_attn_norm_w, L0_attn_Wo, L0_ffn_Wq, L0_ffn_Wk, L0_ffn_Wv, L0_ffn_Ws, L0_ffn_Wd, L0_ffn_Wo):

    def _L0_attn_ref(hidden_states, conv_w, Wq, Wk, Wv, Wb, Wg, norm_w, Wo):
        import jax, jax.numpy as jnp
        import numpy as np
        from jax.scipy.linalg import solve_triangular
        H = 4
        CHUNK = 64
        NORM_EPS = 1e-05

        def _l2norm(x):
            return x / jnp.clip(jnp.linalg.norm(x, axis=-1, keepdims=True), 1e-12)

        def _deltanet_forward(hidden_states, conv_w, Wq, Wk, Wv, Wb, Wg, norm_w, Wo):
            B, L, D = hidden_states.shape
            Kc = conv_w.shape[1]
            dqh = Wq.shape[1] // H
            dvh = Wv.shape[1] // H
            xp = jnp.pad(hidden_states, ((0, 0), (Kc - 1, 0), (0, 0)))
            h = sum((conv_w[:, i] * xp[:, i:i + L, :] for i in range(Kc)))
            h = jax.nn.silu(h)
            q = (h @ Wq).reshape(B, L, H, dqh).transpose(0, 2, 1, 3)
            k = (h @ Wk).reshape(B, L, H, dqh).transpose(0, 2, 1, 3)
            v = (h @ Wv).reshape(B, L, H, dvh).transpose(0, 2, 1, 3)
            q = _l2norm(q)
            k = _l2norm(k)
            beta = jax.nn.sigmoid(h @ Wb).transpose(0, 2, 1)
            qm = q.reshape(B * H, L, dqh)
            km = k.reshape(B * H, L, dqh)
            vm = v.reshape(B * H, L, dvh)
            bm = beta.reshape(B * H, L)
            Nc = L // CHUNK
            eye = jnp.eye(CHUNK, dtype=q.dtype)

            def per_head(qh, kh, vh, bh):
                qs = qh.reshape(Nc, CHUNK, dqh)
                ks_ = kh.reshape(Nc, CHUNK, dqh)
                vs = vh.reshape(Nc, CHUNK, dvh)
                bs = bh.reshape(Nc, CHUNK)

                def step(S, xs):
                    qc, kc, vc, bc = xs
                    kb = kc * bc[:, None]
                    A = jnp.tril(kb @ kc.T, -1)
                    U = solve_triangular(eye + A, vc * bc[:, None] - kb @ S, lower=True)
                    o = qc @ S + jnp.tril(qc @ kc.T) @ U
                    return (S + kc.T @ U, o)
                S0 = jnp.zeros((dqh, dvh), qh.dtype)
                _, o = jax.lax.scan(step, S0, (qs, ks_, vs, bs))
                return o.reshape(L, dvh)
            o = jax.vmap(per_head)(qm, km, vm, bm)
            o = o.reshape(B, H, L, dvh).transpose(0, 2, 1, 3)
            g = (h @ Wg).reshape(B, L, H, dvh)
            rms = o * jax.lax.rsqrt(jnp.mean(o * o, axis=-1, keepdims=True) + NORM_EPS)
            out = rms * norm_w * (g * jax.nn.sigmoid(g))
            return out.reshape(B, L, H * dvh) @ Wo
        return _deltanet_forward(hidden_states, conv_w, Wq, Wk, Wv, Wb, Wg, norm_w, Wo)

    def _L0_ffn_ref(x, Wq, Wk, Wv, Ws, Wd, Wo):
        import jax, jax.numpy as jnp
        import numpy as np
        B, T, DIM = (2, 256, 128)
        H, DH, E, K = (16, 64, 8, 2)
        scale = DH ** (-0.5)
        q = jnp.einsum('btc,hdc->bhtd', x, Wq)
        k = jnp.einsum('btc,hdc->bhtd', x, Wk)
        gate_v = jnp.einsum('btc,hec->bthe', x, Ws)
        w, sel = jax.lax.top_k(gate_v, K)
        wsig = jax.nn.sigmoid(w)
        oh = jax.nn.one_hot(sel, E, dtype=x.dtype)
        mix_v = jnp.einsum('bthk,bthke->bthe', wsig, oh)
        proj_v = jnp.einsum('btc,edc->bted', x, Wv)
        v = jnp.einsum('bthe,bted->bhtd', mix_v, proj_v)
        scores = jnp.einsum('bhid,bhjd->bhij', q * scale, k)
        probs = jax.nn.softmax(scores, axis=-1)
        attn = jnp.einsum('bhij,bhjd->bihd', probs, v)
        gate_o = jnp.einsum('btc,hec->bthe', x, Wd)
        _, sel_o = jax.lax.top_k(gate_o, K)
        mask_o = jax.nn.one_hot(sel_o, E, dtype=x.dtype).sum(axis=3)
        res = jnp.einsum('bthe,bthd,efd->bthf', mask_o, attn, Wo)
        return res.sum(axis=2)
    x = L0_attn_hidden_states
    x = x + 0.5 * _L0_ffn_ref(_layernorm(x, axis=-1), L0_ffn_Wq, L0_ffn_Wk, L0_ffn_Wv, L0_ffn_Ws, L0_ffn_Wd, L0_ffn_Wo)
    x = x + _L0_attn_ref(_layernorm(x, axis=-1), L0_attn_conv_w, L0_attn_Wq, L0_attn_Wk, L0_attn_Wv, L0_attn_Wb, L0_attn_Wg, L0_attn_norm_w, L0_attn_Wo)
    x = x + 0.5 * _L0_ffn_ref(_layernorm(x, axis=-1), L0_ffn_Wq, L0_ffn_Wk, L0_ffn_Wv, L0_ffn_Ws, L0_ffn_Wd, L0_ffn_Wo)
    return x

_drawn_inputs = setup_inputs


def setup_inputs(seed=0):
    import zlib

    import numpy as np

    out = dict(_drawn_inputs(seed))
    spreads = {'L0_attn_norm_w': (1.0, 0.6)}
    factors = {'L0_attn_conv_w': 8.0,
     'L0_attn_Wq': 8.0,
     'L0_attn_Wk': 8.0,
     'L0_attn_Wv': 8.0,
     'L0_attn_Wb': 8.0,
     'L0_attn_Wg': 8.0,
     'L0_attn_Wo': 8.0,
     'L0_ffn_Wq': 8.0,
     'L0_ffn_Wk': 8.0,
     'L0_ffn_Wv': 3.478,
     'L0_ffn_Ws': 4.405,
     'L0_ffn_Wd': 4.921,
     'L0_ffn_Wo': 3.427}
    for name, (base, spread) in spreads.items():
        noise = np.random.default_rng([zlib.crc32(name.encode()), seed]).standard_normal(out[name].shape)
        drawn = base * np.exp(spread * noise) if base else spread * noise
        out[name] = jnp.asarray(drawn.astype(out[name].dtype))
    for name, factor in factors.items():
        out[name] = (out[name] * factor).astype(out[name].dtype)
    return out
```

```python
import concourse.bass as bass
from concourse import mybir
from contextlib import ExitStack

F32 = mybir.dt.float32
F32R = mybir.dt.float32r
ALU = mybir.AluOpType
ACT = mybir.ActivationFunctionType
X = mybir.AxisListType.X

B, L, C = 8, 256, 128
P = 128
NT = L // P
H, DH, E = 16, 64, 8
NQ, NL = 4, 32
DV1 = DH + 1
NPAIR = H * DH // P
HD, DK, DV, CH = 4, 16, 32, 64
DP = 32
LEVELS = 6
NEG_BIG = -3.0e38
CONSTS, POOL_STEPS, DVE_FFN, DVE_DELTA, MASKS = 14, 6, 20, 24, 10
PHASES = 3
EPS = 1e-5

SETUP_JOBS = [(f"w{j}", j % 2) for j in range(8)]
FFN_JOBS = ([("xT", 0), ("gate", 1), ("pv0", 0), ("pv1", 1)]
            + [(f"qk{j}", j % 2) for j in range(8)]
            + [("mT", 0)] + [(f"vmix{j}", (j + 1) % 2) for j in range(4)]
            + [(f"omix{j}", (j + 1) % 2) for j in range(4)] + [("res", 1)]
            + [(f"S{h}", 2 + h % 2) for h in range(H)]
            + [(f"ST{h}", 4 + h % 2) for h in range(H)]
            + [(f"at{g}", 6 + g % 2) for g in range(H // 2)])


DELTA_JOBS = ([("xT", 0), ("proj0", 1), ("proj1", 2), ("tq0", 3), ("tq1", 4)]
              + [(f"gram0{h}", (5 + h) % 8) for h in range(HD)] + [(f"gram1{h}", 1 + h) for h in range(HD)]
              + [(f"{w}{k}{t}", 2 * b + t) for k in range(1, LEVELS) for b, w in enumerate("TUV") for t in range(NT)
                 if w != "U" or k < LEVELS - 1]
              + [("WT", 6), ("Uv", 7)]
              + [("ws1", 0), ("S1", 2), ("ws2", 1), ("S2", 2), ("ws3", 0), ("S3", 2)]
              + [("o0", 3), ("o1", 4), ("yT", 5), ("fin", 6)])


class Chain:

    def __init__(self, eng, sem):
        self.eng, self.sem, self.base, self.i, self.per, self.n = eng, sem, 0, 0, 0, 0

    def loop(self, i, per):
        self.base, self.i, self.per, self.n = self.base + self.n, i, per, 0

    def end(self, times):
        assert self.n == self.per, self.n
        self.base, self.i, self.per, self.n = self.base + times * self.per, 0, 0, 0

    def link(self, ins):
        self.n += 1
        ins.then_inc(self.sem, 1)
        self.eng.wait_ge(self.sem, self.i * self.per + (self.base + self.n))


class Jobs:

    def __init__(self, jobs, base, times):
        self.base, self.per, self.at = dict(base), {b: 0 for b in range(8)}, {}
        for name, bank in jobs:
            self.at[name] = (bank, self.per[bank])
            self.per[bank] += 1
        self.end = {b: base[b] + times * self.per[b] for b in range(8)}

    def bank(self, name):
        return self.at[name][0]

    def before(self, name, i):
        bank, k = self.at[name]
        return i * self.per[bank] + (self.base[bank] + k)

    def done(self, name, i):
        bank, k = self.at[name]
        return i * self.per[bank] + (self.base[bank] + k + 1)


def build(nc, hid, conv_w, dWq, dWk, dWv, dWb, dWg, norm_w, dWo, fWq, fWk, fWv, fWs, fWd, fWo, out):
    with ExitStack() as ctx:
        def sb(name, shape, dt=F32):
            return ctx.enter_context(nc.sbuf_tensor(name, shape, dt))

        def sem(name):
            return ctx.enter_context(nc.semaphore(name))

        ident = sb("ident", [P, P])
        own16 = sb("own16", [P, 8])
        neg_half16 = sb("neg_half16", [P, NT * 2 * HD])
        tie = sb("tie", [P, E])
        self_f = sb("self_f", [P, H, P])
        sel = sb("sel", [P, H, P], F32R)
        wst = sb("wst", [P, 22, C])
        wost = sb("wost", [P, E, DH])
        WTh = sb("WTh", [P, 16, P], F32R)
        WTl = sb("WTl", [P, 16, P], F32R)
        WvT = sb("WvT", [P, 4 * P])
        WgT = sb("WgT", [P, 2 * P])
        WoT = sb("WoT", [DH, E, P])
        x = sb("x", [P, B * NT, C])
        stat = sb("stat", [P, NT, 6])
        mv = sb("mv", [P, NT, 4])
        mean = sb("mean", [P, NT])
        vare = sb("vare", [P, NT])
        rstd = sb("rstd", [P, NT])
        xn = sb("xn", [P, NT, C])
        xT = sb("xT", [P, L])
        xTh = sb("xTh", [P, L], F32R)
        xTl = sb("xTl", [P, L], F32R)
        gate = sb("gate", [P, 64, E])
        egate = sb("egate", [P, NT, H, E])
        gdif = sb("gdif", [P, 64, E])
        gsel = sb("gsel", [P, 64, E])
        gsel2 = sb("gsel2", [P, 64, E])
        gmax = sb("gmax", [P, 64])
        grank = sb("grank", [P, 64])
        mask = sb("mask", [P, NT, 2, H, E])
        sig = sb("sig", [P, NT, H, E])
        mix = sb("mix", [P, H, NT, E, 2])
        mixT = sb("mixT", [P, H, NL])
        bdv = sb("bdv", [P, NL, 8, H])
        pv = sb("pv", [P, NT, E, 2, DH])
        pvT = sb("pvT", [P, NL, DH])
        vm = sb("vm", [P, NL, DH])
        v = sb("v", [P, NT * H, DV1])
        qk = {(w, part): sb(f"{w}{part}", [P, NPAIR, L], F32R) for w in "qk" for part in "hl"}
        negm = sb("negm", [P, NT, H])
        nmT = sb("nmT", [P, L], F32R)
        PT = sb("PT", [P, 4, NT, L])
        attn = sb("attn", [P, NT, H, DV1])
        rden = sb("rden", [P, NT * H])
        maskw = sb("maskw", [P, E, NT * H])
        maskT = sb("maskT", [P, E, NL])
        bdo = sb("bdo", [P, NL, 8, E])
        aT = sb("aT", [P, NL, DH])
        yT = sb("yT", [DH, NT, E, NQ, NL])

        convw = sb("convw", [P, 4])
        normw = sb("normw", [P, DV])
        dW = sb("dW", [P, 2 * HD * DK + 2 * HD * DV + HD])
        dWo_sb = sb("dWo_sb", [P, C])

        def over(tensor, at, *shape):
            n = 1
            for m in shape:
                n *= m
            names = "abcd"[:len(shape)]
            return tensor[:, at:at + n].rearrange(f"p ({' '.join(names)}) -> p {' '.join(names)}", **dict(zip(names, shape)))

        f_bdv = bdv[:, :, :, :].rearrange("p l m h -> p (l m h)")
        f_aT = aT[:, :, :].rearrange("p l d -> p (l d)")
        f_bdo = bdo[:, :, :, :].rearrange("p l m e -> p (l m e)")
        f_PT = PT[:, :, :, :].rearrange("p a n t -> p (a n t)")
        f_attn = attn[:, :, :, :].rearrange("p n h d -> p (n h d)")
        f_vm = vm[:, :, :].rearrange("p l d -> p (l d)")
        f_self = self_f[:, :, :].rearrange("p h m -> p (h m)")
        AA = over(f_bdv, 0, NT * HD, 3, P)
        XX = over(f_aT, 0, NT * HD, 2, P)
        TT = over(f_bdo, 0, NT, HD, P)
        WT = over(f_bdo, 1024, L)
        Uv = over(f_bdo, 1280, NT, P)
        U = over(f_bdo, 1536, NT, P)
        St = over(f_PT, 1536, 4, P)
        qkp = over(f_PT, 0, NT, 3, HD, DP)
        qkT = over(f_PT, 768, NT, 3, P)
        NPR = 2 * HD * DK + 2 * HD * DV + HD
        pr = over(f_attn, 0, NT, NPR)
        o_sb = over(f_attn, 800, NT, P)
        osq = over(f_attn, 1056, NT, P)
        y = over(f_attn, 1312, NT, P)
        yT_d = over(f_attn, 1568, L)
        vb = over(f_attn, 1824, NT, P)
        xpad = over(f_vm, 0, L + 3)
        hacc = over(f_vm, 260, L)
        hexp = over(f_vm, 516, L)
        hT = over(f_vm, 772, L)
        sqs = over(f_vm, 1028, NT, 2 * HD * DK)
        sg = over(f_vm, 1284, NT, HD * DV + HD)
        gn = over(f_vm, 1548, NT, P)
        ss = over(f_vm, 1804, NT, 2 * HD)
        rn = over(f_vm, 1820, NT, 2 * HD)
        ms = over(f_vm, 1836, NT, HD)
        rr = over(f_vm, 1844, NT, HD)
        msc = over(f_vm, 1852, NT, HD)
        m3 = over(f_self, 0, 3, P)
        m0 = over(f_self, 384, 2, P)
        mlev = over(f_self, 640, LEVELS - 1, P)
        mhead = over(f_self, 1280, P)

        bank = [ctx.enter_context(nc.psum_tensor(f"bank{b}", [P, 512], F32)) for b in range(8)]
        full = [sem(f"full{b}") for b in range(8)]
        free = [sem(f"free{b}") for b in range(8)]

        hid_in = sem("hid_in")
        w_in = sem("w_in")
        const_done = sem("const_done")
        wT_hi = sem("wT_hi")
        dve_step = sem("dve_step")
        pool_step = sem("pool_step")
        var_ready = sem("var_ready")
        rstd_ready = sem("rstd_ready")
        xn_ready = sem("xn_ready")
        xlo_ready = sem("xlo_ready")
        egate_ready = sem("egate_ready")
        mixT_ready = sem("mixT_ready")
        bdv_ready = sem("bdv_ready")
        pvT_ready = sem("pvT_ready")
        qkhi_ready = sem("qkhi_ready")
        v_ready = sem("v_ready")
        maskT_ready = sem("maskT_ready")
        bdo_ready = sem("bdo_ready")
        aT_ready = sem("aT_ready")
        masks_done = sem("masks_done")
        dw_in = sem("dw_in")
        sel_ready = sem("sel_ready")
        act_step = sem("act_step")
        conv_ready = sem("conv_ready")
        hexp_ready = sem("hexp_ready")
        hT_ready = sem("hT_ready")
        ss_ready = sem("ss_ready")
        rn_ready = sem("rn_ready")
        gexp_ready = sem("gexp_ready")
        qkp_ready = sem("qkp_ready")
        X0_ready = sem("X0_ready")
        U_ready = sem("U_ready")
        ms_ready = sem("ms_ready")
        rr_ready = sem("rr_ready")
        y_ready = sem("y_ready")
        stored = sem("stored")

        base = {b: 0 for b in range(8)}
        setup = Jobs(SETUP_JOBS, base, 1)
        ffn = [Jobs(FFN_JOBS, setup.end, B)]
        delta = Jobs(DELTA_JOBS, ffn[0].end, B)
        ffn.append(Jobs(FFN_JOBS, delta.end, B))
        CREDIT = {b: 0 if b < 2 else 1 for b in range(8)}

        def turn(eng, jobs, name, i):
            b = jobs.bank(name)
            n = jobs.before(name, i) + CREDIT[b]
            if isinstance(n, int) and n == 0:
                return
            eng.wait_ge(free[b], n)

        def filled(eng, jobs, name, i):
            eng.wait_ge(full[jobs.bank(name)], jobs.done(name, i))

        def moved(eng, jobs, name, i):
            b = jobs.bank(name)
            eng.wait_ge(free[b], jobs.done(name, i) + CREDIT[b])

        def heads(h, part):
            return slice(DH * (h % 2), DH * (h % 2) + DH)

        block = ctx.enter_context(nc.Block())

        @block.sync
        def _(sp):
            sp.dma_start(x[:, :, :], hid.rearrange("b (n p) c -> p (b n) c", p=P)).then_inc(hid_in, 16)
            sp.dma_start(wst[:, 0:8, :], fWq.rearrange("h d c -> (h d) c").rearrange("(n p) c -> p n c", p=P)).then_inc(w_in, 16)
            sp.dma_start(wst[:, 8:16, :], fWk.rearrange("h d c -> (h d) c").rearrange("(n p) c -> p n c", p=P)).then_inc(w_in, 16)
            sp.dma_start(wst[:, 16:20, :], fWv.rearrange("h d c -> (h d) c").rearrange("(n p) c -> p n c", p=P)).then_inc(w_in, 16)
            sp.dma_start(wst[:, 20, :], fWs.rearrange("h e c -> (h e) c")).then_inc(w_in, 16)
            sp.dma_start(wst[:, 21, :], fWd.rearrange("h e c -> (h e) c")).then_inc(w_in, 16)
            sp.dma_start(wost[:, :, :], fWo.rearrange("e f d -> f e d")).then_inc(w_in, 16)
            sp.dma_start(convw[:, :], conv_w).then_inc(dw_in, 16)
            sp.dma_start(normw[:, :], norm_w.unsqueeze(0).to_broadcast([P, DV])).then_inc(dw_in, 16)
            at = 0
            for w in (dWq, dWk, dWv, dWg, dWb):
                sp.dma_start(dW[:, at:at + w.shape[1]], w).then_inc(dw_in, 16)
                at += w.shape[1]
            sp.dma_start(dWo_sb[:, :], dWo).then_inc(dw_in, 16)
            if PHASES == 1:
                moved(sp, ffn[0], "res", B - 1)
            elif PHASES == 2:
                moved(sp, delta, "fin", B - 1)
            else:
                moved(sp, ffn[1], "res", B - 1)
            sp.dma_start(out.rearrange("b (n p) c -> p (b n) c", p=P), x[:, :, :]).then_inc(stored, 16)
            sp.wait_ge(stored, 16)

        @block.gpsimd
        def _(pool):
            step = Chain(pool, pool_step)
            pool.memset(neg_half16[:, :], -0.5).then_inc(const_done, 1)
            for e in range(E):
                pool.memset(tie[:, e:e + 1], float(E - e)).then_inc(const_done, 1)
            step.link(pool.memset(ident[:, :], 0.0))
            pool.affine_select(out=ident[:, :], in_=ident[:, :], compare_op=ALU.not_equal, fill=1.0,
                               base=0, pattern=[[-1, P]], channel_multiplier=1).then_inc(const_done, 1)
            step.link(pool.memset(own16[:, :], 1.0))
            step.link(pool.affine_select(out=own16[:, :], in_=own16[:, :], compare_op=ALU.is_ge, fill=0.0,
                                         base=0, pattern=[[-16, 8]], channel_multiplier=1))
            step.link(pool.affine_select(out=own16[:, :], in_=own16[:, :], compare_op=ALU.is_ge, fill=0.0,
                                         base=15, pattern=[[16, 8]], channel_multiplier=-1))
            step.link(pool.memset(self_f[:, :, :], 0.0))
            for first in (0, DH):
                step.link(pool.affine_select(out=self_f[:, :, :], in_=self_f[:, :, :], compare_op=ALU.not_equal,
                                             fill=1.0, base=-first, pattern=[[-1, H], [0, P]], channel_multiplier=1))
            pool.memset(mix[:, :, :, :, :], 0.0).then_inc(const_done, 1)
            pool.memset(pv[:, :, :, :, :], 0.0).then_inc(const_done, 1)
            pool.memset(v[:, :, DH:DV1], 1.0).then_inc(const_done, 1)
            pool.memset(nmT[:, :].bitcast(F32), 0.0).then_inc(const_done, 1)

            pool.wait_ge(sel_ready, 1)

            def keep(ap, base, pattern, channel, last=False):
                ins = pool.affine_select(out=ap, in_=ap, compare_op=ALU.is_ge, fill=0.0, base=base, pattern=pattern,
                                         channel_multiplier=channel)
                if last:
                    ins.then_inc(masks_done, 1)
                else:
                    step.link(ins)

            step.link(pool.memset(m3[:, :, :], 1.0))
            step.link(pool.memset(m3[CH:P, 0, 0:CH], 0.0))
            step.link(pool.memset(m3[0:CH, 1:3, CH:P], 0.0))
            keep(m3[:, 0, :], -1, [[-1, P]], 1, True)
            keep(m3[:, 1, :], -1, [[1, P]], -1, True)
            keep(m3[:, 2, :], 0, [[1, P]], -1, True)
            step.link(pool.memset(mhead, 1.0))
            keep(mhead, 0, [[-DP, HD], [0, DV]], 1)
            keep(mhead, DP - 1, [[DP, HD], [0, DV]], -1, True)
            for k in range(LEVELS):
                s, mask_k = 1 << k, m0[:, 0, :] if k == 0 else mlev[:, k - 1, :]
                halves = mask_k.rearrange("p (n two s) -> p n two s", two=2, s=s)
                step.link(pool.memset(mask_k, 1.0))
                step.link(pool.memset(halves[:, :, 1, :], 0.0))
                keep(halves[:, :, 0, :], -s, [[-2 * s, P // (2 * s)], [0, s]], 1)
                keep(halves[:, :, 0, :], 2 * s - 1, [[2 * s, P // (2 * s)], [0, s]], -1, k > 0)
            step.link(pool.memset(m0[:, 1, :], 0.0))
            odd = m0[:, 1, :].rearrange("p (n two) -> p n two", two=2)[:, :, 1]
            pool.affine_select(out=odd, in_=odd, compare_op=ALU.not_equal, fill=1.0, base=0,
                               pattern=[[-2, P // 2]], channel_multiplier=1).then_inc(masks_done, 1)

            def delta_entry(i):
                pool.wait_ge(var_ready, i + (B + 1))
                pool.tensor_tensor(rstd[:, :], vare[:, :], neg_half16[:, 0:NT], ALU.pow).then_inc(rstd_ready, 1)
                pool.wait_ge(ss_ready, i + 1)
                pool.tensor_tensor(rn[:, :, :], ss[:, :, :], neg_half16[:, :].rearrange("p (n g) -> p n g", n=NT),
                                   ALU.pow).then_inc(rn_ready, 1)
                pool.wait_ge(ms_ready, i + 1)
                pool.tensor_tensor(rr[:, :, :], ms[:, :, :], neg_half16[:, 0:NT * HD].rearrange("p (n g) -> p n g", n=NT),
                                   ALU.pow).then_inc(rr_ready, 1)

            def ffn_entry(i, n, ln):
                pool.wait_ge(var_ready, ln + 1)
                pool.tensor_tensor(rstd[:, :], vare[:, :], neg_half16[:, 0:NT], ALU.pow).then_inc(rstd_ready, 1)
                pool.wait_ge(mixT_ready, n + 1)
                pool.tensor_tensor(bdv[:, :, :, :],
                                   mixT[:, :, :].rearrange("p h l -> p l h").unsqueeze(2).to_broadcast([P, NL, 8, H]),
                                   own16[:, :].unsqueeze(1).unsqueeze(3).to_broadcast([P, NL, 8, H]),
                                   ALU.mult).then_inc(bdv_ready, 1)
                pool.wait_ge(maskT_ready, n + 1)
                pool.tensor_tensor(bdo[:, :, :, :],
                                   maskT[:, :, :].rearrange("p e l -> p l e").unsqueeze(2).to_broadcast([P, NL, 8, E]),
                                   own16[:, :].unsqueeze(1).unsqueeze(3).to_broadcast([P, NL, 8, E]),
                                   ALU.mult).then_inc(bdo_ready, 1)

            with pool.Fori(0, B) as i:
                ffn_entry(i, i, i)
            if PHASES > 1:
                with pool.Fori(0, B) as i:
                    delta_entry(i)
            if PHASES > 2:
                with pool.Fori(0, B) as i:
                    ffn_entry(i, i + B, i + 2 * B)

        @block.vector
        def _(dve):
            step = Chain(dve, dve_step)
            dve.wait_ge(const_done, CONSTS)
            dve.wait_ge(pool_step, POOL_STEPS)
            dve.tensor_copy(sel[:, :, :], self_f[:, :, :]).then_inc(sel_ready, 1)
            for b in range(2, 8):
                dve.sem_inc(free[b], 1)
            for j in range(4):
                dve.wait_ge(wT_hi, j + 1)
                dve.tensor_tensor(WTl[:, 4 * j:4 * j + 4, :], bank[j % 2][:, :].rearrange("p (n c) -> p n c", c=P),
                                  WTh[:, 4 * j:4 * j + 4, :].bitcast(F32), ALU.subtract).then_inc(free[j % 2], 1)

            def layer_stats(i):
                for t in range(NT):
                    last = dve.bn_stats(stat[:, t, :], x[:, bass.ds(i * NT + t, 1), :].rearrange("p a c -> p (a c)"))
                step.link(last)
                dve.tensor_tensor(mv[:, :, 0], stat[:, :, 1], stat[:, :, 4], ALU.add)
                dve.tensor_tensor(mv[:, :, 1], stat[:, :, 1], stat[:, :, 4], ALU.subtract)
                step.link(dve.tensor_tensor(mv[:, :, 2], stat[:, :, 2], stat[:, :, 5], ALU.add))
                dve.tensor_scalar(mean[:, :], mv[:, :, 0], 0.5, None, ALU.mult)
                dve.scalar_tensor_tensor(mv[:, :, 3], mv[:, :, 1], 0.25, mv[:, :, 1], ALU.mult, ALU.mult)
                step.link(dve.tensor_scalar(mv[:, :, 2], mv[:, :, 2], 1.0 / C, EPS, ALU.mult, ALU.add))
                dve.tensor_tensor(vare[:, :], mv[:, :, 2], mv[:, :, 3], ALU.add).then_inc(var_ready, 1)

            def normalize(i, ln):
                dve.wait_ge(rstd_ready, ln + 1)
                for t in range(NT):
                    dve.tensor_scalar(xn[:, t, :], x[:, bass.ds(i * NT + t, 1), :].rearrange("p a c -> p (a c)"),
                                      mean[:, t:t + 1], rstd[:, t:t + 1], ALU.subtract, ALU.mult).then_inc(xn_ready, 1)

            def delta_entry(jobs, i):
                def heads_over(ap, width):
                    return ap.unsqueeze(3).to_broadcast([P, NT, HD, width])

                def by_head(ap, width):
                    return ap.rearrange("p n (h d) -> p n h d", d=width)

                layer_stats(i)
                normalize(i, i + B)
                moved(dve, jobs, "xT", i)
                step.link(dve.tensor_scalar(hacc[:, :], xpad[:, 3:3 + L], convw[:, 3:4], None, ALU.mult))
                for k in (2, 1):
                    step.link(dve.scalar_tensor_tensor(hacc[:, :], xpad[:, k:k + L], convw[:, k:k + 1], hacc[:, :], ALU.mult, ALU.add))
                dve.scalar_tensor_tensor(hacc[:, :], xpad[:, 0:L], convw[:, 0:1], hacc[:, :], ALU.mult, ALU.add).then_inc(conv_ready, 1)
                dve.wait_ge(hexp_ready, i + 1)
                step.link(dve.tensor_scalar(hexp[:, :], hexp[:, :], 1.0, None, ALU.add))
                step.link(dve.reciprocal(hexp[:, :], hexp[:, :]))
                dve.tensor_tensor(hT[:, :], hacc[:, :], hexp[:, :], ALU.mult).then_inc(hT_ready, 1)
                moved(dve, jobs, "proj0", i)
                moved(dve, jobs, "proj1", i)
                qk_w = 2 * HD * DK
                step.link(dve.tensor_tensor(sqs[:, :, :], pr[:, :, 0:qk_w], pr[:, :, 0:qk_w], ALU.mult))
                step.link(dve.tensor_reduce(ss[:, :, :], sqs[:, :, :].rearrange("p n (g d) -> p n g d", d=DK), X, ALU.add))
                dve.tensor_scalar(ss[:, :, :], ss[:, :, :], 1e-24, None, ALU.max).then_inc(ss_ready, 1)
                dve.wait_ge(gexp_ready, i + 1)
                step.link(dve.tensor_scalar(sg[:, :, :], sg[:, :, :], 1.0, None, ALU.add))
                step.link(dve.reciprocal(sg[:, :, :], sg[:, :, :]))
                beta = sg[:, :, HD * DV:HD * DV + HD]
                dve.tensor_tensor(by_head(vb[:, :, :], DV), by_head(pr[:, :, qk_w:qk_w + HD * DV], DV), heads_over(beta, DV), ALU.mult)
                step.link(dve.tensor_tensor(gn[:, :, :], pr[:, :, qk_w + HD * DV:qk_w + 2 * HD * DV], sg[:, :, 0:HD * DV], ALU.mult))
                step.link(dve.tensor_tensor(by_head(gn[:, :, :], DV), by_head(gn[:, :, :], DV),
                                            normw[:, :].unsqueeze(1).unsqueeze(1).to_broadcast([P, NT, HD, DV]), ALU.mult))
                dve.wait_ge(rn_ready, i + 1)
                for w, at, g in ((2, 0, 0), (0, HD * DK, HD)):
                    step.link(dve.tensor_tensor(qkp[:, :, w, :, 0:DK], by_head(pr[:, :, at:at + HD * DK], DK),
                                                heads_over(rn[:, :, g:g + HD], DK), ALU.mult))
                dve.tensor_tensor(qkp[:, :, 1, :, 0:DK], qkp[:, :, 0, :, 0:DK], heads_over(beta, DK), ALU.mult).then_inc(qkp_ready, 1)
                for t in range(NT):
                    for h in range(HD):
                        filled(dve, jobs, f"gram{t}{h}", i)
                        dve.tensor_tensor(AA[:, HD * t + h, :, :], bank[jobs.bank(f"gram{t}{h}")][:, 0:3 * P].rearrange("p (w t) -> p w t", w=3),
                                          m3[:, :, :], ALU.mult).then_inc(free[jobs.bank(f"gram{t}{h}")], 1)
                for h in range(HD):
                    moved(dve, jobs, f"gram1{h}", i)
                step.link(dve.scalar_tensor_tensor(XX[:, :, :, :].rearrange("p g w t -> p g (w t)"),
                                                   AA[:, :, 0:2, :].rearrange("p g w t -> p g (w t)"), -1.0,
                                                   m0[:, :, :].rearrange("p w t -> p (w t)").unsqueeze(1).to_broadcast([P, NT * HD, 2 * P]),
                                                   ALU.mult, ALU.mult))
                dve.tensor_tensor(XX[:, :, :, :].rearrange("p g w t -> p (g w) t"), XX[:, :, :, :].rearrange("p g w t -> p (g w) t"),
                                  ident[:, :].unsqueeze(1).to_broadcast([P, NT * HD * 2, P]), ALU.add).then_inc(X0_ready, 1)
                for k in range(1, LEVELS):
                    for t in range(NT):
                        filled(dve, jobs, f"T{k}{t}", i)
                        dve.tensor_tensor(TT[:, t, :, :], bank[jobs.bank(f"T{k}{t}")][:, :].rearrange("p (h t) -> p h t", h=HD),
                                          mlev[:, k - 1, :].unsqueeze(1).to_broadcast([P, HD, P]),
                                          ALU.mult).then_inc(free[jobs.bank(f"T{k}{t}")], 1)
                    for t in range(NT):
                        for w, name in enumerate("UV"):
                            if name == "U" and k == LEVELS - 1:
                                continue
                            job = f"{name}{k}{t}"
                            filled(dve, jobs, job, i)
                            if k == 1 and t == 0 and w == 0:
                                dve.wait_ge(X0_ready, i + 1)
                            elif k > 1:
                                moved(dve, jobs, f"{name}{k - 1}{t}", i)
                            half = XX[:, HD * t:HD * t + HD, w, :]
                            dve.tensor_tensor(half, half, bank[jobs.bank(job)][:, :].rearrange("p (h t) -> p h t", h=HD),
                                              ALU.subtract).then_inc(free[jobs.bank(job)], 1)
                moved(dve, jobs, "Uv", i)
                step.link(dve.tensor_copy(U[0:CH, 0, :], Uv[0:CH, 0, :]))
                dve.sem_inc(U_ready, 1)
                for c in range(1, 2 * NT):
                    t, r = c // 2, slice(CH * (c % 2), CH * (c % 2) + CH)
                    filled(dve, jobs, f"S{c}", i)
                    dve.tensor_tensor(St[:, c, :], bank[jobs.bank(f"S{c}")][:, 0:P], mhead, ALU.mult).then_inc(free[jobs.bank(f"S{c}")], 1)
                    filled(dve, jobs, f"ws{c}", i)
                    step.link(dve.tensor_tensor(U[r, t, :], Uv[r, t, :], bank[jobs.bank(f"ws{c}")][r, 0:P], ALU.subtract))
                    dve.sem_inc(U_ready, 1)
                    dve.sem_inc(free[jobs.bank(f"ws{c}")], 1)
                moved(dve, jobs, "o0", i)
                moved(dve, jobs, "o1", i)
                step.link(dve.tensor_tensor(osq[:, :, :], o_sb[:, :, :], o_sb[:, :, :], ALU.mult))
                step.link(dve.tensor_reduce(msc[:, :, :], by_head(osq[:, :, :], DV), X, ALU.add))
                dve.tensor_scalar(ms[:, :, :], msc[:, :, :], 1.0 / DV, EPS, ALU.mult, ALU.add).then_inc(ms_ready, 1)
                step.link(dve.tensor_tensor(y[:, :, :], o_sb[:, :, :], gn[:, :, :], ALU.mult))
                dve.wait_ge(rr_ready, i + 1)
                dve.tensor_tensor(by_head(y[:, :, :], DV), by_head(y[:, :, :], DV), heads_over(rr[:, :, :], DV), ALU.mult).then_inc(y_ready, 1)
                filled(dve, jobs, "fin", i)
                xi = x[:, bass.ds(i * NT, NT), :]
                dve.tensor_tensor(xi, xi, bank[jobs.bank("fin")][:, 0:NT * C].rearrange("p (n c) -> p n c", c=C),
                                  ALU.add).then_inc(free[jobs.bank("fin")], 1)

            def ffn_entry(jobs, i, n, ln):
                xi = x[:, bass.ds(i * NT, NT), :]
                layer_stats(i)
                normalize(i, ln)
                moved(dve, jobs, "xT", i)
                dve.tensor_tensor(xTl[:, :], xT[:, :], xTh[:, :].bitcast(F32), ALU.subtract).then_inc(xlo_ready, 1)

                def low_part(j):
                    w, c = "qk"[j % 2], 2 * (j // 2)
                    dve.wait_ge(qkhi_ready, 8 * n + (j + 1))
                    dve.tensor_tensor(qk[w, "l"][:, c:c + 2, :],
                                      bank[jobs.bank(f"qk{j}")][:, :].rearrange("p (a t) -> p a t", a=2),
                                      qk[w, "h"][:, c:c + 2, :].bitcast(F32),
                                      ALU.subtract).then_inc(free[jobs.bank(f"qk{j}")], 1)

                def head_max(h):
                    filled(dve, jobs, f"S{h}", i)
                    dve.tensor_reduce(negm[:, :, h], bank[jobs.bank(f"S{h}")][:, :].rearrange("p (n j) -> p n j", n=NT),
                                      X, ALU.max, negate=True).then_inc(free[jobs.bank(f"S{h}")], 1)

                low_part(0)
                low_part(1)
                for g in range(3):
                    low_part(2 * g + 2)
                    low_part(2 * g + 3)
                    for h in range(4 * g, 4 * g + 4):
                        head_max(h)
                for h in range(12, 16):
                    head_max(h)
                def groups(ap):
                    return ap.unsqueeze(2).to_broadcast([P, 64, E])
                ties = tie[:, :].unsqueeze(1).to_broadcast([P, 64, E])
                moved(dve, jobs, "gate", i)
                step.link(dve.tensor_reduce(gmax[:, :], gate[:, :, :], X, ALU.max))
                step.link(dve.tensor_tensor(gdif[:, :, :], gate[:, :, :], groups(gmax[:, :]), ALU.subtract))
                step.link(dve.scalar_tensor_tensor(gsel[:, :, :], gdif[:, :, :], 0.0, ties, ALU.is_ge, ALU.mult))
                step.link(dve.tensor_reduce(grank[:, :], gsel[:, :, :], X, ALU.max))
                step.link(dve.tensor_tensor(gsel2[:, :, :], gsel[:, :, :], groups(grank[:, :]), ALU.is_equal))
                step.link(dve.scalar_tensor_tensor(gdif[:, :, :], gsel2[:, :, :], NEG_BIG, gdif[:, :, :], ALU.mult, ALU.add))
                step.link(dve.tensor_reduce(gmax[:, :], gdif[:, :, :], X, ALU.max))
                step.link(dve.tensor_tensor(gdif[:, :, :], gdif[:, :, :], groups(gmax[:, :]), ALU.subtract))
                step.link(dve.scalar_tensor_tensor(gsel[:, :, :], gdif[:, :, :], 0.0, ties, ALU.is_ge, ALU.mult))
                step.link(dve.tensor_reduce(grank[:, :], gsel[:, :, :], X, ALU.max))
                step.link(dve.tensor_tensor(gsel[:, :, :], gsel[:, :, :], groups(grank[:, :]), ALU.is_equal))
                step.link(dve.tensor_tensor(mask[:, :, :, :, :].rearrange("p n s h e -> p (n s h) e"),
                                            gsel[:, :, :], gsel2[:, :, :], ALU.add))
                dve.wait_ge(egate_ready, n + 1)
                step.link(dve.tensor_scalar(sig[:, :, :, :], egate[:, :, :, :], 1.0, None, ALU.add))
                step.link(dve.reciprocal(sig[:, :, :, :], sig[:, :, :, :]))
                step.link(dve.tensor_tensor(mix[:, :, :, :, 0].rearrange("p h n e -> p n h e"), mask[:, :, 0, :, :],
                                            sig[:, :, :, :], ALU.mult))
                dve.transpose(mixT[:, :, :], mix[:, :, :, :, :].rearrange("p h n e x -> p h (n e x)")).then_inc(mixT_ready, 1)
                moved(dve, jobs, "pv0", i)
                moved(dve, jobs, "pv1", i)
                dve.transpose(pvT[:, :, :].rearrange("p l d -> p d l"),
                              pv[:, :, :, :, :].rearrange("p n e x d -> p d (n e x)")).then_inc(pvT_ready, 1)
                moved(dve, jobs, "vmix2", i)
                moved(dve, jobs, "vmix3", i)
                dve.transpose(v[:, :, 0:DH].rearrange("p g d -> p d g"),
                              vm[:, :, :].rearrange("p l d -> p d l")).then_inc(v_ready, 1)
                moved(dve, jobs, "at6", i)
                moved(dve, jobs, "at7", i)
                step.link(dve.reciprocal(rden[:, :], attn[:, :, :, DH].rearrange("p n h -> p (n h)")))
                step.link(dve.tensor_tensor(maskw[:, :, :].rearrange("p e (n h) -> p n h e", n=NT), mask[:, :, 1, :, :],
                                            rden[:, :].rearrange("p (n h) -> p n h", n=NT).unsqueeze(3).to_broadcast([P, NT, H, E]),
                                            ALU.mult))
                dve.transpose(maskT[:, :, :], maskw[:, :, :]).then_inc(maskT_ready, 1)
                dve.transpose(aT[:, :, :].rearrange("p l d -> p d l"),
                              attn[:, :, :, 0:DH].rearrange("p n h d -> p d (n h)")).then_inc(aT_ready, 1)
                filled(dve, jobs, "res", i)
                dve.scalar_tensor_tensor(xi, bank[jobs.bank("res")][:, 0:NT * C].rearrange("p (n c) -> p n c", c=C),
                                         0.5, xi, ALU.mult, ALU.add).then_inc(free[jobs.bank("res")], 1)

            dve.wait_ge(hid_in, 16)
            with dve.Fori(0, B) as i:
                step.loop(i, DVE_FFN)
                ffn_entry(ffn[0], i, i, i)
            step.end(B)
            if PHASES > 1:
                dve.wait_ge(masks_done, MASKS)
                dve.wait_ge(dw_in, 8 * 16)
                moved(dve, ffn[0], "res", B - 1)
                step.link(dve.memset(xpad[:, 0:3], 0.0))
                step.link(dve.memset(qkp[:, :, :, :, DK:DP], 0.0))
                step.link(dve.memset(St[:, 0, :], 0.0))
                with dve.Fori(0, B) as i:
                    step.loop(i, DVE_DELTA)
                    delta_entry(delta, i)
                step.end(B)
            if PHASES > 2:
                moved(dve, delta, "fin", B - 1)
                with dve.Fori(0, B) as i:
                    step.loop(i, DVE_FFN)
                    ffn_entry(ffn[1], i, i + B, i + 2 * B)
                step.end(B)

        @block.scalar
        def _(act):
            for j in range(6):
                filled(act, setup, f"w{j}", 0)
                src = bank[j % 2][:, :].rearrange("p (n c) -> p n c", c=P)
                if j < 4:
                    act.activation(WTh[:, 4 * j:4 * j + 4, :], src, ACT.Copy).then_inc(wT_hi, 1)
                elif j == 4:
                    act.activation(WvT[:, :], bank[0][:, :], ACT.Copy).then_inc(free[0], 1)
                else:
                    act.activation(WgT[:, :], bank[1][:, 0:2 * P], ACT.Copy).then_inc(free[1], 1)
            for j in range(6, 8):
                filled(act, setup, f"w{j}", 0)
                act.activation(WoT[:, 4 * (j - 6):4 * (j - 6) + 4, :],
                               bank[j % 2][0:DH, :].rearrange("p (n c) -> p n c", c=P), ACT.Copy).then_inc(free[j % 2], 1)

            def ffn_entry(jobs, i, n, ln):
                filled(act, jobs, "xT", i)
                act.activation(xT[:, :], bank[jobs.bank("xT")][:, 0:L], ACT.Copy)
                act.activation(xTh[:, :], bank[jobs.bank("xT")][:, 0:L], ACT.Copy).then_inc(free[jobs.bank("xT")], 1)
                filled(act, jobs, "gate", i)
                act.activation(gate[:, :, :], bank[jobs.bank("gate")][:, :].rearrange("p (g e) -> p g e", e=E),
                               ACT.Copy).then_inc(free[jobs.bank("gate")], 1)
                moved(act, jobs, "gate", i)
                act.activation(egate[:, :, :, :], gate[:, :, :].rearrange("p (n s h) e -> p n s (h e)", n=NT, s=2)[:, :, 0, :],
                               ACT.Exp, scale=-1.0).then_inc(egate_ready, 1)
                for t in range(NT):
                    filled(act, jobs, f"pv{t}", i)
                    act.activation(pv[:, t, :, 0, :], bank[jobs.bank(f"pv{t}")][:, :].rearrange("p (e d) -> p e d", d=DH),
                                   ACT.Copy).then_inc(free[jobs.bank(f"pv{t}")], 1)
                for j in range(8):
                    w, c = "qk"[j % 2], 2 * (j // 2)
                    filled(act, jobs, f"qk{j}", i)
                    act.activation(qk[w, "h"][:, c:c + 2, :],
                                   bank[jobs.bank(f"qk{j}")][:, :].rearrange("p (a t) -> p a t", a=2),
                                   ACT.Copy).then_inc(qkhi_ready, 1)
                filled(act, jobs, "mT", i)
                act.activation(nmT[0:H, :], bank[jobs.bank("mT")][0:H, 0:L], ACT.Copy)
                act.activation(nmT[DH:DH + H, :], bank[jobs.bank("mT")][0:H, 0:L], ACT.Copy).then_inc(free[jobs.bank("mT")], 1)
                for j in range(4):
                    filled(act, jobs, f"vmix{j}", i)
                    act.activation(vm[:, 8 * j:8 * j + 8, :], bank[jobs.bank(f"vmix{j}")][:, :].rearrange("p (l d) -> p l d", d=DH),
                                   ACT.Copy).then_inc(free[jobs.bank(f"vmix{j}")], 1)

                def attn_out(g):
                    filled(act, jobs, f"at{g}", i)
                    act.activation(attn[:, :, 2 * g:2 * g + 2, :].rearrange("p n h d -> p h n d"),
                                   bank[jobs.bank(f"at{g}")][:, 0:4 * DV1].rearrange("p (h n d) -> p h n d", h=2, n=NT),
                                   ACT.Copy).then_inc(free[jobs.bank(f"at{g}")], 1)

                for h in range(H):
                    filled(act, jobs, f"ST{h}", i)
                    if h >= 4:
                        filled(act, jobs, f"at{h // 2 - 2}", i)
                    act.activation(PT[:, h % 4, :, :], bank[jobs.bank(f"ST{h}")][:, :].rearrange("p (n t) -> p n t", n=NT),
                                   ACT.Exp, scale=DH ** -0.5).then_inc(free[jobs.bank(f"ST{h}")], 1)
                    if h % 2 and h >= 3:
                        attn_out(h // 2 - 1)
                attn_out(H // 2 - 1)
                for j in range(4):
                    filled(act, jobs, f"omix{j}", i)
                    act.activation(yT[:, :, :, :, 8 * j:8 * j + 8].rearrange("p n e q l -> p q (n e) l"),
                                   bank[jobs.bank(f"omix{j}")][0:DH, :].rearrange("p (l q c) -> p q c l", q=NQ, c=NT * E),
                                   ACT.Copy).then_inc(free[jobs.bank(f"omix{j}")], 1)

            def delta_entry(jobs, i):
                filled(act, jobs, "xT", i)
                act.activation(xpad[:, 3:3 + L], bank[jobs.bank("xT")][:, 0:L], ACT.Copy).then_inc(free[jobs.bank("xT")], 1)
                act.wait_ge(conv_ready, i + 1)
                act.activation(hexp[:, :], hacc[:, :], ACT.Exp, scale=-1.0).then_inc(hexp_ready, 1)
                for t in range(NT):
                    filled(act, jobs, f"proj{t}", i)
                    act.activation(pr[:, t, :], bank[jobs.bank(f"proj{t}")][:, 0:NPR], ACT.Copy).then_inc(free[jobs.bank(f"proj{t}")], 1)
                moved(act, jobs, "proj0", i)
                moved(act, jobs, "proj1", i)
                act.activation(sg[:, :, :], pr[:, :, NPR - HD * DV - HD:NPR], ACT.Exp, scale=-1.0).then_inc(gexp_ready, 1)
                for t in range(NT):
                    filled(act, jobs, f"tq{t}", i)
                    act.activation(qkT[:, t, :, :].rearrange("p w t -> p (w t)"), bank[jobs.bank(f"tq{t}")][:, 0:3 * P],
                                   ACT.Copy).then_inc(free[jobs.bank(f"tq{t}")], 1)
                filled(act, jobs, "WT", i)
                act.activation(WT[:, :], bank[jobs.bank("WT")][:, 0:L], ACT.Copy).then_inc(free[jobs.bank("WT")], 1)
                filled(act, jobs, "Uv", i)
                act.activation(Uv[:, :, :].rearrange("p n m -> p (n m)"), bank[jobs.bank("Uv")][:, 0:L],
                               ACT.Copy).then_inc(free[jobs.bank("Uv")], 1)
                for t in range(NT):
                    filled(act, jobs, f"o{t}", i)
                    act.activation(o_sb[:, t, :], bank[jobs.bank(f"o{t}")][:, 0:P], ACT.Copy).then_inc(free[jobs.bank(f"o{t}")], 1)
                filled(act, jobs, "yT", i)
                act.activation(yT_d[:, :], bank[jobs.bank("yT")][:, 0:L], ACT.Copy).then_inc(free[jobs.bank("yT")], 1)

            with act.Fori(0, B) as i:
                ffn_entry(ffn[0], i, i, i)
            if PHASES > 1:
                with act.Fori(0, B) as i:
                    delta_entry(delta, i)
            if PHASES > 2:
                with act.Fori(0, B) as i:
                    ffn_entry(ffn[1], i, i + B, i + 2 * B)

        @block.tensor
        def _(pe):
            pe.wait_ge(const_done, CONSTS)
            pe.wait_ge(w_in, 6 * 16)
            for j in range(6):
                turn(pe, setup, f"w{j}", 0)
                for k in range(4 if j < 5 else 2):
                    last = pe.transpose(bank[j % 2][:, P * k:P * k + P], wst[:, 4 * j + k, :], ident[:, :])
                last.then_inc(full[j % 2], 1)
            for j in range(6, 8):
                turn(pe, setup, f"w{j}", 0)
                for k in range(4):
                    last = pe.transpose(bank[j % 2][0:DH, P * k:P * k + P], wost[:, 4 * (j - 6) + k, :], ident[:, :])
                last.then_inc(full[j % 2], 1)

            def ffn_entry(jobs, i, n, ln):
                def out_of(name):
                    turn(pe, jobs, name, i)
                    return bank[jobs.bank(name)]

                def done(last, name):
                    last.then_inc(full[jobs.bank(name)], 1)

                o = out_of("xT")
                pe.wait_ge(xn_ready, 2 * ln + 2)
                for t in range(NT):
                    last = pe.transpose(o[:, P * t:P * t + P], xn[:, t, :], ident[:, :])
                done(last, "xT")
                moved(pe, jobs, "xT", i)
                o = out_of("gate")
                for t in range(NT):
                    last = pe.matmul(o[:, 2 * P * t:2 * P * t + 2 * P], xT[:, P * t:P * t + P], WgT[:, :], start=True, stop=True)
                done(last, "gate")
                for t in range(NT):
                    o = out_of(f"pv{t}")
                    done(pe.matmul(o[:, :], xT[:, P * t:P * t + P], WvT[:, :], start=True, stop=True), f"pv{t}")

                pe.wait_ge(xlo_ready, n + 1)

                def project(j):
                    o = out_of(f"qk{j}")
                    for a in range(2):
                        c = 8 * (j % 2) + 2 * (j // 2) + a
                        oa = o[:, L * a:L * a + L]
                        pe.matmul(oa, WTh[:, c, :], xTh[:, :], start=True, stop=False)
                        pe.matmul(oa, WTh[:, c, :], xTl[:, :], start=False, stop=False)
                        last = pe.matmul(oa, WTl[:, c, :], xTh[:, :], start=False, stop=True)
                    done(last, f"qk{j}")

                def shift_scores(h):
                    o, r, c = out_of(f"S{h}"), heads(h, 0), h // 2
                    for t in range(NT):
                        last = pe.matmul(o[:, L * t:L * t + L], qk["q", "h"][r, c, P * t:P * t + P],
                                         qk["k", "h"][r, c, :], start=True, stop=True)
                    done(last, f"S{h}")

                for g in range(4):
                    project(2 * g)
                    project(2 * g + 1)
                    if g:
                        pe.wait_ge(qkhi_ready, 8 * n + 2 * g)
                        for h in range(4 * g - 4, 4 * g):
                            shift_scores(h)
                pe.wait_ge(qkhi_ready, 8 * n + 8)
                for h in range(12, 16):
                    shift_scores(h)

                o = out_of("mT")
                moved(pe, jobs, "S14", i)
                moved(pe, jobs, "S15", i)
                for t in range(NT):
                    last = pe.transpose(o[0:H, P * t:P * t + P], negm[:, t, :], ident[:, :])
                done(last, "mT")

                pe.wait_ge(pvT_ready, n + 1)
                pe.wait_ge(bdv_ready, n + 1)
                for j in range(4):
                    o = out_of(f"vmix{j}")
                    for k in range(8):
                        last = pe.matmul(o[:, DH * k:DH * k + DH], bdv[:, 8 * j + k, :, :].rearrange("p m h -> p (m h)"),
                                         pvT[:, 8 * j + k, :], start=True, stop=True)
                    done(last, f"vmix{j}")

                def scores(h):
                    o, r, c = out_of(f"ST{h}"), heads(h, 0), h // 2
                    for t in range(NT):
                        ot, tj = o[:, L * t:L * t + L], slice(P * t, P * t + P)
                        pe.matmul(ot, qk["k", "h"][r, c, tj], qk["q", "h"][r, c, :], start=True, stop=False)
                        pe.matmul(ot, qk["k", "h"][r, c, tj], qk["q", "l"][r, c, :], start=False, stop=False)
                        pe.matmul(ot, qk["k", "l"][r, c, tj], qk["q", "h"][r, c, :], start=False, stop=False)
                        last = pe.matmul(ot, sel[r, h, :], nmT[r, :], start=False, stop=True)
                    done(last, f"ST{h}")

                def attend(h):
                    g = h // 2
                    o = out_of(f"at{g}") if h % 2 == 0 else bank[jobs.bank(f"at{g}")]
                    moved(pe, jobs, f"ST{h}", i)
                    for t in range(NT):
                        ot = o[:, (2 * (h % 2) + t) * DV1:(2 * (h % 2) + t + 1) * DV1]
                        for tj in range(NT):
                            last = pe.matmul(ot, PT[:, h % 4, tj, P * t:P * t + P], v[:, H * tj + h, :],
                                             start=(tj == 0), stop=(tj == NT - 1))
                    if h % 2:
                        done(last, f"at{g}")

                moved(pe, jobs, "qk7", i)
                moved(pe, jobs, "qk6", i)
                moved(pe, jobs, "mT", i)
                scores(0)
                scores(1)
                pe.wait_ge(v_ready, n + 1)
                for h in range(2, H):
                    attend(h - 2)
                    scores(h)
                attend(H - 2)
                attend(H - 1)

                pe.wait_ge(aT_ready, n + 1)
                pe.wait_ge(bdo_ready, n + 1)
                for j in range(4):
                    o = out_of(f"omix{j}")
                    for k in range(8):
                        last = pe.matmul(o[0:DH, DH * k:DH * k + DH], aT[:, 8 * j + k, :],
                                         bdo[:, 8 * j + k, :, :].rearrange("p m e -> p (m e)"), start=True, stop=True)
                    done(last, f"omix{j}")
                o = out_of("res")
                moved(pe, jobs, "omix2", i)
                moved(pe, jobs, "omix3", i)
                for t in range(NT):
                    for e in range(E):
                        last = pe.matmul(o[:, C * t:C * t + C], yT[:, t, e, :, :].rearrange("d q l -> d (q l)"), WoT[:, e, :], start=(e == 0), stop=(e == E - 1))
                done(last, "res")

            def delta_entry(jobs, i):
                def out_of(name):
                    turn(pe, jobs, name, i)
                    return bank[jobs.bank(name)]

                def done(last, name):
                    last.then_inc(full[jobs.bank(name)], 1)

                o = out_of("xT")
                pe.wait_ge(xn_ready, 2 * i + (2 * B + 2))
                for t in range(NT):
                    last = pe.transpose(o[:, P * t:P * t + P], xn[:, t, :], ident[:, :])
                done(last, "xT")
                pe.wait_ge(hT_ready, i + 1)
                for t in range(NT):
                    o = out_of(f"proj{t}")
                    done(pe.matmul(o[:, 0:NPR], hT[:, P * t:P * t + P], dW[:, :], start=True, stop=True), f"proj{t}")
                pe.wait_ge(qkp_ready, i + 1)
                for t in range(NT):
                    o = out_of(f"tq{t}")
                    for w in range(3):
                        last = pe.transpose(o[:, P * w:P * w + P], qkp[:, t, w, :, :].rearrange("p h d -> p (h d)"), ident[:, :])
                    done(last, f"tq{t}")
                for t in range(NT):
                    moved(pe, jobs, f"tq{t}", i)
                    for h in range(HD):
                        o, r = out_of(f"gram{t}{h}"), slice(DP * h, DP * h + DP)
                        pe.matmul(o[:, 0:P], qkT[r, t, 1, :], qkT[r, t, 0, :], start=True, stop=True)
                        done(pe.matmul(o[:, P:3 * P], qkT[r, t, 0, :], qkT[r, t, 1:3, :].rearrange("p w t -> p (w t)"),
                                       start=True, stop=True), f"gram{t}{h}")
                pe.wait_ge(X0_ready, i + 1)
                for k in range(1, LEVELS):
                    for t in range(NT):
                        if k > 1:
                            moved(pe, jobs, f"U{k - 1}{t}", i)
                            moved(pe, jobs, f"V{k - 1}{t}", i)
                        o = out_of(f"T{k}{t}")
                        for h in range(HD):
                            last = pe.matmul(o[:, P * h:P * h + P], AA[:, HD * t + h, 1, :], XX[:, HD * t + h, 0, :], start=True, stop=True)
                        done(last, f"T{k}{t}")
                    for t in range(NT):
                        moved(pe, jobs, f"T{k}{t}", i)
                        if k < LEVELS - 1:
                            o = out_of(f"U{k}{t}")
                            for h in range(HD):
                                last = pe.matmul(o[:, P * h:P * h + P], XX[:, HD * t + h, 1, :], TT[:, t, h, :], start=True, stop=True)
                            done(last, f"U{k}{t}")
                        o = out_of(f"V{k}{t}")
                        for h in range(HD):
                            last = pe.matmul(o[:, P * h:P * h + P], TT[:, t, h, :], XX[:, HD * t + h, 1, :], start=True, stop=True)
                        done(last, f"V{k}{t}")
                moved(pe, jobs, f"V{LEVELS - 1}0", i)
                moved(pe, jobs, f"V{LEVELS - 1}1", i)
                o = out_of("WT")
                for t in range(NT):
                    for h in range(HD):
                        last = pe.matmul(o[DP * h:DP * h + DP, P * t:P * t + P], qkp[:, t, 1, h, :], XX[:, HD * t + h, 1, :],
                                         start=True, stop=True)
                done(last, "WT")
                o = out_of("Uv")
                for t in range(NT):
                    for h in range(HD):
                        last = pe.matmul(o[:, P * t + DV * h:P * t + DV * h + DV], XX[:, HD * t + h, 1, :],
                                         vb[:, t, DV * h:DV * h + DV], start=True, stop=True)
                done(last, "Uv")
                moved(pe, jobs, "WT", i)
                for c in range(1, 2 * NT):
                    t, r = (c - 1) // 2, slice(CH * ((c - 1) % 2), CH * ((c - 1) % 2) + CH)
                    o = out_of(f"S{c}")
                    pe.wait_ge(U_ready, 4 * i + c)
                    done(pe.matmul(o[:, 0:P], qkp[r, t, 0, :, :].rearrange("p h d -> p (h d)"), U[r, t, :],
                                   start=(c == 1), stop=(c == 2 * NT - 1), skip_group_check=True), f"S{c}")
                    moved(pe, jobs, f"S{c}", i)
                    o, r = out_of(f"ws{c}"), slice(CH * (c % 2), CH * (c % 2) + CH)
                    done(pe.matmul(o[r, 0:P], WT[:, CH * c:CH * c + CH], St[:, c, :], start=True, stop=True), f"ws{c}")
                pe.wait_ge(U_ready, 4 * i + 4)
                for t in range(NT):
                    o = out_of(f"o{t}")
                    for half in range(2):
                        pe.matmul(o[CH * half:CH * half + CH, 0:P], qkT[:, t, 2, CH * half:CH * half + CH], St[:, 2 * t + half, :],
                                  start=True, stop=False, skip_group_check=True)
                    for h in range(HD):
                        last = pe.matmul(o[:, DV * h:DV * h + DV], AA[:, HD * t + h, 2, :], U[:, t, DV * h:DV * h + DV],
                                         start=False, stop=True, skip_group_check=True)
                    done(last, f"o{t}")
                pe.wait_ge(y_ready, i + 1)
                o = out_of("yT")
                for t in range(NT):
                    last = pe.transpose(o[:, P * t:P * t + P], y[:, t, :], ident[:, :])
                done(last, "yT")
                moved(pe, jobs, "yT", i)
                o = out_of("fin")
                for t in range(NT):
                    last = pe.matmul(o[:, C * t:C * t + C], yT_d[:, P * t:P * t + P], dWo_sb[:, :], start=True, stop=True)
                done(last, "fin")

            with pe.Fori(0, B) as i:
                ffn_entry(ffn[0], i, i, i)
            if PHASES > 1:
                with pe.Fori(0, B) as i:
                    delta_entry(delta, i)
            if PHASES > 2:
                with pe.Fori(0, B) as i:
                    ffn_entry(ffn[1], i, i + B, i + 2 * B)


_INS = ["L0_attn_hidden_states", "L0_attn_conv_w", "L0_attn_Wq", "L0_attn_Wk", "L0_attn_Wv", "L0_attn_Wb", "L0_attn_Wg",
        "L0_attn_norm_w", "L0_attn_Wo", "L0_ffn_Wq", "L0_ffn_Wk", "L0_ffn_Wv", "L0_ffn_Ws", "L0_ffn_Wd", "L0_ffn_Wo"]


def kernel(**inputs):
    import numpy as np
    import concourse.bacc as bacc
    from concourse.bass_utils import run_bass_kernel_spmd as run

    nc = bacc.Bacc("TRN2", target_bir_lowering=False, num_devices=1)
    arrays, args = {}, []
    for name in _INS:
        a = np.ascontiguousarray(inputs[name])
        arrays[name] = a
        args.append(nc.dram_tensor(name, a.shape, mybir.dt.from_np(a.dtype), kind="ExternalInput").ap())
    args.append(nc.dram_tensor("out", (B, L, C), F32, kind="ExternalOutput").ap())
    build(nc, *args)
    r = run(nc, [arrays], core_ids=[0])
    return r.results[0]["out"]
```

```python
import concourse.bass as bass
from concourse import mybir
from contextlib import ExitStack

F32 = mybir.dt.float32
F32R = mybir.dt.float32r
ALU = mybir.AluOpType
ACT = mybir.ActivationFunctionType
X = mybir.AxisListType.X

B, L, C = 8, 256, 128
P = 128
NT = L // P
H, DH, E = 16, 64, 8
NQ, NL = 4, 32
DV1 = DH + 1
NPAIR = H * DH // P
HD, DK, DV, CH = 4, 16, 32, 64
DP = 32
LEVELS = 6
NEG_BIG = -3.0e38
CONSTS, POOL_STEPS, DVE_FFN, DVE_DELTA, MASKS = 14, 6, 21, 50, 6
PHASES = 3
EPS = 1e-5

SETUP_JOBS = [(f"w{j}", j % 2) for j in range(8)]
FFN_FRONT = ([("xT", 0), ("gate", 1), ("pv0", 0), ("pv1", 1)]
             + [(f"qk{c}", c % 2) for c in range(NPAIR)]
             + [(f"vmix{j}", j % 2) for j in range(4)] + [("mT", 0)]
             + [(f"S{h}", 2 + h % 2) for h in range(H)])
FFN_BACK = ([(f"omix{j}", (j + 1) % 2) for j in range(4)] + [("res", 1)]
            + [(f"ST{h}", 4 + h % 2) for h in range(H)]
            + [(f"at{g}", 6 + g % 2) for g in range(H // 2)])
PROJECT = {2: (0,), 3: (1,), 4: (2,), 5: (3,), 6: (4,), 7: (5,), 8: (6, 7)}
SHIFT = {3: (0,), 4: (1,), 5: (2,), 6: (3,), 7: (4,), 8: (5, 6), 9: (7,)}
INVERSE = [(w, k, t) for k in range(1, LEVELS)
           for w, t in ([("T", 0), ("T", 1), ("U", 0), ("V", 0), ("U", 1), ("V", 1)] if k < LEVELS - 1 else
                        [("T", 0), ("T", 1), ("V", 0), ("V", 1)])]
SCAN_AT = {0: ["S1"], 1: ["ws1"], 3: ["S2"], 4: ["ws2"], 6: ["S3"], 7: ["ws3"], 8: ["out"],
           9: ["square"], 13: ["gate"], 14: ["turn"], 16: ["residual"]}
FRONT_AT = {0: ["normalize"], 2: ["xT"], 3: ["conv3"], 4: ["conv2"], 5: ["conv1", "conv0"],
            7: ["silu"], 9: ["proj"], 10: ["norms"], 13: ["sigmoids0"], 14: ["sigmoids1"], 15: ["keys"], 16: ["tq"], 17: ["gates"],
            19: ["gram00", "gram01"], 20: ["gram02", "gram03"], 21: ["X0_0"], 24: ["gram10", "gram11"],
            25: ["gram12", "gram13", "X0_1"]}
DELTA_ORDER = [("scan", "start"), ("front", "stats")]
for g, group in enumerate(INVERSE):
    DELTA_ORDER += [("inverse", group)] + [("scan", w) for w in SCAN_AT.get(g, ())] + [("front", w) for w in FRONT_AT.get(g, ())]
DELTA_ORDER += [("inverse", "WT"), ("inverse", "Uv")]
DELTA_BANKS = {"S1": [("S1", 4)], "ws1": [("ws1", 5)], "S2": [("S2", 4)], "ws2": [("ws2", 5)], "S3": [("S3", 4)],
               "ws3": [("ws3", 5)], "out": [("o0", 5), ("o1", 4)], "turn": [("yT", 5)], "residual": [("fin", 4)],
               "WT": [("WT", 5)], "Uv": [("Uv", 4)], "xT": [("xT", 6)], "proj": [("proj0", 7), ("proj1", 6)],
               "tq": [("tq0", 7), ("tq1", 6)]}
DELTA_BANKS.update({f"gram{t}{h}": [(f"gram{t}{h}", 7 - h % 2)] for t in range(NT) for h in range(HD)})
DELTA_BANKS.update({(w, k, t): [(f"{w}{k}{t}", {"T": t, "U": 2, "V": 3}[w])] for w, k, t in INVERSE})
DELTA_BANKS["V", LEVELS - 1, 1] = [(f"V{LEVELS - 1}1", 2)]


def delta_jobs(stages, tag):
    return [(name + tag, b) for stage, step in DELTA_ORDER if stage in stages for name, b in DELTA_BANKS.get(step, ())]


class Chain:

    def __init__(self, eng, sem):
        self.eng, self.sem, self.base, self.i, self.per, self.n = eng, sem, 0, 0, 0, 0

    def loop(self, i, per):
        self.base, self.i, self.per, self.n = self.base + self.n, i, per, 0

    def end(self, times):
        assert self.n == self.per, self.n
        self.base, self.i, self.per, self.n = self.base + times * self.per, 0, 0, 0

    def link(self, ins):
        self.n += 1
        ins.then_inc(self.sem, 1)
        self.eng.wait_ge(self.sem, self.i * self.per + (self.base + self.n))


class Jobs:

    def __init__(self, jobs, base, times):
        self.base, self.per, self.at = dict(base), {b: 0 for b in range(8)}, {}
        for name, bank in jobs:
            self.at[name] = (bank, self.per[bank])
            self.per[bank] += 1
        self.end = {b: base[b] + times * self.per[b] for b in range(8)}

    def bank(self, name):
        return self.at[name][0]

    def before(self, name, i):
        bank, k = self.at[name]
        return i * self.per[bank] + (self.base[bank] + k)

    def done(self, name, i):
        bank, k = self.at[name]
        return i * self.per[bank] + (self.base[bank] + k + 1)


def build(nc, hid, conv_w, dWq, dWk, dWv, dWb, dWg, norm_w, dWo, fWq, fWk, fWv, fWs, fWd, fWo, out):
    with ExitStack() as ctx:
        def sb(name, shape, dt=F32):
            return ctx.enter_context(nc.sbuf_tensor(name, shape, dt))

        def sem(name):
            return ctx.enter_context(nc.semaphore(name))

        ident = sb("ident", [P, P])
        own16 = sb("own16", [P, 8])
        neg_half16 = sb("neg_half16", [P, NT * 2 * HD])
        tie = sb("tie", [P, E])
        self_f = sb("self_f", [P, H, P])
        sel = sb("sel", [P, H, P], F32R)
        WTh = sb("WTh", [P, 16, P], F32R)
        WTl = sb("WTl", [P, 16, P], F32R)
        WvT = sb("WvT", [P, 4 * P])
        WgT = sb("WgT", [P, 2 * P])
        WoT = sb("WoT", [DH, E, P])
        x = sb("x", [P, B * NT, C])
        bdv = sb("bdv", [P, NL, 8, H])
        staged = bdv[:, :, :, :].rearrange("p l m h -> p (l m h)")
        wst = staged[:, 0:22 * C].rearrange("p (n c) -> p n c", c=C)
        wost = staged[:, 22 * C:22 * C + E * DH].rearrange("p (e d) -> p e d", d=DH)
        stat = sb("stat", [P, NT, 6])
        mv = sb("mv", [P, NT, 4])
        mean = sb("mean", [P, NT])
        vare = sb("vare", [P, NT])
        rstd = sb("rstd", [P, NT])
        xn = sb("xn", [P, NT, C])
        xT = sb("xT", [P, L])
        xTh = sb("xTh", [P, L], F32R)
        xTl = sb("xTl", [P, L], F32R)
        gate = sb("gate", [P, 64, E])
        egate = sb("egate", [P, NT, H, E])
        gdif = sb("gdif", [P, 64, E])
        gsel = sb("gsel", [P, 64, E])
        gsel2 = sb("gsel2", [P, 64, E])
        gmax = sb("gmax", [P, 64])
        grank = sb("grank", [P, 64])
        mask = sb("mask", [P, NT, 2, H, E])
        masko = sb("masko", [P, NT, H, E])
        sig = sb("sig", [P, NT, H, E])
        mix = sb("mix", [P, H, NT, E, 2])
        mixT = sb("mixT", [P, H, NL])
        pv = sb("pv", [P, NT, E, 2, DH])
        pvT = sb("pvT", [P, NL, DH])
        vm = sb("vm", [P, NL, DH])
        v = sb("v", [P, NT * H, DV1])
        negm = sb("negm", [P, NT, H])
        nmT = sb("nmT", [P, L], F32R)
        PT = sb("PT", [P, 4, NT, L])
        attn = sb("attn", [P, NT, H, DV1])
        rden = sb("rden", [P, NT * H])
        maskw = sb("maskw", [P, E, NT * H])
        maskT = sb("maskT", [P, E, NL])
        bdo = sb("bdo", [P, NL, 8, E])
        aT = sb("aT", [P, NL, DH])
        yT = sb("yT", [DH, NT, E, NQ, NL])

        convw = sb("convw", [P, 4])
        normw = sb("normw", [P, DV])
        dW = sb("dW", [P, 2 * HD * DK + 2 * HD * DV + HD])
        dWo_sb = sb("dWo_sb", [P, C])

        with nc.sbuf_tensor("qkh", [P, NPAIR, 2, L], F32R) as qkh, nc.sbuf_tensor("qkl", [P, NPAIR, 2, L], F32R) as qkl:
            pass
        odd_h = sb("odd_h", [P, NPAIR * 2 * L])
        odd_l = sb("odd_l", [P, NPAIR * 2 * L])

        def over(tensor, at, *shape):
            n = 1
            for m in shape:
                n *= m
            names = "abcd"[:len(shape)]
            return tensor[:, at:at + n].rearrange(f"p ({' '.join(names)}) -> p {' '.join(names)}", **dict(zip(names, shape)))

        f_bdv = bdv[:, :, :, :].rearrange("p l m h -> p (l m h)")
        f_aT = aT[:, :, :].rearrange("p l d -> p (l d)")
        f_bdo = bdo[:, :, :, :].rearrange("p l m e -> p (l m e)")
        f_PT = PT[:, :, :, :].rearrange("p a n t -> p (a n t)")
        f_attn = attn[:, :, :, :].rearrange("p n h d -> p (n h d)")
        f_vm = vm[:, :, :].rearrange("p l d -> p (l d)")
        f_self = self_f[:, :, :].rearrange("p h m -> p (h m)")
        AA_of = [over(f_bdv, 0, NT * HD, 3, P), over(odd_h, 0, NT * HD, 3, P)]
        XX_of = [over(f_aT, 0, NT * HD, 2, P), over(odd_l, 0, NT * HD, 2, P)]
        qkp_of = [over(f_PT, 0, NT, 3, HD, DP), over(odd_l, 2048, NT, 3, HD, DP)]
        qkT_of = [over(f_PT, 768, NT, 3, P), over(odd_l, 2816, NT, 3, P)]
        vb_of = [over(f_attn, 1824, NT, P), over(odd_l, 3584, NT, P)]
        gn_of = [over(f_vm, 1548, NT, P), over(odd_l, 3840, NT, P)]
        TT = over(f_bdo, 0, NT, HD, P)
        WT = over(f_bdo, 1024, L)
        Uv = over(f_bdo, 1280, NT, P)
        U = over(f_bdo, 1536, NT, P)
        St = over(f_PT, 1536, 4, P)
        NPR = 2 * HD * DK + 2 * HD * DV + HD
        pr = over(f_attn, 0, NT, NPR)
        o_sb = over(f_attn, 800, NT, P)
        osq = over(f_attn, 1056, NT, P)
        y = over(f_attn, 1312, NT, P)
        yT_d = over(f_attn, 1568, L)
        xpad = over(f_vm, 0, L + 3)
        hacc = over(f_vm, 260, L)
        hexp = over(f_vm, 516, L)
        hT = over(f_vm, 772, L)
        sqs = over(f_vm, 1028, NT, 2 * HD * DK)
        sg = over(f_vm, 1284, NT, HD * DV + HD)
        ss = over(f_vm, 1804, NT, 2 * HD)
        rn = over(f_vm, 1820, NT, 2 * HD)
        ms = over(f_vm, 1836, NT, HD)
        rr = over(f_vm, 1844, NT, HD)
        msc = over(f_vm, 1852, NT, HD)
        m3 = over(f_self, 0, 3, P)
        m0 = over(f_self, 384, 2, P)
        mlev = over(f_self, 640, LEVELS - 1, P)
        mhead = over(f_self, 1280, P)

        bank = [ctx.enter_context(nc.psum_tensor(f"bank{b}", [P, 512], F32)) for b in range(8)]
        full = [sem(f"full{b}") for b in range(8)]
        free = [sem(f"free{b}") for b in range(8)]

        hid_in = sem("hid_in")
        w_in = sem("w_in")
        const_done = sem("const_done")
        wT_hi = sem("wT_hi")
        dve_step = sem("dve_step")
        pool_step = sem("pool_step")
        var_ready = sem("var_ready")
        rstd_ready = sem("rstd_ready")
        xn_ready = sem("xn_ready")
        xlo_ready = sem("xlo_ready")
        egate_ready = sem("egate_ready")
        mixT_ready = sem("mixT_ready")
        bdv_ready = sem("bdv_ready")
        pvT_ready = sem("pvT_ready")
        qkhi_ready = sem("qkhi_ready")
        v_ready = sem("v_ready")
        maskT_ready = sem("maskT_ready")
        bdo_ready = sem("bdo_ready")
        aT_ready = sem("aT_ready")
        masks_done = sem("masks_done")
        dw_in = sem("dw_in")
        sel_ready = sem("sel_ready")
        conv_ready = sem("conv_ready")
        hexp_ready = sem("hexp_ready")
        hT_ready = sem("hT_ready")
        ss_ready = sem("ss_ready")
        rn_ready = sem("rn_ready")
        gexp_ready = sem("gexp_ready")
        qkp_ready = sem("qkp_ready")
        X0_ready = sem("X0_ready")
        U_ready = sem("U_ready")
        ms_ready = sem("ms_ready")
        rr_ready = sem("rr_ready")
        y_ready = sem("y_ready")
        stored = sem("stored")

        base = {b: 0 for b in range(8)}
        setup = Jobs(SETUP_JOBS, base, 1)


        def ffn_phase(base):
            first = Jobs(FFN_FRONT, base, 1)
            loop = Jobs(FFN_FRONT + FFN_BACK, first.end, B - 1)
            return first, loop, Jobs(FFN_BACK, loop.end, 1)

        ffn = [ffn_phase(setup.end)]
        delta = [Jobs(delta_jobs(("front",), ""), ffn[0][2].end, 1)]
        delta.append(Jobs(delta_jobs(("inverse", "front"), ""), delta[-1].end, 1))
        delta.append(Jobs(delta_jobs(("inverse", "scan", "front"), "a") + delta_jobs(("inverse", "scan", "front"), "b"),
                          delta[-1].end, B // 2 - 1))
        delta.append(Jobs(delta_jobs(("inverse", "scan"), ""), delta[-1].end, 1))
        delta.append(Jobs(delta_jobs(("scan",), ""), delta[-1].end, 1))
        ffn.append(ffn_phase(delta[-1].end))

        def delta_loop(eng, turn_of, chain=None, per=0):
            turn_of(delta[0], 0, "", None, None, 0, 1)
            turn_of(delta[1], 0, "", 0, None, 1, 0)
            with eng.Fori(0, B // 2 - 1) as i:
                if chain:
                    chain.loop(i, per)
                turn_of(delta[2], i, "a", 2 * i + 1, 2 * i, 2 * i + 2, 1)
                turn_of(delta[2], i, "b", 2 * i + 2, 2 * i + 1, 2 * i + 3, 0)
            if chain:
                chain.end(B // 2 - 1)
            turn_of(delta[3], 0, "", B - 1, B - 2, None, 1)
            turn_of(delta[4], 0, "", None, B - 1, None, 0)

        def ffn_loop(eng, phase, turn_of, chain=None, per=0):
            first, loop, last = ffn[phase]
            turn_of(first, 0, None, 0)
            with eng.Fori(0, B - 1) as i:
                if chain:
                    chain.loop(i, per)
                turn_of(loop, i, i, i + 1)
            if chain:
                chain.end(B - 1)
            turn_of(last, 0, B - 1, None)
        CREDIT = {b: 0 if b < 2 else 1 for b in range(8)}

        def turn(eng, jobs, name, i):
            b = jobs.bank(name)
            n = jobs.before(name, i) + CREDIT[b]
            if isinstance(n, int) and n == 0:
                return
            eng.wait_ge(free[b], n)

        def filled(eng, jobs, name, i):
            eng.wait_ge(full[jobs.bank(name)], jobs.done(name, i))

        def moved(eng, jobs, name, i):
            b = jobs.bank(name)
            eng.wait_ge(free[b], jobs.done(name, i) + CREDIT[b])

        def heads(h, part):
            return slice(DH * (h % 2), DH * (h % 2) + DH)

        block = ctx.enter_context(nc.Block())

        @block.sync
        def _(sp):
            sp.dma_start(x[:, :, :], hid.rearrange("b (n p) c -> p (b n) c", p=P)).then_inc(hid_in, 16)
            sp.dma_start(wst[:, 0:8, :], fWq.rearrange("h d c -> (h d) c").rearrange("(n p) c -> p n c", p=P)).then_inc(w_in, 16)
            sp.dma_start(wst[:, 8:16, :], fWk.rearrange("h d c -> (h d) c").rearrange("(n p) c -> p n c", p=P)).then_inc(w_in, 16)
            sp.dma_start(wst[:, 16:20, :], fWv.rearrange("h d c -> (h d) c").rearrange("(n p) c -> p n c", p=P)).then_inc(w_in, 16)
            sp.dma_start(wst[:, 20, :], fWs.rearrange("h e c -> (h e) c")).then_inc(w_in, 16)
            sp.dma_start(wst[:, 21, :], fWd.rearrange("h e c -> (h e) c")).then_inc(w_in, 16)
            sp.dma_start(wost[:, :, :], fWo.rearrange("e f d -> f e d")).then_inc(w_in, 16)
            sp.dma_start(convw[:, :], conv_w).then_inc(dw_in, 16)
            sp.dma_start(normw[:, :], norm_w.unsqueeze(0).to_broadcast([P, DV])).then_inc(dw_in, 16)
            at = 0
            for w in (dWq, dWk, dWv, dWg, dWb):
                sp.dma_start(dW[:, at:at + w.shape[1]], w).then_inc(dw_in, 16)
                at += w.shape[1]
            sp.dma_start(dWo_sb[:, :], dWo).then_inc(dw_in, 16)
            if PHASES == 1:
                moved(sp, ffn[0][2], "res", 0)
            elif PHASES == 2:
                moved(sp, delta[4], "fin", 0)
            else:
                moved(sp, ffn[1][2], "res", 0)
            sp.dma_start(out.rearrange("b (n p) c -> p (b n) c", p=P), x[:, :, :]).then_inc(stored, 16)
            sp.wait_ge(stored, 16)

        @block.gpsimd
        def _(pool):
            step = Chain(pool, pool_step)
            pool.memset(neg_half16[:, :], -0.5).then_inc(const_done, 1)
            for e in range(E):
                pool.memset(tie[:, e:e + 1], float(E - e)).then_inc(const_done, 1)
            step.link(pool.memset(ident[:, :], 0.0))
            pool.affine_select(out=ident[:, :], in_=ident[:, :], compare_op=ALU.not_equal, fill=1.0,
                               base=0, pattern=[[-1, P]], channel_multiplier=1).then_inc(const_done, 1)
            step.link(pool.memset(own16[:, :], 1.0))
            step.link(pool.affine_select(out=own16[:, :], in_=own16[:, :], compare_op=ALU.is_ge, fill=0.0,
                                         base=0, pattern=[[-16, 8]], channel_multiplier=1))
            step.link(pool.affine_select(out=own16[:, :], in_=own16[:, :], compare_op=ALU.is_ge, fill=0.0,
                                         base=15, pattern=[[16, 8]], channel_multiplier=-1))
            step.link(pool.memset(self_f[:, :, :], 0.0))
            for first in (0, DH):
                step.link(pool.affine_select(out=self_f[:, :, :], in_=self_f[:, :, :], compare_op=ALU.not_equal,
                                             fill=1.0, base=-first, pattern=[[-1, H], [0, P]], channel_multiplier=1))
            pool.memset(mix[:, :, :, :, :], 0.0).then_inc(const_done, 1)
            pool.memset(pv[:, :, :, :, :], 0.0).then_inc(const_done, 1)
            pool.memset(v[:, :, DH:DV1], 1.0).then_inc(const_done, 1)
            pool.memset(nmT[:, :].bitcast(F32), 0.0).then_inc(const_done, 1)

            pool.wait_ge(sel_ready, 1)

            def keep(ap, base, pattern, channel, last=False):
                ins = pool.affine_select(out=ap, in_=ap, compare_op=ALU.is_ge, fill=0.0, base=base, pattern=pattern,
                                         channel_multiplier=channel)
                if last:
                    ins.then_inc(masks_done, 1)
                else:
                    step.link(ins)

            step.link(pool.memset(m3[:, :, :], 1.0))
            step.link(pool.memset(m3[CH:P, 0, 0:CH], 0.0))
            step.link(pool.memset(m3[0:CH, 1:3, CH:P], 0.0))
            keep(m3[:, 0, :], -1, [[-1, P]], 1, True)
            keep(m3[:, 1, :], -1, [[1, P]], -1, True)
            keep(m3[:, 2, :], 0, [[1, P]], -1, True)
            step.link(pool.memset(mhead, 1.0))
            keep(mhead, 0, [[-DP, HD], [0, DV]], 1)
            keep(mhead, DP - 1, [[DP, HD], [0, DV]], -1, True)
            for k in range(LEVELS):
                s, mask_k = 1 << k, m0[:, 0, :] if k == 0 else mlev[:, k - 1, :]
                halves = mask_k.rearrange("p (n two s) -> p n two s", two=2, s=s)
                step.link(pool.memset(mask_k, 1.0))
                step.link(pool.memset(halves[:, :, 1, :], 0.0))
                keep(halves[:, :, 0, :], -s, [[-2 * s, P // (2 * s)], [0, s]], 1)
                keep(halves[:, :, 0, :], 2 * s - 1, [[2 * s, P // (2 * s)], [0, s]], -1)
            step.link(pool.memset(m0[:, 1, :], 0.0))
            odd = m0[:, 1, :].rearrange("p (n two) -> p n two", two=2)[:, :, 1]
            step.link(pool.affine_select(out=odd, in_=odd, compare_op=ALU.not_equal, fill=1.0, base=0,
                                         pattern=[[-2, P // 2]], channel_multiplier=1))
            pool.wait_ge(const_done, CONSTS)
            for m in (m0, mlev):
                pool.tensor_tensor(m, ident[:, :].unsqueeze(1).to_broadcast([P, m.shape[1], P]), m, ALU.subtract).then_inc(masks_done, 1)

            def delta_turn(jobs, i, tag, inverse, scan, front, s):
                AA, XX = AA_of[1 - s], XX_of[1 - s]
                for stage, what in DELTA_ORDER:
                    if stage == "front" and front is not None:
                        if what == "stats":
                            pool.wait_ge(var_ready, front + (B + 1))
                            pool.tensor_tensor(rstd[:, :], vare[:, :], neg_half16[:, 0:NT], ALU.pow).then_inc(rstd_ready, 1)
                        elif what == "norms":
                            pool.wait_ge(ss_ready, front + 1)
                            pool.tensor_tensor(rn[:, :, :], ss[:, :, :], neg_half16[:, :].rearrange("p (n g) -> p n g", n=NT),
                                               ALU.pow).then_inc(rn_ready, 1)
                    if stage == "scan" and scan is not None and what == "square":
                        pool.wait_ge(ms_ready, scan + 1)
                        pool.tensor_tensor(rr[:, :, :], ms[:, :, :], neg_half16[:, 0:NT * HD].rearrange("p (n g) -> p n g", n=NT),
                                           ALU.pow).then_inc(rr_ready, 1)

            def ffn_turn(phase):
                def turn_of(jobs, i, back, front):
                    if front is not None:
                        n, ln = front + phase * B, front + 2 * phase * B
                        pool.wait_ge(var_ready, ln + 1)
                        pool.tensor_tensor(rstd[:, :], vare[:, :], neg_half16[:, 0:NT], ALU.pow).then_inc(rstd_ready, 1)
                        pool.wait_ge(mixT_ready, n + 1)
                        pool.tensor_tensor(bdv[:, :, :, :],
                                           mixT[:, :, :].rearrange("p h l -> p l h").unsqueeze(2).to_broadcast([P, NL, 8, H]),
                                           own16[:, :].unsqueeze(1).unsqueeze(3).to_broadcast([P, NL, 8, H]),
                                           ALU.mult).then_inc(bdv_ready, 1)
                    if back is not None:
                        pool.wait_ge(maskT_ready, back + (phase * B + 1))
                        pool.tensor_tensor(bdo[:, :, :, :],
                                           maskT[:, :, :].rearrange("p e l -> p l e").unsqueeze(2).to_broadcast([P, NL, 8, E]),
                                           own16[:, :].unsqueeze(1).unsqueeze(3).to_broadcast([P, NL, 8, E]),
                                           ALU.mult).then_inc(bdo_ready, 1)
                return turn_of

            ffn_loop(pool, 0, ffn_turn(0))
            if PHASES > 1:
                delta_loop(pool, delta_turn)
            if PHASES > 2:
                ffn_loop(pool, 1, ffn_turn(1))

        @block.vector
        def _(dve):
            step = Chain(dve, dve_step)
            dve.wait_ge(const_done, CONSTS)
            dve.wait_ge(pool_step, POOL_STEPS)
            dve.tensor_copy(sel[:, :, :], self_f[:, :, :]).then_inc(sel_ready, 1)
            for b in range(2, 8):
                dve.sem_inc(free[b], 1)
            for j in range(4):
                dve.wait_ge(wT_hi, j + 1)
                dve.tensor_tensor(WTl[:, 4 * j:4 * j + 4, :], bank[j % 2][:, :].rearrange("p (n c) -> p n c", c=P),
                                  WTh[:, 4 * j:4 * j + 4, :].bitcast(F32), ALU.subtract).then_inc(free[j % 2], 1)

            def layer_stats(i):
                for t in range(NT):
                    last = dve.bn_stats(stat[:, t, :], x[:, bass.ds(i * NT + t, 1), :].rearrange("p a c -> p (a c)"))
                step.link(last)
                dve.tensor_tensor(mv[:, :, 0], stat[:, :, 1], stat[:, :, 4], ALU.add)
                dve.tensor_tensor(mv[:, :, 1], stat[:, :, 1], stat[:, :, 4], ALU.subtract)
                step.link(dve.tensor_tensor(mv[:, :, 2], stat[:, :, 2], stat[:, :, 5], ALU.add))
                dve.tensor_scalar(mean[:, :], mv[:, :, 0], 0.5, None, ALU.mult)
                dve.scalar_tensor_tensor(mv[:, :, 3], mv[:, :, 1], 0.25, mv[:, :, 1], ALU.mult, ALU.mult)
                step.link(dve.tensor_scalar(mv[:, :, 2], mv[:, :, 2], 1.0 / C, EPS, ALU.mult, ALU.add))
                dve.tensor_tensor(vare[:, :], mv[:, :, 2], mv[:, :, 3], ALU.add).then_inc(var_ready, 1)

            def normalize(i, ln):
                dve.wait_ge(rstd_ready, ln + 1)
                for t in range(NT):
                    dve.tensor_scalar(xn[:, t, :], x[:, bass.ds(i * NT + t, 1), :].rearrange("p a c -> p (a c)"),
                                      mean[:, t:t + 1], rstd[:, t:t + 1], ALU.subtract, ALU.mult).then_inc(xn_ready, 1)

            def delta_turn(jobs, i, tag, inverse, scan, front, s):
                qk_w, v_w = 2 * HD * DK, HD * DV

                def heads_over(ap, width):
                    return ap.unsqueeze(3).to_broadcast([P, NT, HD, width])

                def by_head(ap, width):
                    return ap.rearrange("p n (h d) -> p n h d", d=width)

                def front_step(what):
                    AA, qkp, vb, gn = AA_of[1 - s], qkp_of[1 - s], vb_of[1 - s], gn_of[1 - s]
                    beta = sg[:, :, v_w:v_w + HD]
                    if what == "stats":
                        layer_stats(front)
                    elif what == "normalize":
                        normalize(front, front + B)
                    elif what == "conv3":
                        moved(dve, jobs, f"xT{tag}", i)
                        step.link(dve.tensor_scalar(hacc[:, :], xpad[:, 3:3 + L], convw[:, 3:4], None, ALU.mult))
                    elif what in ("conv2", "conv1"):
                        k = int(what[4])
                        step.link(dve.scalar_tensor_tensor(hacc[:, :], xpad[:, k:k + L], convw[:, k:k + 1], hacc[:, :], ALU.mult, ALU.add))
                    elif what == "conv0":
                        dve.scalar_tensor_tensor(hacc[:, :], xpad[:, 0:L], convw[:, 0:1], hacc[:, :], ALU.mult, ALU.add).then_inc(conv_ready, 1)
                    elif what == "silu":
                        dve.wait_ge(hexp_ready, front + 1)
                        step.link(dve.tensor_scalar(hexp[:, :], hexp[:, :], 1.0, None, ALU.add))
                        step.link(dve.reciprocal(hexp[:, :], hexp[:, :]))
                        dve.tensor_tensor(hT[:, :], hacc[:, :], hexp[:, :], ALU.mult).then_inc(hT_ready, 1)
                    elif what == "norms":
                        moved(dve, jobs, f"proj0{tag}", i)
                        moved(dve, jobs, f"proj1{tag}", i)
                        step.link(dve.tensor_tensor(sqs[:, :, :], pr[:, :, 0:qk_w], pr[:, :, 0:qk_w], ALU.mult))
                        step.link(dve.tensor_reduce(ss[:, :, :], sqs[:, :, :].rearrange("p n (g d) -> p n g d", d=DK), X, ALU.add))
                        dve.tensor_scalar(ss[:, :, :], ss[:, :, :], 1e-24, None, ALU.max).then_inc(ss_ready, 1)
                    elif what == "sigmoids0":
                        dve.wait_ge(gexp_ready, front + 1)
                        step.link(dve.tensor_scalar(sg[:, :, :], sg[:, :, :], 1.0, None, ALU.add))
                        dve.reciprocal(sg[:, 0, :], sg[:, 0, :])
                    elif what == "sigmoids1":
                        step.link(dve.reciprocal(sg[:, 1, :], sg[:, 1, :]))
                    elif what == "keys":
                        dve.wait_ge(rn_ready, front + 1)
                        for w, at, g in ((2, 0, 0), (0, HD * DK, HD)):
                            step.link(dve.tensor_tensor(qkp[:, :, w, :, 0:DK], by_head(pr[:, :, at:at + HD * DK], DK),
                                                        heads_over(rn[:, :, g:g + HD], DK), ALU.mult))
                        dve.tensor_tensor(qkp[:, :, 1, :, 0:DK], qkp[:, :, 0, :, 0:DK], heads_over(beta, DK), ALU.mult).then_inc(qkp_ready, 1)
                    elif what == "gates":
                        dve.tensor_tensor(by_head(vb[:, :, :], DV), by_head(pr[:, :, qk_w:qk_w + v_w], DV), heads_over(beta, DV), ALU.mult)
                        step.link(dve.tensor_tensor(gn[:, :, :], pr[:, :, qk_w + v_w:qk_w + 2 * v_w], sg[:, :, 0:v_w], ALU.mult))
                        step.link(dve.tensor_tensor(by_head(gn[:, :, :], DV), by_head(gn[:, :, :], DV),
                                                    normw[:, :].unsqueeze(1).unsqueeze(1).to_broadcast([P, NT, HD, DV]), ALU.mult))
                    elif what.startswith("gram"):
                        b, g = jobs.bank(what + tag), HD * int(what[4]) + int(what[5])
                        filled(dve, jobs, what + tag, i)
                        dve.tensor_tensor(AA[:, g, :, :], bank[b][:, 0:3 * P].rearrange("p (w t) -> p w t", w=3),
                                          m3[:, :, :], ALU.mult).then_inc(free[b], 1)

                    elif what.startswith("X0"):
                        t = int(what[3])
                        at = AA[:, HD * t:HD * t + HD, 0:2, :]
                        for h in range(HD):
                            moved(dve, jobs, f"gram{t}{h}{tag}", i)
                        step.link(dve.tensor_tensor(at, at, ident[:, :].unsqueeze(1).unsqueeze(1).to_broadcast([P, HD, 2, P]), ALU.add))
                        dve.tensor_tensor(XX_of[1 - s][:, HD * t:HD * t + HD, :, :].rearrange("p h w t -> p h (w t)"),
                                          at.rearrange("p h w t -> p h (w t)"),
                                          m0[:, :, :].rearrange("p w t -> p (w t)").unsqueeze(1).to_broadcast([P, HD, 2 * P]),
                                          ALU.mult).then_inc(X0_ready, 1)

                def scan_step(what):
                    gn = gn_of[1 - s]
                    if what == "start":
                        step.link(dve.tensor_copy(U[0:CH, 0, :], Uv[0:CH, 0, :]))
                        dve.sem_inc(U_ready, 1)
                    elif what[0] == "S":
                        c, b = int(what[1]), jobs.bank(what + tag)
                        filled(dve, jobs, what + tag, i)
                        dve.tensor_tensor(St[:, c, :], bank[b][:, 0:P], mhead, ALU.mult).then_inc(free[b], 1)
                    elif what[0:2] == "ws":
                        c, b = int(what[2]), jobs.bank(what + tag)
                        t, r = c // 2, slice(CH * (c % 2), CH * (c % 2) + CH)
                        filled(dve, jobs, what + tag, i)
                        step.link(dve.tensor_tensor(U[r, t, :], Uv[r, t, :], bank[b][r, 0:P], ALU.subtract))
                        dve.sem_inc(U_ready, 1)
                        dve.sem_inc(free[b], 1)
                    elif what == "square":
                        moved(dve, jobs, f"o0{tag}", i)
                        moved(dve, jobs, f"o1{tag}", i)
                        step.link(dve.tensor_tensor(osq[:, :, :], o_sb[:, :, :], o_sb[:, :, :], ALU.mult))
                        step.link(dve.tensor_reduce(msc[:, :, :], by_head(osq[:, :, :], DV), X, ALU.add))
                        dve.tensor_scalar(ms[:, :, :], msc[:, :, :], 1.0 / DV, EPS, ALU.mult, ALU.add).then_inc(ms_ready, 1)
                        step.link(dve.tensor_tensor(y[:, :, :], o_sb[:, :, :], gn[:, :, :], ALU.mult))
                    elif what == "gate":
                        dve.wait_ge(rr_ready, scan + 1)
                        dve.tensor_tensor(by_head(y[:, :, :], DV), by_head(y[:, :, :], DV), heads_over(rr[:, :, :], DV), ALU.mult).then_inc(y_ready, 1)
                    elif what == "residual":
                        b = jobs.bank(f"fin{tag}")
                        filled(dve, jobs, f"fin{tag}", i)
                        xi = x[:, bass.ds(scan * NT, NT), :]
                        dve.tensor_tensor(xi, xi, bank[b][:, 0:NT * C].rearrange("p (n c) -> p n c", c=C), ALU.add).then_inc(free[b], 1)

                for stage, what in DELTA_ORDER:
                    if stage == "inverse" and inverse is not None and what[0] == "T":
                        k, t = what[1:]
                        job = f"T{k}{t}{tag}"
                        filled(dve, jobs, job, i)
                        dve.tensor_tensor(TT[:, t, :, :], bank[jobs.bank(job)][:, :].rearrange("p (h t) -> p h t", h=HD),
                                          mlev[:, k - 1, :].unsqueeze(1).to_broadcast([P, HD, P]),
                                          ALU.mult).then_inc(free[jobs.bank(job)], 1)
                    elif stage == "scan" and scan is not None:
                        scan_step(what)
                    elif stage == "front" and front is not None:
                        front_step(what)
                if inverse is not None:
                    moved(dve, jobs, f"Uv{tag}", i)

            def ffn_turn(phase):
                def turn_of(jobs, i, back, front):
                    n, ln = (None, None) if front is None else (front + phase * B, front + 2 * phase * B)

                    def groups(ap):
                        return ap.unsqueeze(2).to_broadcast([P, 64, E])

                    ties = tie[:, :].unsqueeze(1).to_broadcast([P, 64, E])

                    def top_two(part):
                        if part == 0:
                            moved(dve, jobs, "gate", i)
                            step.link(dve.tensor_reduce(gmax[:, :], gate[:, :, :], X, ALU.max))
                            step.link(dve.tensor_tensor(gdif[:, :, :], gate[:, :, :], groups(gmax[:, :]), ALU.subtract))
                            step.link(dve.scalar_tensor_tensor(gsel[:, :, :], gdif[:, :, :], 0.0, ties, ALU.is_ge, ALU.mult))
                        elif part == 1:
                            step.link(dve.tensor_reduce(grank[:, :], gsel[:, :, :], X, ALU.max))
                            step.link(dve.tensor_tensor(gsel2[:, :, :], gsel[:, :, :], groups(grank[:, :]), ALU.is_equal))
                            step.link(dve.scalar_tensor_tensor(gdif[:, :, :], gsel2[:, :, :], NEG_BIG, gdif[:, :, :], ALU.mult, ALU.add))
                        elif part == 2:
                            step.link(dve.tensor_reduce(gmax[:, :], gdif[:, :, :], X, ALU.max))
                            step.link(dve.tensor_tensor(gdif[:, :, :], gdif[:, :, :], groups(gmax[:, :]), ALU.subtract))
                            step.link(dve.scalar_tensor_tensor(gsel[:, :, :], gdif[:, :, :], 0.0, ties, ALU.is_ge, ALU.mult))
                        elif part == 3:
                            step.link(dve.tensor_reduce(grank[:, :], gsel[:, :, :], X, ALU.max))
                            step.link(dve.tensor_tensor(gsel[:, :, :], gsel[:, :, :], groups(grank[:, :]), ALU.is_equal))
                            step.link(dve.tensor_tensor(mask[:, :, :, :, :].rearrange("p n s h e -> p (n s h) e"),
                                                        gsel[:, :, :], gsel2[:, :, :], ALU.add))

                    def value_mix():
                        dve.wait_ge(egate_ready, n + 1)
                        step.link(dve.tensor_scalar(sig[:, :, :, :], egate[:, :, :, :], 1.0, None, ALU.add))
                        step.link(dve.reciprocal(sig[:, :, :, :], sig[:, :, :, :]))
                        step.link(dve.tensor_tensor(mix[:, :, :, :, 0].rearrange("p h n e -> p n h e"), mask[:, :, 0, :, :],
                                                    sig[:, :, :, :], ALU.mult))
                        dve.transpose(mixT[:, :, :], mix[:, :, :, :, :].rearrange("p h n e x -> p h (n e x)")).then_inc(mixT_ready, 1)

                    def values_turned():
                        moved(dve, jobs, "pv0", i)
                        moved(dve, jobs, "pv1", i)
                        dve.transpose(pvT[:, :, :].rearrange("p l d -> p d l"),
                                      pv[:, :, :, :, :].rearrange("p n e x d -> p d (n e x)")).then_inc(pvT_ready, 1)

                    def low_part(c):
                        b = jobs.bank(f"qk{c}")
                        dve.wait_ge(qkhi_ready, NPAIR * n + (c + 1))
                        dve.tensor_tensor(qkl[:, c, :, :], bank[b][:, :].rearrange("p (a t) -> p a t", a=2),
                                          qkh[:, c, :, :].bitcast(F32), ALU.subtract).then_inc(free[b], 1)

                    def head_max(h):
                        b = jobs.bank(f"S{h}")
                        filled(dve, jobs, f"S{h}", i)
                        dve.tensor_reduce(negm[:, :, h], bank[b][:, :].rearrange("p (n j) -> p n j", n=NT),
                                          X, ALU.max, negate=True).then_inc(free[b], 1)

                    if back is not None:
                        step.link(dve.tensor_copy(masko[:, :, :, :], mask[:, :, 1, :, :]))
                    if front is not None:
                        layer_stats(front)
                        normalize(front, ln)
                        moved(dve, jobs, "xT", i)
                        dve.tensor_tensor(xTl[:, :], xT[:, :], xTh[:, :].bitcast(F32), ALU.subtract).then_inc(xlo_ready, 1)
                        top_two(0)
                        for k in range(2, 10):
                            for c in PROJECT.get(k, ()):
                                low_part(c)
                                if k == 8 and c == 6:
                                    head_max(10)
                                    head_max(11)
                            for c in SHIFT.get(k, ()):
                                if (k, c) != (8, 5):
                                    head_max(2 * c)
                                    head_max(2 * c + 1)
                            if k == 2:
                                top_two(1)
                            elif k == 3:
                                top_two(2)
                            elif k == 4:
                                top_two(3)
                            elif k == 5:
                                value_mix()
                            elif k == 6:
                                values_turned()
                    if back is not None:
                        nb = back + phase * B
                        moved(dve, jobs, "at6", i)
                        moved(dve, jobs, "at7", i)
                        step.link(dve.reciprocal(rden[:, :], attn[:, :, :, DH].rearrange("p n h -> p (n h)")))
                        step.link(dve.tensor_tensor(maskw[:, :, :].rearrange("p e (n h) -> p n h e", n=NT), masko[:, :, :, :],
                                                    rden[:, :].rearrange("p (n h) -> p n h", n=NT).unsqueeze(3).to_broadcast([P, NT, H, E]),
                                                    ALU.mult))
                        dve.transpose(maskT[:, :, :], maskw[:, :, :]).then_inc(maskT_ready, 1)
                        dve.transpose(aT[:, :, :].rearrange("p l d -> p d l"),
                                      attn[:, :, :, 0:DH].rearrange("p n h d -> p d (n h)")).then_inc(aT_ready, 1)
                    if front is not None:
                        moved(dve, jobs, "vmix2", i)
                        moved(dve, jobs, "vmix3", i)
                        dve.transpose(v[:, :, 0:DH].rearrange("p g d -> p d g"),
                                      vm[:, :, :].rearrange("p l d -> p d l")).then_inc(v_ready, 1)
                    if back is not None:
                        xi = x[:, bass.ds(back * NT, NT), :]
                        filled(dve, jobs, "res", i)
                        dve.scalar_tensor_tensor(xi, bank[jobs.bank("res")][:, 0:NT * C].rearrange("p (n c) -> p n c", c=C),
                                                 0.5, xi, ALU.mult, ALU.add).then_inc(free[jobs.bank("res")], 1)
                return turn_of

            dve.wait_ge(hid_in, 16)
            ffn_loop(dve, 0, ffn_turn(0), step, DVE_FFN)
            if PHASES > 1:
                dve.wait_ge(masks_done, MASKS)
                dve.wait_ge(dw_in, 8 * 16)
                moved(dve, ffn[0][2], "res", 0)
                step.link(dve.memset(xpad[:, 0:3], 0.0))
                for qkp in qkp_of:
                    step.link(dve.memset(qkp[:, :, :, :, DK:DP], 0.0))
                step.link(dve.memset(St[:, 0, :], 0.0))
                delta_loop(dve, delta_turn, step, DVE_DELTA)
            if PHASES > 2:
                moved(dve, delta[4], "fin", 0)
                ffn_loop(dve, 1, ffn_turn(1), step, DVE_FFN)

        @block.scalar
        def _(act):
            for j in range(6):
                filled(act, setup, f"w{j}", 0)
                src = bank[j % 2][:, :].rearrange("p (n c) -> p n c", c=P)
                if j < 4:
                    act.activation(WTh[:, 4 * j:4 * j + 4, :], src, ACT.Copy).then_inc(wT_hi, 1)
                elif j == 4:
                    act.activation(WvT[:, :], bank[0][:, :], ACT.Copy).then_inc(free[0], 1)
                else:
                    act.activation(WgT[:, :], bank[1][:, 0:2 * P], ACT.Copy).then_inc(free[1], 1)
            for j in range(6, 8):
                filled(act, setup, f"w{j}", 0)
                act.activation(WoT[:, 4 * (j - 6):4 * (j - 6) + 4, :],
                               bank[j % 2][0:DH, :].rearrange("p (n c) -> p n c", c=P), ACT.Copy).then_inc(free[j % 2], 1)

            def ffn_turn(phase):
                def turn_of(jobs, i, back, front):
                    def read(name):
                        filled(act, jobs, name, i)
                        return bank[jobs.bank(name)]

                    def freeing(name):
                        return free[jobs.bank(name)]

                    def probabilities(h):
                        o = read(f"ST{h}")
                        if h >= 4:
                            filled(act, jobs, f"at{h // 2 - 2}", i)
                        act.activation(PT[:, h % 4, :, :], o[:, :].rearrange("p (n t) -> p n t", n=NT),
                                       ACT.Exp, scale=DH ** -0.5).then_inc(freeing(f"ST{h}"), 1)

                    def attn_out(g):
                        act.activation(attn[:, :, 2 * g:2 * g + 2, :].rearrange("p n h d -> p h n d"),
                                       read(f"at{g}")[:, 0:4 * DV1].rearrange("p (h n d) -> p h n d", h=2, n=NT),
                                       ACT.Copy).then_inc(freeing(f"at{g}"), 1)

                    def high_part(c):
                        act.activation(qkh[:, c, :, :], read(f"qk{c}")[:, :].rearrange("p (a t) -> p a t", a=2),
                                       ACT.Copy).then_inc(qkhi_ready, 1)

                    def expert_values(t):
                        act.activation(pv[:, t, :, 0, :], read(f"pv{t}")[:, :].rearrange("p (e d) -> p e d", d=DH),
                                       ACT.Copy).then_inc(freeing(f"pv{t}"), 1)

                    for k in range(9):
                        if back is not None and k < 8:
                            probabilities(2 * k)
                            probabilities(2 * k + 1)
                        if front is not None and k == 1:
                            act.activation(xT[:, :], read("xT")[:, 0:L], ACT.Copy)
                            act.activation(xTh[:, :], read("xT")[:, 0:L], ACT.Copy).then_inc(freeing("xT"), 1)
                            act.activation(gate[:, :, :], read("gate")[:, :].rearrange("p (g e) -> p g e", e=E),
                                           ACT.Copy).then_inc(freeing("gate"), 1)
                            moved(act, jobs, "gate", i)
                            act.activation(egate[:, :, :, :], gate[:, :, :].rearrange("p (n s h) e -> p n s (h e)", n=NT, s=2)[:, :, 0, :],
                                           ACT.Exp, scale=-1.0).then_inc(egate_ready, 1)
                            expert_values(0)
                        if front is not None and k == 2:
                            expert_values(1)
                        if front is not None:
                            for c in PROJECT.get(k, ())[0:1]:
                                high_part(c)
                        if back is not None and k >= 1:
                            attn_out(k - 1)
                        if front is not None:
                            for c in PROJECT.get(k, ())[1:]:
                                high_part(c)
                    if front is not None:
                        for j in range(4):
                            act.activation(vm[:, 8 * j:8 * j + 8, :], read(f"vmix{j}")[:, :].rearrange("p (l d) -> p l d", d=DH),
                                           ACT.Copy).then_inc(freeing(f"vmix{j}"), 1)
                        act.activation(nmT[0:H, :], read("mT")[0:H, 0:L], ACT.Copy)
                        act.activation(nmT[DH:DH + H, :], read("mT")[0:H, 0:L], ACT.Copy).then_inc(freeing("mT"), 1)
                    if back is not None:
                        for j in range(4):
                            act.activation(yT[:, :, :, :, 8 * j:8 * j + 8].rearrange("p n e q l -> p q (n e) l"),
                                           read(f"omix{j}")[0:DH, :].rearrange("p (l q c) -> p q c l", q=NQ, c=NT * E),
                                           ACT.Copy).then_inc(freeing(f"omix{j}"), 1)
                return turn_of

            def delta_turn(jobs, i, tag, inverse, scan, front, s):
                XX, qkT = XX_of[s], qkT_of[1 - s]

                def out_of(job):
                    filled(act, jobs, job + tag, i)
                    return bank[jobs.bank(job + tag)]

                def freeing(job):
                    return free[jobs.bank(job + tag)]

                for stage, what in DELTA_ORDER:
                    if stage == "inverse" and inverse is not None:
                        if what[0] in ("U", "V") and what != "Uv":
                            (w, k, t), job = what, f"{what[0]}{what[1]}{what[2]}"
                            act.activation(XX[:, HD * t:HD * t + HD, 0 if w == "U" else 1, :],
                                           out_of(job)[:, :].rearrange("p (h t) -> p h t", h=HD), ACT.Copy).then_inc(freeing(job), 1)
                        elif what == "WT":
                            act.activation(WT[:, :], out_of("WT")[:, 0:L], ACT.Copy).then_inc(freeing("WT"), 1)
                        elif what == "Uv":
                            act.activation(Uv[:, :, :].rearrange("p n m -> p (n m)"), out_of("Uv")[:, 0:L], ACT.Copy).then_inc(freeing("Uv"), 1)
                    elif stage == "scan" and scan is not None:
                        if what == "out":
                            for t in range(NT):
                                act.activation(o_sb[:, t, :], out_of(f"o{t}")[:, 0:P], ACT.Copy).then_inc(freeing(f"o{t}"), 1)
                        elif what == "turn":
                            act.activation(yT_d[:, :], out_of("yT")[:, 0:L], ACT.Copy).then_inc(freeing("yT"), 1)
                    elif stage == "front" and front is not None:
                        if what == "xT":
                            act.activation(xpad[:, 3:3 + L], out_of("xT")[:, 0:L], ACT.Copy).then_inc(freeing("xT"), 1)
                        elif what == "conv0":
                            act.wait_ge(conv_ready, front + 1)
                            act.activation(hexp[:, :], hacc[:, :], ACT.Exp, scale=-1.0).then_inc(hexp_ready, 1)
                        elif what == "proj":
                            for t in range(NT):
                                act.activation(pr[:, t, :], out_of(f"proj{t}")[:, 0:NPR], ACT.Copy).then_inc(freeing(f"proj{t}"), 1)
                            moved(act, jobs, f"proj0{tag}", i)
                            moved(act, jobs, f"proj1{tag}", i)
                            act.activation(sg[:, :, :], pr[:, :, NPR - HD * DV - HD:NPR], ACT.Exp, scale=-1.0).then_inc(gexp_ready, 1)
                        elif what == "tq":
                            for t in range(NT):
                                act.activation(qkT[:, t, :, :].rearrange("p w t -> p (w t)"), out_of(f"tq{t}")[:, 0:3 * P],
                                               ACT.Copy).then_inc(freeing(f"tq{t}"), 1)

            ffn_loop(act, 0, ffn_turn(0))
            if PHASES > 1:
                delta_loop(act, delta_turn)
            if PHASES > 2:
                ffn_loop(act, 1, ffn_turn(1))

        @block.tensor
        def _(pe):
            pe.wait_ge(const_done, CONSTS)
            pe.wait_ge(w_in, 6 * 16)
            for j in range(6):
                turn(pe, setup, f"w{j}", 0)
                for k in range(4 if j < 5 else 2):
                    last = pe.transpose(bank[j % 2][:, P * k:P * k + P], wst[:, 4 * j + k, :], ident[:, :])
                last.then_inc(full[j % 2], 1)
            for j in range(6, 8):
                turn(pe, setup, f"w{j}", 0)
                for k in range(4):
                    last = pe.transpose(bank[j % 2][0:DH, P * k:P * k + P], wost[:, 4 * (j - 6) + k, :], ident[:, :])
                last.then_inc(full[j % 2], 1)

            def ffn_turn(phase):
                def turn_of(jobs, i, back, front):
                    def out_of(name):
                        turn(pe, jobs, name, i)
                        return bank[jobs.bank(name)]

                    def done(last, name):
                        last.then_inc(full[jobs.bank(name)], 1)

                    def inputs_turned():
                        o = out_of("xT")
                        pe.wait_ge(xn_ready, 2 * front + (4 * phase * B + 2))
                        for t in range(NT):
                            last = pe.transpose(o[:, P * t:P * t + P], xn[:, t, :], ident[:, :])
                        done(last, "xT")

                    def gates():
                        moved(pe, jobs, "xT", i)
                        o = out_of("gate")
                        for t in range(NT):
                            last = pe.matmul(o[:, 2 * P * t:2 * P * t + 2 * P], xT[:, P * t:P * t + P], WgT[:, :], start=True, stop=True)
                        done(last, "gate")

                    def expert_values(t):
                        o = out_of(f"pv{t}")
                        done(pe.matmul(o[:, :], xT[:, P * t:P * t + P], WvT[:, :], start=True, stop=True), f"pv{t}")

                    def project(c):
                        o = out_of(f"qk{c}")
                        for a in range(2):
                            w, oa = NPAIR * a + c, o[:, L * a:L * a + L]
                            pe.matmul(oa, WTh[:, w, :], xTh[:, :], start=True, stop=False)
                            pe.matmul(oa, WTh[:, w, :], xTl[:, :], start=False, stop=False)
                            last = pe.matmul(oa, WTl[:, w, :], xTh[:, :], start=False, stop=True)
                        done(last, f"qk{c}")

                    def shift_scores(h):
                        o, r, c = out_of(f"S{h}"), heads(h, 0), h // 2
                        for t in range(NT):
                            last = pe.matmul(o[:, L * t:L * t + L], qkh[r, c, 0, P * t:P * t + P], qkh[r, c, 1, :], start=True, stop=True)
                        done(last, f"S{h}")

                    def scores(h):
                        o, r, c = out_of(f"ST{h}"), heads(h, 0), h // 2
                        for t in range(NT):
                            ot, tj = o[:, L * t:L * t + L], slice(P * t, P * t + P)
                            pe.matmul(ot, qkh[r, c, 1, tj], qkh[r, c, 0, :], start=True, stop=False)
                            pe.matmul(ot, qkh[r, c, 1, tj], qkl[r, c, 0, :], start=False, stop=False)
                            pe.matmul(ot, qkl[r, c, 1, tj], qkh[r, c, 0, :], start=False, stop=False)
                            last = pe.matmul(ot, sel[r, h, :], nmT[r, :], start=False, stop=True)
                        done(last, f"ST{h}")

                    def attend(h):
                        g = h // 2
                        o = out_of(f"at{g}") if h % 2 == 0 else bank[jobs.bank(f"at{g}")]
                        moved(pe, jobs, f"ST{h}", i)
                        for t in range(NT):
                            ot = o[:, (2 * (h % 2) + t) * DV1:(2 * (h % 2) + t + 1) * DV1]
                            for tj in range(NT):
                                last = pe.matmul(ot, PT[:, h % 4, tj, P * t:P * t + P], v[:, H * tj + h, :],
                                                 start=(tj == 0), stop=(tj == NT - 1))
                        if h % 2:
                            done(last, f"at{g}")

                    for k in range(10):
                        if back is not None and k < 8:
                            scores(2 * k)
                            scores(2 * k + 1)
                        if front is not None and k == 1:
                            inputs_turned()
                        if back is not None and 1 <= k <= 8:
                            if k == 1:
                                pe.wait_ge(v_ready, back + (phase * B + 1))
                            attend(2 * k - 2)
                            attend(2 * k - 1)
                        if front is not None and k == 1:
                            gates()
                            expert_values(0)
                        if front is not None and k == 2:
                            expert_values(1)
                            pe.wait_ge(xlo_ready, front + (phase * B + 1))
                        if front is not None:
                            for c in PROJECT.get(k, ()):
                                project(c)
                            for c in SHIFT.get(k, ()):
                                pe.wait_ge(qkhi_ready, NPAIR * front + (NPAIR * phase * B + c + 1))
                                shift_scores(2 * c)
                                shift_scores(2 * c + 1)
                    if front is not None:
                        pe.wait_ge(pvT_ready, front + (phase * B + 1))
                        pe.wait_ge(bdv_ready, front + (phase * B + 1))
                        for j in range(4):
                            o = out_of(f"vmix{j}")
                            for k in range(8):
                                last = pe.matmul(o[:, DH * k:DH * k + DH], bdv[:, 8 * j + k, :, :].rearrange("p m h -> p (m h)"),
                                                 pvT[:, 8 * j + k, :], start=True, stop=True)
                            done(last, f"vmix{j}")
                        o = out_of("mT")
                        moved(pe, jobs, "S14", i)
                        moved(pe, jobs, "S15", i)
                        for t in range(NT):
                            last = pe.transpose(o[0:H, P * t:P * t + P], negm[:, t, :], ident[:, :])
                        done(last, "mT")
                    if back is not None:
                        pe.wait_ge(aT_ready, back + (phase * B + 1))
                        pe.wait_ge(bdo_ready, back + (phase * B + 1))
                        for j in range(4):
                            o = out_of(f"omix{j}")
                            for k in range(8):
                                last = pe.matmul(o[0:DH, DH * k:DH * k + DH], aT[:, 8 * j + k, :],
                                                 bdo[:, 8 * j + k, :, :].rearrange("p m e -> p (m e)"), start=True, stop=True)
                            done(last, f"omix{j}")
                        o = out_of("res")
                        moved(pe, jobs, "omix2", i)
                        moved(pe, jobs, "omix3", i)
                        for t in range(NT):
                            for e in range(E):
                                last = pe.matmul(o[:, C * t:C * t + C], yT[:, t, e, :, :].rearrange("d q l -> d (q l)"), WoT[:, e, :],
                                                 start=(e == 0), stop=(e == E - 1))
                        done(last, "res")
                    if front is not None:
                        moved(pe, jobs, "qk6", i)
                        moved(pe, jobs, "qk7", i)
                        moved(pe, jobs, "mT", i)
                return turn_of

            def delta_turn(jobs, i, tag, inverse, scan, front, s):
                def out_of(job):
                    turn(pe, jobs, job + tag, i)
                    return bank[jobs.bank(job + tag)]

                def done(last, job):
                    last.then_inc(full[jobs.bank(job + tag)], 1)

                def wait_moved(job):
                    moved(pe, jobs, job + tag, i)

                def inverse_step(what):
                    AA, XX, qkp, vb = AA_of[s], XX_of[s], qkp_of[s], vb_of[s]
                    if what == "WT":
                        wait_moved(f"V{LEVELS - 1}0")
                        wait_moved(f"V{LEVELS - 1}1")
                        o = out_of("WT")
                        for t in range(NT):
                            for h in range(HD):
                                last = pe.matmul(o[DP * h:DP * h + DP, P * t:P * t + P], qkp[:, t, 1, h, :], XX[:, HD * t + h, 1, :],
                                                 start=True, stop=True)
                        done(last, "WT")
                    elif what == "Uv":
                        o = out_of("Uv")
                        for t in range(NT):
                            for h in range(HD):
                                last = pe.matmul(o[:, P * t + DV * h:P * t + DV * h + DV], XX[:, HD * t + h, 1, :],
                                                 vb[:, t, DV * h:DV * h + DV], start=True, stop=True)
                        done(last, "Uv")
                    else:
                        w, k, t = what
                        if w == "T":
                            if k == 1:
                                pe.wait_ge(X0_ready, 2 * inverse + (t + 1))
                            else:
                                wait_moved(f"U{k - 1}{t}")
                                wait_moved(f"V{k - 1}{t}")
                        elif w == "U" or k == LEVELS - 1:
                            wait_moved(f"T{k}{t}")
                        o = out_of(f"{w}{k}{t}")
                        for h in range(HD):
                            a, xx, n = AA[:, HD * t + h, 1, :], XX[:, HD * t + h, :, :], TT[:, t, h, :]
                            left, right = {"T": (a, xx[:, 0, :]), "U": (xx[:, 1, :], n), "V": (n, xx[:, 1, :])}[w]
                            last = pe.matmul(o[:, P * h:P * h + P], left, right, start=True, stop=True)
                        done(last, f"{w}{k}{t}")

                def scan_step(what):
                    AA, qkp, qkT = AA_of[1 - s], qkp_of[1 - s], qkT_of[1 - s]
                    if what[0] == "S":
                        c = int(what[1])
                        t, r = (c - 1) // 2, slice(CH * ((c - 1) % 2), CH * ((c - 1) % 2) + CH)
                        pe.wait_ge(U_ready, 4 * scan + c)
                        o = out_of(what)
                        done(pe.matmul(o[:, 0:P], qkp[r, t, 0, :, :].rearrange("p h d -> p (h d)"), U[r, t, :],
                                       start=(c == 1), stop=(c == 2 * NT - 1), skip_group_check=True), what)
                    elif what[0:2] == "ws":
                        c = int(what[2])
                        wait_moved(f"S{c}")
                        o, r = out_of(what), slice(CH * (c % 2), CH * (c % 2) + CH)
                        done(pe.matmul(o[r, 0:P], WT[:, CH * c:CH * c + CH], St[:, c, :], start=True, stop=True), what)
                    elif what == "out":
                        pe.wait_ge(U_ready, 4 * scan + 4)
                        for t in range(NT):
                            o = out_of(f"o{t}")
                            for half in range(2):
                                pe.matmul(o[CH * half:CH * half + CH, 0:P], qkT[:, t, 2, CH * half:CH * half + CH], St[:, 2 * t + half, :],
                                          start=True, stop=False, skip_group_check=True)
                            for h in range(HD):
                                last = pe.matmul(o[:, DV * h:DV * h + DV], AA[:, HD * t + h, 2, :], U[:, t, DV * h:DV * h + DV],
                                                 start=False, stop=True, skip_group_check=True)
                            done(last, f"o{t}")
                    elif what == "turn":
                        pe.wait_ge(y_ready, scan + 1)
                        o = out_of("yT")
                        for t in range(NT):
                            last = pe.transpose(o[:, P * t:P * t + P], y[:, t, :], ident[:, :])
                        done(last, "yT")
                    elif what == "residual":
                        wait_moved("yT")
                        o = out_of("fin")
                        for t in range(NT):
                            last = pe.matmul(o[:, C * t:C * t + C], yT_d[:, P * t:P * t + P], dWo_sb[:, :], start=True, stop=True)
                        done(last, "fin")

                def front_step(what):
                    qkp, qkT = qkp_of[1 - s], qkT_of[1 - s]
                    if what == "xT":
                        pe.wait_ge(xn_ready, 2 * front + (2 * B + 2))
                        o = out_of("xT")
                        for t in range(NT):
                            last = pe.transpose(o[:, P * t:P * t + P], xn[:, t, :], ident[:, :])
                        done(last, "xT")
                    elif what == "proj":
                        pe.wait_ge(hT_ready, front + 1)
                        for t in range(NT):
                            o = out_of(f"proj{t}")
                            done(pe.matmul(o[:, 0:NPR], hT[:, P * t:P * t + P], dW[:, :], start=True, stop=True), f"proj{t}")
                    elif what == "tq":
                        pe.wait_ge(qkp_ready, front + 1)
                        for t in range(NT):
                            o = out_of(f"tq{t}")
                            for w in range(3):
                                last = pe.transpose(o[:, P * w:P * w + P], qkp[:, t, w, :, :].rearrange("p h d -> p (h d)"), ident[:, :])
                            done(last, f"tq{t}")
                    elif what.startswith("gram"):
                        t, h = int(what[4]), int(what[5])
                        if h == 0:
                            wait_moved(f"tq{t}")
                        o, r = out_of(what), slice(DP * h, DP * h + DP)
                        pe.matmul(o[:, 0:P], qkT[r, t, 1, :], qkT[r, t, 0, :], start=True, stop=True)
                        done(pe.matmul(o[:, P:3 * P], qkT[r, t, 0, :], qkT[r, t, 1:3, :].rearrange("p w t -> p (w t)"),
                                       start=True, stop=True), what)

                for stage, what in DELTA_ORDER:
                    if stage == "inverse" and inverse is not None:
                        inverse_step(what)
                    elif stage == "scan" and scan is not None:
                        scan_step(what)
                    elif stage == "front" and front is not None:
                        front_step(what)
                if inverse is not None:
                    wait_moved("WT")

            ffn_loop(pe, 0, ffn_turn(0))
            if PHASES > 1:
                delta_loop(pe, delta_turn)
            if PHASES > 2:
                ffn_loop(pe, 1, ffn_turn(1))


_INS = ["L0_attn_hidden_states", "L0_attn_conv_w", "L0_attn_Wq", "L0_attn_Wk", "L0_attn_Wv", "L0_attn_Wb", "L0_attn_Wg",
        "L0_attn_norm_w", "L0_attn_Wo", "L0_ffn_Wq", "L0_ffn_Wk", "L0_ffn_Wv", "L0_ffn_Ws", "L0_ffn_Wd", "L0_ffn_Wo"]


def kernel(**inputs):
    import numpy as np
    import concourse.bacc as bacc
    from concourse.bass_utils import run_bass_kernel_spmd as run

    nc = bacc.Bacc("TRN2", target_bir_lowering=False, num_devices=1)
    arrays, args = {}, []
    for name in _INS:
        a = np.ascontiguousarray(inputs[name])
        arrays[name] = a
        args.append(nc.dram_tensor(name, a.shape, mybir.dt.from_np(a.dtype), kind="ExternalInput").ap())
    args.append(nc.dram_tensor("out", (B, L, C), F32, kind="ExternalOutput").ap())
    build(nc, *args)
    r = run(nc, [arrays], core_ids=[0])
    return r.results[0]["out"]
```

```python
import concourse.bass as bass
from concourse import mybir
from contextlib import ExitStack

F32 = mybir.dt.float32
F32R = mybir.dt.float32r
ALU = mybir.AluOpType
ACT = mybir.ActivationFunctionType
X = mybir.AxisListType.X

B, L, C = 8, 256, 128
P = 128
NT = L // P
H, DH, E = 16, 64, 8
NQ, NL = 4, 32
DV1 = DH + 1
NPAIR = H * DH // P
HD, DK, DV, CH = 4, 16, 32, 64
DP = 32
LEVELS = 6
NEG_BIG = -3.0e38
CONSTS, POOL_STEPS, MASKS, DVE_FFN, DVE_DELTA = 13, 6, 5, 21, 54
EPS = 1e-5

SETUP_JOBS = [("Wg", 1), ("Wv", 0), ("Wqk0", 4), ("Wqk2", 5), ("Wqk1", 4), ("Wqk3", 5), ("Wo0", 4), ("Wo1", 5)]
BETWEEN = {0: ["v", "weights", "keep"], 1: ["xT", "aT"], 2: ["low", "gate", "pv0"], 3: [("qk", 0), "omix2"],
           4: [("qk", 2), "omix3"], 5: [("shift", 1), ("qk", 4)], 6: [("shift", 3), ("qk", 6)], 7: [("shift", 5), ("qk", 7), "vmix0"], 8: [("shift", 7)]}
AFTER = {2: [("top", 0), "omix0", "pv1", "omix1", ("top", 1), "sigmoids"], 3: [("top", 2), ("qk", 1)],
         4: [("shift", 0), ("top", 3), "mix", "res", ("qk", 3)],
         5: [("shift", 2), "pvT", ("qk", 5)], 6: [("shift", 4)],
         7: [("shift", 6), "vmix1", "stats"], 8: ["vmix2", "mT", "vmix3", "normalize"]}
STAGE_OF = {"weights": "output", "aT": "output", "res": "output", "keep": "attend", "v": "attend", "stats": "norm", "normalize": "norm"}
STAGE_OF.update({f"omix{j}": "output" for j in range(4)})
FFN_ORDER = []
for k in range(9):
    if k < 8:
        FFN_ORDER.append(("attend", ("scores", k)))
    FFN_ORDER += [(STAGE_OF.get(what, "front"), what) for what in BETWEEN.get(k, ())]
    if k:
        FFN_ORDER.append(("attend", ("values", k - 1)))
    FFN_ORDER += [(STAGE_OF.get(what, "front"), what) for what in AFTER.get(k, ())]
FFN_BANKS, side = {}, 0
for stage, what in FFN_ORDER:
    name, c = what if isinstance(what, tuple) else (what, None)
    if what == "mT":
        FFN_BANKS[what] = [("mT", 2)]
    elif what in ("xT", "gate", "pv0", "pv1", "res") or name == "qk" or name[1:4] == "mix":
        FFN_BANKS[what] = [(f"qk{c}" if name == "qk" else what, side)]
        side = 1 - side
    elif name == "shift":
        FFN_BANKS[what] = [(f"S{h}", 2 + h % 2) for h in (2 * c, 2 * c + 1)]
    elif name == "scores":
        FFN_BANKS[what] = [(f"ST{h}", 4 + h % 2) for h in (2 * c, 2 * c + 1)]
    elif name == "values":
        FFN_BANKS[what] = [(f"at{c}", 6 + c % 2)]


def ffn_jobs(stages):
    return [job for stage, what in FFN_ORDER if stage in stages for job in FFN_BANKS.get(what, ())]


INVERSE = [(w, k, t) for k in range(1, LEVELS)
           for w, t in ([("T", 0), ("T", 1), ("U", 0), ("V", 0), ("U", 1), ("V", 1)] if k < LEVELS - 1 else
                        [("T", 0), ("T", 1), ("V", 0), ("V", 1)])]
SCAN_AT = {1: ["S1"], 2: ["ws1"], 3: ["S2"], 4: ["ws2"], 6: ["S3"], 7: ["ws3"], 8: ["out"],
           9: ["square"], 13: ["gate"], 15: ["turn"], 17: ["residual"]}
FRONT_AT = {1: ["stats"], 3: ["normalize"], 4: ["xT"], 5: ["conv3", "conv2"], 7: ["conv1", "conv0"],
            8: ["silu"], 10: ["proj"], 11: ["norms"], 13: ["sigmoids0"], 14: ["sigmoids1"], 15: ["keys"], 17: ["tq", "gates"],
            19: ["gram00", "gram01"], 20: ["gram02", "gram03"], 21: ["X0_0"], 24: ["gram10", "gram11"],
            25: ["gram12"], 27: ["gram13", "X0_1"]}
DELTA_ORDER = [("scan", "start")]
for g, group in enumerate(INVERSE):
    DELTA_ORDER += [("inverse", group)] + [("scan", w) for w in SCAN_AT.get(g, ())] + [("front", w) for w in FRONT_AT.get(g, ())]
DELTA_ORDER += [("inverse", "WT"), ("inverse", "Uv")]
DELTA_BANKS = {"S1": [("S1", 4)], "ws1": [("ws1", 5)], "S2": [("S2", 4)], "ws2": [("ws2", 5)], "S3": [("S3", 4)],
               "ws3": [("ws3", 5)], "out": [("o0", 5), ("o1", 4)], "turn": [("yT", 5)], "residual": [("fin", 4)],
               "WT": [("WT", 5)], "Uv": [("Uv", 4)], "xT": [("xT", 6)], "proj": [("proj0", 7), ("proj1", 6)],
               "tq": [("tq0", 7), ("tq1", 6)]}
DELTA_BANKS.update({f"gram{t}{h}": [(f"gram{t}{h}", 7 - h % 2)] for t in range(NT) for h in range(HD)})
DELTA_BANKS.update({(w, k, t): [(f"{w}{k}{t}", {"T": t, "U": 2, "V": 3}[w])] for w, k, t in INVERSE})
DELTA_BANKS["V", LEVELS - 1, 1] = [(f"V{LEVELS - 1}1", 2)]


def delta_jobs(stages, tag):
    return [(name + tag, b) for stage, step in DELTA_ORDER if stage in stages for name, b in DELTA_BANKS.get(step, ())]


def parts(order, marks):
    steps, taken, out = [what for _, what in order], set(), []
    for mark, extra in marks:
        part = set(steps[:steps.index(mark) + 1]) - taken
        taken |= part
        out.append((part, set(extra)))
    return out + [(set(steps) - taken, set())]


FIRST_INPUTS = {"xT", "low", "gate", "pv0", "pv1", ("top", 0), ("top", 1)}

CONVOLUTION = {"stats", "normalize", "xT", "conv3", "conv2", "conv1", "conv0", "silu"}
LAST_ATTENTION = parts(FFN_ORDER, [(("scores", 3), ["stats"]), (("scores", 4), ["normalize"]), (("values", 3), ["xT"]),
                                   (("scores", 5), ["conv3"]), (("values", 4), ["conv2"]), (("scores", 6), ["conv1", "conv0"]),
                                   (("scores", 7), ["silu"])])
CONVOLVED = [what for stage, what in DELTA_ORDER if stage == "front" and what not in CONVOLUTION]
KEYS = CONVOLVED.index("keys")
LAST_MIX = parts(FFN_ORDER, [("omix0", ["proj", "norms"]), ("omix1", ["sigmoids0"]), ("omix2", ["sigmoids1"]), ("omix3", CONVOLVED[KEYS:])])
LAST_INVERSE = parts(DELTA_ORDER, [(INVERSE[0], ["stats"]), (INVERSE[1], ["normalize"]), (INVERSE[3], ["xT"]), (INVERSE[4], ["low", "gate"]),
                                   (INVERSE[7], ["pv0"]), (INVERSE[8], [("top", 0)]), (INVERSE[10], ["pv1", ("top", 1)]),
                                   (INVERSE[13], ["sigmoids"]), (INVERSE[14], [("top", 2)]), (INVERSE[16], [("top", 3)]),
                                   (INVERSE[19], ["mix"]), (INVERSE[21], ["pvT"])])
EARLY = set().union(*(extra for _, extra in LAST_INVERSE)) - {"stats", "normalize"}
EARLY_BANKS = [("xT", 6), ("gate", 7), ("pv0", 6), ("pv1", 7)]
LAST_SCAN = parts(DELTA_ORDER, [("S1", [("qk", 0)]), ("S2", [("qk", 1), ("shift", 0)]), ("S3", [("qk", 2), ("shift", 1)]),
                               ("ws3", [("qk", 3)]), ("out", [("shift", 2)]), ("square", [("shift", 3)]), ("gate", [("qk", 4)])])
FRONT_REST = {what for _, what in FFN_ORDER} - EARLY - set().union(*(extra for _, extra in LAST_SCAN))


class Chain:

    def __init__(self, eng, sem):
        self.eng, self.sem, self.base, self.i, self.per, self.n = eng, sem, 0, 0, 0, 0

    def loop(self, i, per):
        self.base, self.i, self.per, self.n = self.base + self.n, i, per, 0

    def end(self, times):
        assert self.n == self.per, self.n
        self.base, self.i, self.per, self.n = self.base + times * self.per, 0, 0, 0

    def link(self, ins):
        self.n += 1
        ins.then_inc(self.sem, 1)
        self.eng.wait_ge(self.sem, self.i * self.per + (self.base + self.n))


class Jobs:

    def __init__(self, jobs, base, times):
        self.base, self.per, self.at = dict(base), {b: 0 for b in range(8)}, {}
        for name, bank in jobs:
            self.at[name] = (bank, self.per[bank])
            self.per[bank] += 1
        self.end = {b: base[b] + times * self.per[b] for b in range(8)}

    def bank(self, name):
        return self.at[name][0]

    def before(self, name, i):
        bank, k = self.at[name]
        return i * self.per[bank] + (self.base[bank] + k)

    def done(self, name, i):
        bank, k = self.at[name]
        return i * self.per[bank] + (self.base[bank] + k + 1)


def build(nc, hid, conv_w, dWq, dWk, dWv, dWb, dWg, norm_w, dWo, fWq, fWk, fWv, fWs, fWd, fWo, out):
    with ExitStack() as ctx:
        def sb(name, shape, dt=F32):
            return ctx.enter_context(nc.sbuf_tensor(name, shape, dt))

        def sem(name):
            return ctx.enter_context(nc.semaphore(name))

        ident = sb("ident", [P, P])
        own16 = sb("own16", [P, 8])
        neg_half16 = sb("neg_half16", [P, NT * 2 * HD])
        tie = sb("tie", [P, E])
        self_f = sb("self_f", [P, H, P])
        sel = sb("sel", [P, H, P], F32R)
        WTh = sb("WTh", [P, 16, P], F32R)
        WTl = sb("WTl", [P, 16, P], F32R)
        WvT = sb("WvT", [P, 4 * P])
        WgT = sb("WgT", [P, 2 * P])
        WoT = sb("WoT", [DH, E, P])
        x = sb("x", [P, B * NT, C])
        bdv = sb("bdv", [P, NL, 8, H])
        staged = bdv[:, :, :, :].rearrange("p l m h -> p (l m h)")
        wst = staged[:, 0:22 * C].rearrange("p (n c) -> p n c", c=C)
        wost = staged[:, 22 * C:22 * C + E * DH].rearrange("p (e d) -> p e d", d=DH)
        stat = sb("stat", [P, NT, 6])
        mv = sb("mv", [P, NT, 4])
        mean = sb("mean", [P, NT])
        vare = sb("vare", [P, NT])
        rstd = sb("rstd", [P, NT])
        xn = sb("xn", [P, NT, C])
        xT = sb("xT", [P, L])
        xTh = sb("xTh", [P, L], F32R)
        xTl = sb("xTl", [P, L], F32R)
        gate = sb("gate", [P, 64, E])
        egate = sb("egate", [P, NT, H, E])
        gdif = sb("gdif", [P, 64, E])
        gsel = sb("gsel", [P, 64, E])
        gsel2 = sb("gsel2", [P, 64, E])
        gmax = sb("gmax", [P, 64])
        grank = sb("grank", [P, 64])
        mask = sb("mask", [P, NT, 2, H, E])
        masko = sb("masko", [P, NT, H, E])
        sig = sb("sig", [P, NT, H, E])
        mix = sb("mix", [P, H, NT, E, 2])
        mixT = sb("mixT", [P, H, NL])
        pv = sb("pv", [P, NT, E, 2, DH])
        pvT = sb("pvT", [P, NL, DH])
        vm = sb("vm", [P, NL, DH])
        v = sb("v", [P, NT * H, DV1])
        negm = sb("negm", [P, NT, H])
        nmT = sb("nmT", [P, L], F32R)
        PT = sb("PT", [P, 4, NT, L])
        attn = sb("attn", [P, NT, H, DV1])
        rden = sb("rden", [P, NT * H])
        maskw = sb("maskw", [P, E, NT * H])
        maskT = sb("maskT", [P, E, NL])
        bdo = sb("bdo", [P, NL, 8, E])
        aT = sb("aT", [P, NL, DH])
        yT = sb("yT", [DH, NT, E, NQ, NL])

        convw = sb("convw", [P, 4])
        normw = sb("normw", [P, DV])
        dW = sb("dW", [P, 2 * HD * DK + 2 * HD * DV + HD])
        dWo_sb = sb("dWo_sb", [P, C])

        with nc.sbuf_tensor("qkh", [P, NPAIR, 2, L], F32R) as qkh, nc.sbuf_tensor("qkl", [P, NPAIR, 2, L], F32R) as qkl:
            pass
        odd_h = sb("odd_h", [P, NPAIR * 2 * L])
        odd_l = sb("odd_l", [P, NPAIR * 2 * L])

        def over(tensor, at, *shape):
            n = 1
            for m in shape:
                n *= m
            names = "abcd"[:len(shape)]
            return tensor[:, at:at + n].rearrange(f"p ({' '.join(names)}) -> p {' '.join(names)}", **dict(zip(names, shape)))

        f_bdv = bdv[:, :, :, :].rearrange("p l m h -> p (l m h)")
        f_aT = aT[:, :, :].rearrange("p l d -> p (l d)")
        f_bdo = bdo[:, :, :, :].rearrange("p l m e -> p (l m e)")
        f_PT = PT[:, :, :, :].rearrange("p a n t -> p (a n t)")
        f_attn = attn[:, :, :, :].rearrange("p n h d -> p (n h d)")
        f_vm = vm[:, :, :].rearrange("p l d -> p (l d)")
        f_self = self_f[:, :, :].rearrange("p h m -> p (h m)")
        AA_of = [over(f_bdv, 0, NT * HD, 2, P), over(odd_h, 2048, NT * HD, 2, P)]
        XX_of = [over(f_aT, 0, NT * HD, 2, P), over(odd_l, 0, NT * HD, 2, P)]
        qkp_of = [over(f_PT, 0, NT, 3, HD, DP), over(odd_l, 2048, NT, 3, HD, DP)]
        qkT_of = [over(f_PT, 768, NT, 3, P), over(odd_l, 2816, NT, 3, P)]
        vb_of = [over(f_attn, 1824, NT, P), over(odd_h, 0, NT, P)]
        gn_of = [over(f_vm, 1548, NT, P), over(odd_l, 3840, NT, P)]
        TT = over(f_bdo, 0, NT, HD, P)
        WT = over(f_bdo, 1024, L)
        Uv = over(f_bdo, 1280, NT, P)
        U = over(f_bdo, 1536, NT, P)
        St = over(f_PT, 1536, 4, P)
        NPR = 2 * HD * DK + 2 * HD * DV + HD
        pr = over(f_attn, 0, NT, NPR)
        o_sb = over(f_attn, 800, NT, P)
        osq = over(f_attn, 1056, NT, P)
        y = over(f_attn, 1312, NT, P)
        yT_d = over(f_attn, 1568, L)
        xpad = over(f_vm, 0, L + 3)
        hacc = over(f_vm, 260, L)
        hexp = over(f_vm, 516, L)
        hT = over(f_vm, 772, L)
        sqs = over(f_vm, 1028, NT, 2 * HD * DK)
        sg = over(f_vm, 1284, NT, HD * DV + HD)
        ss = over(f_vm, 1804, NT, 2 * HD)
        rn = over(f_vm, 1820, NT, 2 * HD)
        ms = over(f_vm, 1836, NT, HD)
        rr = over(f_vm, 1844, NT, HD)
        msc = over(f_vm, 1852, NT, HD)
        m3 = over(f_self, 0, 2, P)
        m0 = over(f_self, 384, P)
        mlev = over(f_self, 640, LEVELS - 1, P)
        mhead = over(f_self, 1280, P)

        bank = [ctx.enter_context(nc.psum_tensor(f"bank{b}", [P, 512], F32)) for b in range(8)]
        full = [sem(f"full{b}") for b in range(8)]
        free = [sem(f"free{b}") for b in range(8)]

        first_in = sem("first_in")
        hid_in = sem("hid_in")
        Wg_in = sem("Wg_in")
        Wv_in = sem("Wv_in")
        Wqk_in = sem("Wqk_in")
        Wo_in = sem("Wo_in")
        ident_ready = sem("ident_ready")
        const_done = sem("const_done")
        wT_hi = sem("wT_hi")
        dve_step = sem("dve_step")
        pool_step = sem("pool_step")
        var_ready = sem("var_ready")
        rstd_ready = sem("rstd_ready")
        xn_ready = sem("xn_ready")
        xlo_ready = sem("xlo_ready")
        egate_ready = sem("egate_ready")
        mixT_ready = sem("mixT_ready")
        bdv_ready = sem("bdv_ready")
        pvT_ready = sem("pvT_ready")
        qkhi_ready = sem("qkhi_ready")
        v_ready = sem("v_ready")
        maskT_ready = sem("maskT_ready")
        bdo_ready = sem("bdo_ready")
        aT_ready = sem("aT_ready")
        masks_done = sem("masks_done")
        dw_in = sem("dw_in")
        sel_ready = sem("sel_ready")
        conv_ready = sem("conv_ready")
        hexp_ready = sem("hexp_ready")
        hT_ready = sem("hT_ready")
        ss_ready = sem("ss_ready")
        rn_ready = sem("rn_ready")
        gexp_ready = sem("gexp_ready")
        qkp_ready = sem("qkp_ready")
        X0_ready = sem("X0_ready")
        U_ready = sem("U_ready")
        ms_ready = sem("ms_ready")
        rr_ready = sem("rr_ready")
        y_ready = sem("y_ready")
        stored = sem("stored")

        base = {b: 0 for b in range(8)}
        setup = Jobs(SETUP_JOBS, base, 1)

        def ffn_phase(base, early=()):
            phase = [Jobs([job for job in ffn_jobs(("front",)) if job[0] not in early], base, 1)]
            for stages, times in ((("attend", "front"), 1), (("attend", "front", "output"), B - 2), (("attend", "output"), 1), (("output",), 1)):
                phase.append(Jobs(ffn_jobs(stages), phase[-1].end, times))
            return phase

        ffn = [ffn_phase(setup.end)]
        delta = [Jobs([("xT", 2)] + [job for job in delta_jobs(("front",), "") if job[0] != "xT"], ffn[0][-1].end, 1)]
        delta.append(Jobs(delta_jobs(("inverse", "front"), ""), delta[-1].end, 1))
        delta.append(Jobs(delta_jobs(("inverse", "scan", "front"), "a") + delta_jobs(("inverse", "scan", "front"), "b"),
                          delta[-1].end, B // 2 - 1))
        delta.append(Jobs(delta_jobs(("inverse", "scan"), "") + EARLY_BANKS, delta[-1].end, 1))
        delta.append(Jobs(delta_jobs(("scan",), ""), delta[-1].end, 1))
        ffn.append(ffn_phase(delta[-1].end, [name for name, _ in EARLY_BANKS]))

        def layer(eng, ffn_turns, delta_turn, chain=None, setup_first=None, setup_rest=None, before_delta=None, before_keys=None):

            def ffn_until_last(phase, turn):
                jobs = ffn[phase]
                turn(jobs[1], 0, 2, 1, 0, None)
                with eng.Fori(0, B - 3) as i:
                    if chain:
                        chain.loop(i, DVE_FFN)
                    turn(jobs[2], i, i + 3, i + 2, i + 1, i)
                if chain:
                    chain.end(B - 3)
                turn(jobs[2], B - 3, None, B - 1, B - 2, B - 3)

            turn = ffn_turns[0]
            turn(ffn[0][0], 0, 0, None, None, None)
            if setup_first:
                setup_first()
            turn(ffn[0][0], 0, None, 0, None, None, FIRST_INPUTS)
            if setup_rest:
                setup_rest()
            turn(ffn[0][0], 0, 1, 0, None, None, {what for _, what in FFN_ORDER} - FIRST_INPUTS)
            ffn_until_last(0, turn)
            if before_delta:
                before_delta()
            for ffn_part, front_part in LAST_ATTENTION:
                turn(ffn[0][3], 0, None, None, B - 1, B - 2, ffn_part)
                delta_turn(delta[0], 0, "", None, None, 0, 1, front_part)
            for ffn_part, front_part in LAST_MIX:
                turn(ffn[0][4], 0, None, None, None, B - 1, ffn_part)
                if before_keys and "keys" in front_part:
                    before_keys()
                delta_turn(delta[0], 0, "", None, None, 0, 1, front_part)
            delta_turn(delta[1], 0, "", 0, None, 1, 0)
            with eng.Fori(0, B // 2 - 1) as i:
                if chain:
                    chain.loop(i, DVE_DELTA)
                delta_turn(delta[2], i, "a", 2 * i + 1, 2 * i, 2 * i + 2, 1)
                delta_turn(delta[2], i, "b", 2 * i + 2, 2 * i + 1, 2 * i + 3, 0)
            if chain:
                chain.end(B // 2 - 1)
            turn = ffn_turns[1]
            for inverse_part, front_part in LAST_INVERSE:
                delta_turn(delta[3], 0, "", B - 1, B - 2, None, 1, inverse_part)
                turn(delta[3], 0, 0, 0, None, None, front_part)
            for scan_part, front_part in LAST_SCAN:
                delta_turn(delta[4], 0, "", None, B - 1, None, 0, scan_part)
                turn(ffn[1][0], 0, None, 0, None, None, front_part)
            turn(ffn[1][0], 0, 1, 0, None, None, FRONT_REST)
            ffn_until_last(1, turn)
            turn(ffn[1][3], 0, None, None, B - 1, B - 2)
            turn(ffn[1][4], 0, None, None, None, B - 1)

        CREDIT = {b: 0 if b < 2 else 1 for b in range(8)}

        def turn(eng, jobs, name, i):
            b = jobs.bank(name)
            n = jobs.before(name, i) + CREDIT[b]
            if isinstance(n, int) and n == 0:
                return
            eng.wait_ge(free[b], n)

        def filled(eng, jobs, name, i):
            eng.wait_ge(full[jobs.bank(name)], jobs.done(name, i))

        def moved(eng, jobs, name, i):
            b = jobs.bank(name)
            eng.wait_ge(free[b], jobs.done(name, i) + CREDIT[b])

        def all_moved(eng, jobs, names, i, but=None):
            last = {}
            for name in sorted(names, key=lambda name: jobs.at[name][1]):
                last[jobs.bank(name)] = name
            for b, name in last.items():
                if b != but:
                    moved(eng, jobs, name, i)

        def heads(h):
            return slice(DH * (h % 2), DH * (h % 2) + DH)

        block = ctx.enter_context(nc.Block())

        @block.sync
        def _(sp):
            sp.dma_start(x[:, 0:NT, :], hid[0:1].rearrange("b (n p) c -> p (b n) c", p=P)).then_inc(first_in, 16)
            sp.dma_start(wst[:, 0:8, :], fWq.rearrange("h d c -> (h d) c").rearrange("(n p) c -> p n c", p=P)).then_inc(Wqk_in, 16)
            sp.dma_start(wst[:, 8:16, :], fWk.rearrange("h d c -> (h d) c").rearrange("(n p) c -> p n c", p=P)).then_inc(Wqk_in, 16)
            sp.dma_start(wost[:, :, :], fWo.rearrange("e f d -> f e d")).then_inc(Wo_in, 16)
            sp.dma_start(x[:, NT:B * NT, :], hid[1:B].rearrange("b (n p) c -> p (b n) c", p=P)).then_inc(hid_in, 16)
            sp.dma_start(convw[:, :], conv_w).then_inc(dw_in, 16)
            sp.dma_start(normw[:, :], norm_w.unsqueeze(0).to_broadcast([P, DV])).then_inc(dw_in, 16)
            at = 0
            for w in (dWq, dWk, dWv, dWg, dWb):
                sp.dma_start(dW[:, at:at + w.shape[1]], w).then_inc(dw_in, 16)
                at += w.shape[1]
            sp.dma_start(dWo_sb[:, :], dWo).then_inc(dw_in, 16)
            cut = (B - 1) * NT
            moved(sp, ffn[1][3], "res", 0)
            sp.dma_start(out[0:B - 1].rearrange("b (n p) c -> p (b n) c", p=P), x[:, 0:cut, :]).then_inc(stored, 16)
            moved(sp, ffn[1][4], "res", 0)
            sp.dma_start(out[B - 1:B].rearrange("b (n p) c -> p (b n) c", p=P), x[:, cut:cut + NT, :]).then_inc(stored, 16)
            sp.wait_ge(stored, 2 * 16)

        @block.gpsimd
        def _(pool):
            step = Chain(pool, pool_step)
            pool.memset(neg_half16[:, :], -0.5).then_inc(const_done, 1)
            step.link(pool.memset(ident[:, :], 0.0))
            pool.affine_select(out=ident[:, :], in_=ident[:, :], compare_op=ALU.not_equal, fill=1.0,
                               base=0, pattern=[[-1, P]], channel_multiplier=1).then_inc(ident_ready, 1)

            def constants():
                for e in range(E):
                    pool.memset(tie[:, e:e + 1], float(E - e)).then_inc(const_done, 1)
                pool.memset(pv[:, :, :, :, :], 0.0).then_inc(const_done, 1)
                pool.memset(mix[:, :, :, :, :], 0.0).then_inc(const_done, 1)
                pool.memset(v[:, :, DH:DV1], 1.0).then_inc(const_done, 1)
                pool.memset(nmT[:, :].bitcast(F32), 0.0).then_inc(const_done, 1)
                step.link(pool.memset(own16[:, :], 1.0))
                step.link(pool.affine_select(out=own16[:, :], in_=own16[:, :], compare_op=ALU.is_ge, fill=0.0,
                                             base=0, pattern=[[-16, 8]], channel_multiplier=1))
                step.link(pool.affine_select(out=own16[:, :], in_=own16[:, :], compare_op=ALU.is_ge, fill=0.0,
                                             base=15, pattern=[[16, 8]], channel_multiplier=-1))
                step.link(pool.memset(self_f[:, :, :], 0.0))
                step.link(pool.affine_select(out=self_f[:, :, :], in_=self_f[:, :, :], compare_op=ALU.not_equal,
                                             fill=1.0, base=0, pattern=[[-1, H], [0, P]], channel_multiplier=1))

            def masks():
                pool.wait_ge(sel_ready, 1)
                pool.wait_ge(ident_ready, 1)

                def keep(ap, base, pattern, channel, last=False):
                    ins = pool.affine_select(out=ap, in_=ap, compare_op=ALU.is_ge, fill=0.0, base=base, pattern=pattern,
                                             channel_multiplier=channel)
                    if last:
                        ins.then_inc(masks_done, 1)
                    else:
                        step.link(ins)

                step.link(pool.memset(m3[:, :, :], 1.0))
                step.link(pool.memset(m3[0:CH, :, CH:P], 0.0))
                keep(m3[:, 0, :], -1, [[1, P]], -1, True)
                keep(m3[:, 1, :], 0, [[1, P]], -1, True)
                step.link(pool.memset(mhead, 1.0))
                keep(mhead, 0, [[-DP, HD], [0, DV]], 1)
                keep(mhead, DP - 1, [[DP, HD], [0, DV]], -1, True)
                for k in range(1, LEVELS):
                    s, mask_k = 1 << k, mlev[:, k - 1, :]
                    halves = mask_k.rearrange("p (n two s) -> p n two s", two=2, s=s)
                    step.link(pool.memset(mask_k, 1.0))
                    step.link(pool.memset(halves[:, :, 1, :], 0.0))
                    keep(halves[:, :, 0, :], -s, [[-2 * s, P // (2 * s)], [0, s]], 1)
                    keep(halves[:, :, 0, :], 2 * s - 1, [[2 * s, P // (2 * s)], [0, s]], -1)
                step.link(pool.memset(m0, 0.0))
                odd = m0.rearrange("p (n two) -> p n two", two=2)[:, :, 1]
                step.link(pool.affine_select(out=odd, in_=odd, compare_op=ALU.not_equal, fill=1.0, base=0,
                                             pattern=[[-2, P // 2]], channel_multiplier=1))
                pool.tensor_tensor(m0, ident[:, :], m0, ALU.subtract).then_inc(masks_done, 1)
                pool.tensor_tensor(mlev, ident[:, :].unsqueeze(1).to_broadcast([P, LEVELS - 1, P]), mlev, ALU.subtract).then_inc(masks_done, 1)

            def delta_turn(jobs, i, tag, inverse, scan, front, s, part=None):
                AA, XX = AA_of[1 - s], XX_of[1 - s]
                for stage, what in DELTA_ORDER:
                    if part is not None and what not in part:
                        continue
                    if stage == "front" and front is not None:
                        if what == "stats":
                            pool.wait_ge(var_ready, front + (B + 1))
                            pool.tensor_tensor(rstd[:, :], vare[:, :], neg_half16[:, 0:NT], ALU.pow).then_inc(rstd_ready, 1)
                        elif what == "norms":
                            pool.wait_ge(ss_ready, front + 1)
                            pool.tensor_tensor(rn[:, :, :], ss[:, :, :], neg_half16[:, :].rearrange("p (n g) -> p n g", n=NT),
                                               ALU.pow).then_inc(rn_ready, 1)
                    if stage == "scan" and scan is not None and what == "square":
                        pool.wait_ge(ms_ready, scan + 1)
                        pool.tensor_tensor(rr[:, :, :], ms[:, :, :], neg_half16[:, 0:NT * HD].rearrange("p (n g) -> p n g", n=NT),
                                           ALU.pow).then_inc(rr_ready, 1)

            def ffn_turn(phase):
                def turn_of(jobs, i, norm, front, attend, output, part=None):
                    for stage, what in FFN_ORDER:
                        if part is not None and what not in part:
                            continue
                        if norm is not None and what == "stats":
                            pool.wait_ge(var_ready, norm + (2 * phase * B + 1))
                            pool.tensor_tensor(rstd[:, :], vare[:, :], neg_half16[:, 0:NT], ALU.pow).then_inc(rstd_ready, 1)
                        elif stage == "front" and front is not None:
                            if what == "mix":
                                pool.wait_ge(mixT_ready, front + (phase * B + 1))
                                for j in range(0, NL, 8):
                                    pool.tensor_tensor(bdv[:, j:j + 8, :, :],
                                                       mixT[:, :, j:j + 8].rearrange("p h l -> p l h").unsqueeze(2).to_broadcast([P, 8, 8, H]),
                                                       own16[:, :].unsqueeze(1).unsqueeze(3).to_broadcast([P, 8, 8, H]),
                                                       ALU.mult).then_inc(bdv_ready, 1)
                        elif output is not None and what == "weights":
                            pool.wait_ge(maskT_ready, output + (phase * B + 1))
                            for j in range(0, NL, 8):
                                pool.tensor_tensor(bdo[:, j:j + 8, :, :],
                                                   maskT[:, :, j:j + 8].rearrange("p e l -> p l e").unsqueeze(2).to_broadcast([P, 8, 8, E]),
                                                   own16[:, :].unsqueeze(1).unsqueeze(3).to_broadcast([P, 8, 8, E]),
                                                   ALU.mult).then_inc(bdo_ready, 1)
                return turn_of

            layer(pool, (ffn_turn(0), ffn_turn(1)), delta_turn, setup_first=constants, setup_rest=masks)

        @block.vector
        def _(dve):
            step = Chain(dve, dve_step)
            for b in range(2, 8):
                dve.sem_inc(free[b], 1)

            def setup_first():
                dve.wait_ge(const_done, CONSTS)
                dve.wait_ge(ident_ready, 1)

            def setup_rest():
                dve.wait_ge(pool_step, POOL_STEPS)
                dve.tensor_copy(sel[:, :, :], self_f[:, :, :]).then_inc(sel_ready, 1)
                for n, j in enumerate((0, 2, 1, 3)):
                    b = setup.bank(f"Wqk{j}")
                    dve.wait_ge(wT_hi, n + 1)
                    dve.tensor_tensor(WTl[:, 4 * j:4 * j + 4, :], bank[b][:, :].rearrange("p (n c) -> p n c", c=P),
                                      WTh[:, 4 * j:4 * j + 4, :].bitcast(F32), ALU.subtract).then_inc(free[b], 1)
                dve.wait_ge(hid_in, 16)

            def layer_stats(i):
                for t in range(NT):
                    last = dve.bn_stats(stat[:, t, :], x[:, bass.ds(i * NT + t, 1), :].rearrange("p a c -> p (a c)"))
                step.link(last)
                dve.tensor_tensor(mv[:, :, 0], stat[:, :, 1], stat[:, :, 4], ALU.add)
                dve.tensor_tensor(mv[:, :, 1], stat[:, :, 1], stat[:, :, 4], ALU.subtract)
                step.link(dve.tensor_tensor(mv[:, :, 2], stat[:, :, 2], stat[:, :, 5], ALU.add))
                dve.tensor_scalar(mean[:, :], mv[:, :, 0], 0.5, None, ALU.mult)
                dve.scalar_tensor_tensor(mv[:, :, 3], mv[:, :, 1], 0.25, mv[:, :, 1], ALU.mult, ALU.mult)
                step.link(dve.tensor_scalar(mv[:, :, 2], mv[:, :, 2], 1.0 / C, EPS, ALU.mult, ALU.add))
                dve.tensor_tensor(vare[:, :], mv[:, :, 2], mv[:, :, 3], ALU.add).then_inc(var_ready, 1)

            def normalize(i, ln):
                dve.wait_ge(rstd_ready, ln + 1)
                for t in range(NT):
                    dve.tensor_scalar(xn[:, t, :], x[:, bass.ds(i * NT + t, 1), :].rearrange("p a c -> p (a c)"),
                                      mean[:, t:t + 1], rstd[:, t:t + 1], ALU.subtract, ALU.mult).then_inc(xn_ready, 1)

            def delta_turn(jobs, i, tag, inverse, scan, front, s, part=None):
                qk_w, v_w = 2 * HD * DK, HD * DV

                def heads_over(ap, width):
                    return ap.unsqueeze(3).to_broadcast([P, NT, HD, width])

                def by_head(ap, width):
                    return ap.rearrange("p n (h d) -> p n h d", d=width)

                def front_step(what):
                    AA, qkp, vb, gn = AA_of[1 - s], qkp_of[1 - s], vb_of[1 - s], gn_of[1 - s]
                    beta = sg[:, :, v_w:v_w + HD]
                    if what == "stats":
                        layer_stats(front)
                    elif what == "normalize":
                        normalize(front, front + B)
                    elif what == "conv3":
                        if isinstance(front, int) and front == 0:
                            step.link(dve.memset(xpad[:, 0:3], 0.0))
                        moved(dve, jobs, f"xT{tag}", i)
                        step.link(dve.tensor_scalar(hacc[:, :], xpad[:, 3:3 + L], convw[:, 3:4], None, ALU.mult))
                    elif what in ("conv2", "conv1"):
                        k = int(what[4])
                        step.link(dve.scalar_tensor_tensor(hacc[:, :], xpad[:, k:k + L], convw[:, k:k + 1], hacc[:, :], ALU.mult, ALU.add))
                    elif what == "conv0":
                        dve.scalar_tensor_tensor(hacc[:, :], xpad[:, 0:L], convw[:, 0:1], hacc[:, :], ALU.mult, ALU.add).then_inc(conv_ready, 1)
                    elif what == "silu":
                        dve.wait_ge(hexp_ready, front + 1)
                        step.link(dve.tensor_scalar(hexp[:, :], hexp[:, :], 1.0, None, ALU.add))
                        step.link(dve.reciprocal(hexp[:, :], hexp[:, :]))
                        dve.tensor_tensor(hT[:, :], hacc[:, :], hexp[:, :], ALU.mult).then_inc(hT_ready, 1)
                    elif what == "norms":
                        moved(dve, jobs, f"proj0{tag}", i)
                        moved(dve, jobs, f"proj1{tag}", i)
                        step.link(dve.tensor_tensor(sqs[:, :, :], pr[:, :, 0:qk_w], pr[:, :, 0:qk_w], ALU.mult))
                        step.link(dve.tensor_reduce(ss[:, :, :], sqs[:, :, :].rearrange("p n (g d) -> p n g d", d=DK), X, ALU.add))
                        dve.tensor_scalar(ss[:, :, :], ss[:, :, :], 1e-24, None, ALU.max).then_inc(ss_ready, 1)
                    elif what == "sigmoids0":
                        dve.wait_ge(gexp_ready, front + 1)
                        step.link(dve.tensor_scalar(sg[:, :, :], sg[:, :, :], 1.0, None, ALU.add))
                        dve.reciprocal(sg[:, 0, :], sg[:, 0, :])
                    elif what == "sigmoids1":
                        step.link(dve.reciprocal(sg[:, 1, :], sg[:, 1, :]))
                    elif what == "keys":
                        dve.wait_ge(rn_ready, front + 1)
                        for w, at, g in ((2, 0, 0), (0, HD * DK, HD)):
                            step.link(dve.tensor_tensor(qkp[:, :, w, :, 0:DK], by_head(pr[:, :, at:at + HD * DK], DK),
                                                        heads_over(rn[:, :, g:g + HD], DK), ALU.mult))
                        dve.tensor_tensor(qkp[:, :, 1, :, 0:DK], qkp[:, :, 0, :, 0:DK], heads_over(beta, DK), ALU.mult).then_inc(qkp_ready, 1)
                    elif what == "gates":
                        dve.tensor_tensor(by_head(vb[:, :, :], DV), by_head(pr[:, :, qk_w:qk_w + v_w], DV), heads_over(beta, DV), ALU.mult)
                        step.link(dve.tensor_tensor(gn[:, :, :], pr[:, :, qk_w + v_w:qk_w + 2 * v_w], sg[:, :, 0:v_w], ALU.mult))
                        step.link(dve.tensor_tensor(by_head(gn[:, :, :], DV), by_head(gn[:, :, :], DV),
                                                    normw[:, :].unsqueeze(1).unsqueeze(1).to_broadcast([P, NT, HD, DV]), ALU.mult))
                    elif what.startswith("gram"):
                        b, g = jobs.bank(what + tag), HD * int(what[4]) + int(what[5])
                        filled(dve, jobs, what + tag, i)
                        dve.tensor_tensor(AA[:, g, :, :], bank[b][:, 0:2 * P].rearrange("p (w t) -> p w t", w=2),
                                          m3[:, :, :], ALU.mult).then_inc(free[b], 1)

                    elif what.startswith("X0"):
                        t = int(what[3])
                        at, X0 = AA[:, HD * t:HD * t + HD, 0, :], XX_of[1 - s][:, HD * t:HD * t + HD, :, :]
                        for h in range(HD):
                            moved(dve, jobs, f"gram{t}{h}{tag}", i)
                        step.link(dve.tensor_tensor(at, at, ident[:, :].unsqueeze(1).to_broadcast([P, HD, P]), ALU.add))
                        step.link(dve.tensor_tensor(X0[:, :, 1, :], at, m0.unsqueeze(1).to_broadcast([P, HD, P]), ALU.mult))
                        dve.transpose(X0[:, :, 0, :], X0[:, :, 1, :]).then_inc(X0_ready, 1)

                def scan_step(what):
                    gn = gn_of[1 - s]
                    if what == "start":
                        step.link(dve.tensor_copy(U[0:CH, 0, :], Uv[0:CH, 0, :]))
                        dve.sem_inc(U_ready, 1)
                    elif what[0] == "S":
                        c, b = int(what[1]), jobs.bank(what + tag)
                        filled(dve, jobs, what + tag, i)
                        dve.tensor_tensor(St[:, c, :], bank[b][:, 0:P], mhead, ALU.mult).then_inc(free[b], 1)
                    elif what[0:2] == "ws":
                        c, b = int(what[2]), jobs.bank(what + tag)
                        t, r = c // 2, slice(CH * (c % 2), CH * (c % 2) + CH)
                        filled(dve, jobs, what + tag, i)
                        step.link(dve.tensor_tensor(U[r, t, :], Uv[r, t, :], bank[b][r, 0:P], ALU.subtract))
                        dve.sem_inc(U_ready, 1)
                        dve.sem_inc(free[b], 1)
                    elif what == "square":
                        moved(dve, jobs, f"o0{tag}", i)
                        moved(dve, jobs, f"o1{tag}", i)
                        step.link(dve.tensor_tensor(osq[:, :, :], o_sb[:, :, :], o_sb[:, :, :], ALU.mult))
                        step.link(dve.tensor_reduce(msc[:, :, :], by_head(osq[:, :, :], DV), X, ALU.add))
                        dve.tensor_scalar(ms[:, :, :], msc[:, :, :], 1.0 / DV, EPS, ALU.mult, ALU.add).then_inc(ms_ready, 1)
                        step.link(dve.tensor_tensor(y[:, :, :], o_sb[:, :, :], gn[:, :, :], ALU.mult))
                    elif what == "gate":
                        dve.wait_ge(rr_ready, scan + 1)
                        dve.tensor_tensor(by_head(y[:, :, :], DV), by_head(y[:, :, :], DV), heads_over(rr[:, :, :], DV), ALU.mult).then_inc(y_ready, 1)
                    elif what == "residual":
                        b = jobs.bank(f"fin{tag}")
                        filled(dve, jobs, f"fin{tag}", i)
                        xi = x[:, bass.ds(scan * NT, NT), :]
                        dve.tensor_tensor(xi, xi, bank[b][:, 0:NT * C].rearrange("p (n c) -> p n c", c=C), ALU.add).then_inc(free[b], 1)

                for stage, what in DELTA_ORDER:
                    if part is not None and what not in part:
                        continue
                    if stage == "inverse" and inverse is not None and what[0] == "T":
                        k, t = what[1:]
                        job = f"T{k}{t}{tag}"
                        filled(dve, jobs, job, i)
                        dve.tensor_tensor(TT[:, t, :, :], bank[jobs.bank(job)][:, :].rearrange("p (h t) -> p h t", h=HD),
                                          mlev[:, k - 1, :].unsqueeze(1).to_broadcast([P, HD, P]),
                                          ALU.mult).then_inc(free[jobs.bank(job)], 1)
                    elif stage == "scan" and scan is not None:
                        scan_step(what)
                    elif stage == "front" and front is not None:
                        front_step(what)
                if inverse is not None and (part is None or "Uv" in part):
                    moved(dve, jobs, f"Uv{tag}", i)

            def ffn_turn(phase):
                def turn_of(jobs, i, norm, front, attend, output, part=None):
                    n = None if front is None else front + phase * B

                    def groups(ap):
                        return ap.unsqueeze(2).to_broadcast([P, 64, E])

                    ties = tie[:, :].unsqueeze(1).to_broadcast([P, 64, E])

                    def top_two(part):
                        if part == 0:
                            moved(dve, jobs, "gate", i)
                            step.link(dve.tensor_reduce(gmax[:, :], gate[:, :, :], X, ALU.max))
                            step.link(dve.tensor_tensor(gdif[:, :, :], gate[:, :, :], groups(gmax[:, :]), ALU.subtract))
                            step.link(dve.scalar_tensor_tensor(gsel[:, :, :], gdif[:, :, :], 0.0, ties, ALU.is_ge, ALU.mult))
                        elif part == 1:
                            step.link(dve.tensor_reduce(grank[:, :], gsel[:, :, :], X, ALU.max))
                            step.link(dve.tensor_tensor(gsel2[:, :, :], gsel[:, :, :], groups(grank[:, :]), ALU.is_equal))
                            step.link(dve.scalar_tensor_tensor(gdif[:, :, :], gsel2[:, :, :], NEG_BIG, gdif[:, :, :], ALU.mult, ALU.add))
                        elif part == 2:
                            step.link(dve.tensor_reduce(gmax[:, :], gdif[:, :, :], X, ALU.max))
                            step.link(dve.tensor_tensor(gdif[:, :, :], gdif[:, :, :], groups(gmax[:, :]), ALU.subtract))
                            step.link(dve.scalar_tensor_tensor(gsel[:, :, :], gdif[:, :, :], 0.0, ties, ALU.is_ge, ALU.mult))
                        elif part == 3:
                            step.link(dve.tensor_reduce(grank[:, :], gsel[:, :, :], X, ALU.max))
                            step.link(dve.tensor_tensor(gsel[:, :, :], gsel[:, :, :], groups(grank[:, :]), ALU.is_equal))
                            step.link(dve.tensor_tensor(mask[:, :, :, :, :].rearrange("p n s h e -> p (n s h) e"),
                                                        gsel[:, :, :], gsel2[:, :, :], ALU.add))

                    def value_sigmoids():
                        dve.wait_ge(egate_ready, n + 1)
                        step.link(dve.tensor_scalar(sig[:, :, :, :], egate[:, :, :, :], 1.0, None, ALU.add))
                        step.link(dve.reciprocal(sig[:, :, :, :], sig[:, :, :, :]))

                    def value_mix():
                        step.link(dve.tensor_tensor(mix[:, :, :, :, 0].rearrange("p h n e -> p n h e"), mask[:, :, 0, :, :],
                                                    sig[:, :, :, :], ALU.mult))
                        dve.transpose(mixT[:, :, :], mix[:, :, :, :, :].rearrange("p h n e x -> p h (n e x)")).then_inc(mixT_ready, 1)

                    def values_turned():
                        all_moved(dve, jobs, ("pv0", "pv1"), i)
                        dve.transpose(pvT[:, :, :].rearrange("p l d -> p d l"),
                                      pv[:, :, :, :, :].rearrange("p n e x d -> p d (n e x)")).then_inc(pvT_ready, 1)

                    def low_part(c):
                        b = jobs.bank(f"qk{c}")
                        dve.wait_ge(qkhi_ready, NPAIR * n + (c + 1))
                        dve.tensor_tensor(qkl[:, c, :, :], bank[b][:, :].rearrange("p (a t) -> p a t", a=2),
                                          qkh[:, c, :, :].bitcast(F32), ALU.subtract).then_inc(free[b], 1)

                    def head_max(h):
                        b = jobs.bank(f"S{h}")
                        filled(dve, jobs, f"S{h}", i)
                        dve.tensor_reduce(negm[:, :, h], bank[b][:, :].rearrange("p (n j) -> p n j", n=NT),
                                          X, ALU.max, negate=True).then_inc(free[b], 1)

                    def front_step(what):
                        name, c = what if isinstance(what, tuple) else (what, None)
                        if what == "low":
                            moved(dve, jobs, "xT", i)
                            dve.tensor_tensor(xTl[:, :], xT[:, :], xTh[:, :].bitcast(F32), ALU.subtract).then_inc(xlo_ready, 1)
                        elif name == "top":
                            top_two(c)
                        elif what == "sigmoids":
                            value_sigmoids()
                        elif what == "mix":
                            value_mix()
                        elif what == "pvT":
                            values_turned()
                        elif name == "qk":
                            low_part(c)
                        elif name == "shift":
                            head_max(2 * c)
                            head_max(2 * c + 1)

                    def output_step(what):
                        if what == "weights":
                            step.link(dve.reciprocal(rden[:, :], attn[:, :, :, DH].rearrange("p n h -> p (n h)")))
                            step.link(dve.tensor_tensor(maskw[:, :, :].rearrange("p e (n h) -> p n h e", n=NT), masko[:, :, :, :],
                                                        rden[:, :].rearrange("p (n h) -> p n h", n=NT).unsqueeze(3).to_broadcast([P, NT, H, E]),
                                                        ALU.mult))
                            dve.transpose(maskT[:, :, :], maskw[:, :, :]).then_inc(maskT_ready, 1)
                        elif what == "aT":
                            dve.transpose(aT[:, :, :].rearrange("p l d -> p d l"),
                                          attn[:, :, :, 0:DH].rearrange("p n h d -> p d (n h)")).then_inc(aT_ready, 1)
                        elif what == "res":
                            xi = x[:, bass.ds(output * NT, NT), :]
                            filled(dve, jobs, "res", i)
                            dve.scalar_tensor_tensor(xi, bank[jobs.bank("res")][:, 0:NT * C].rearrange("p (n c) -> p n c", c=C),
                                                     0.5, xi, ALU.mult, ALU.add).then_inc(free[jobs.bank("res")], 1)

                    for stage, what in FFN_ORDER:
                        if part is not None and what not in part:
                            continue
                        if stage == "front" and front is not None:
                            front_step(what)
                        elif stage == "output" and output is not None:
                            output_step(what)
                        elif attend is not None and what == "keep":
                            step.link(dve.tensor_copy(masko[:, :, :, :], mask[:, :, 1, :, :]))
                        elif norm is not None and what == "stats":
                            layer_stats(norm)
                        elif norm is not None and what == "normalize":
                            normalize(norm, norm + 2 * phase * B)
                        elif attend is not None and what == "v":
                            dve.transpose(v[:, :, 0:DH].rearrange("p g d -> p d g"),
                                          vm[:, :, :].rearrange("p l d -> p d l")).then_inc(v_ready, 1)
                    if front is not None and (part is None or "vmix3" in part):
                        all_moved(dve, jobs, [f"vmix{j}" for j in range(4)], i)
                    if attend is not None and (part is None or ("values", 7) in part):
                        moved(dve, jobs, "at6", i)
                        moved(dve, jobs, "at7", i)
                return turn_of

            def past_zeros():
                dve.wait_ge(masks_done, MASKS)
                dve.wait_ge(dw_in, 8 * 16)

            def more_zeros():
                for qkp in qkp_of:
                    step.link(dve.memset(qkp[:, :, :, :, DK:DP], 0.0))
                step.link(dve.memset(St[:, 0, :], 0.0))

            dve.wait_ge(first_in, 16)
            layer(dve, (ffn_turn(0), ffn_turn(1)), delta_turn, step, setup_first, setup_rest, past_zeros, more_zeros)

        @block.scalar
        def _(act):
            act.dma_start(wst[:, 20, :], fWs.rearrange("h e c -> (h e) c")).then_inc(Wg_in, 16)
            act.dma_start(wst[:, 21, :], fWd.rearrange("h e c -> (h e) c")).then_inc(Wg_in, 16)
            act.dma_start(wst[:, 16:20, :], fWv.rearrange("h d c -> (h d) c").rearrange("(n p) c -> p n c", p=P)).then_inc(Wv_in, 16)
            def setup_first():
                filled(act, setup, "Wg", 0)
                act.activation(WgT[:, :], bank[1][:, 0:2 * P], ACT.Copy).then_inc(free[1], 1)
                filled(act, setup, "Wv", 0)
                act.activation(WvT[:, :], bank[0][:, :], ACT.Copy).then_inc(free[0], 1)

            def setup_rest():
                for j in (0, 2, 1, 3):
                    filled(act, setup, f"Wqk{j}", 0)
                    act.activation(WTh[:, 4 * j:4 * j + 4, :], bank[setup.bank(f"Wqk{j}")][:, :].rearrange("p (n c) -> p n c", c=P),
                                   ACT.Copy).then_inc(wT_hi, 1)
                for j in range(2):
                    b = setup.bank(f"Wo{j}")
                    filled(act, setup, f"Wo{j}", 0)
                    act.activation(WoT[:, 4 * j:4 * j + 4, :], bank[b][0:DH, :].rearrange("p (n c) -> p n c", c=P),
                                   ACT.Copy).then_inc(free[b], 1)

            def ffn_turn(phase):
                def turn_of(jobs, i, norm, front, attend, output, part=None):
                    def read(name):
                        filled(act, jobs, name, i)
                        return bank[jobs.bank(name)]

                    def freeing(name):
                        return free[jobs.bank(name)]

                    def probabilities(h):
                        o = read(f"ST{h}")
                        if h >= 4:
                            filled(act, jobs, f"at{h // 2 - 2}", i)
                        act.activation(PT[:, h % 4, :, :], o[:, :].rearrange("p (n t) -> p n t", n=NT),
                                       ACT.Exp, scale=DH ** -0.5).then_inc(freeing(f"ST{h}"), 1)

                    def attn_out(g):
                        act.activation(attn[:, :, 2 * g:2 * g + 2, :].rearrange("p n h d -> p h n d"),
                                       read(f"at{g}")[:, 0:4 * DV1].rearrange("p (h n d) -> p h n d", h=2, n=NT),
                                       ACT.Copy).then_inc(freeing(f"at{g}"), 1)

                    def high_part(c):
                        act.activation(qkh[:, c, :, :], read(f"qk{c}")[:, :].rearrange("p (a t) -> p a t", a=2),
                                       ACT.Copy).then_inc(qkhi_ready, 1)

                    def expert_values(t):
                        act.activation(pv[:, t, :, 0, :], read(f"pv{t}")[:, :].rearrange("p (e d) -> p e d", d=DH),
                                       ACT.Copy).then_inc(freeing(f"pv{t}"), 1)

                    def front_step(what):
                        name, c = what if isinstance(what, tuple) else (what, None)
                        if what == "xT":
                            act.activation(xT[:, :], read("xT")[:, 0:L], ACT.Copy)
                            act.activation(xTh[:, :], read("xT")[:, 0:L], ACT.Copy).then_inc(freeing("xT"), 1)
                        elif what == "gate":
                            act.activation(gate[:, :, :], read("gate")[:, :].rearrange("p (g e) -> p g e", e=E),
                                           ACT.Copy).then_inc(freeing("gate"), 1)
                            moved(act, jobs, "gate", i)
                            act.activation(egate[:, :, :, :], gate[:, :, :].rearrange("p (n s h) e -> p n s (h e)", n=NT, s=2)[:, :, 0, :],
                                           ACT.Exp, scale=-1.0).then_inc(egate_ready, 1)
                        elif what in ("pv0", "pv1"):
                            expert_values(int(what[2]))
                        elif name == "qk":
                            high_part(c)
                        elif name[0:4] == "vmix":
                            j = int(name[4])
                            act.activation(vm[:, 8 * j:8 * j + 8, :], read(name)[:, :].rearrange("p (l d) -> p l d", d=DH),
                                           ACT.Copy).then_inc(freeing(name), 1)
                        elif what == "mT":
                            act.activation(nmT[0:H, :], read("mT")[0:H, 0:L], ACT.Copy).then_inc(freeing("mT"), 1)

                    for stage, what in FFN_ORDER:
                        if part is not None and what not in part:
                            continue
                        name, c = what if isinstance(what, tuple) else (what, None)
                        if stage == "front" and front is not None:
                            front_step(what)
                        elif stage == "attend" and attend is not None:
                            if name == "scores":
                                probabilities(2 * c)
                                probabilities(2 * c + 1)
                            elif name == "values":
                                if c == 0 and output is not None:
                                    act.wait_ge(aT_ready, output + (phase * B + 1))
                                attn_out(c)
                        elif output is not None and name[0:4] == "omix":
                            j = int(name[4])
                            act.activation(yT[:, :, :, :, 8 * j:8 * j + 8].rearrange("p n e q l -> p q (n e) l"),
                                           read(name)[0:DH, :].rearrange("p (l q c) -> p q c l", q=NQ, c=NT * E),
                                           ACT.Copy).then_inc(freeing(name), 1)
                return turn_of

            def delta_turn(jobs, i, tag, inverse, scan, front, s, part=None):
                XX, qkT = XX_of[s], qkT_of[1 - s]

                def out_of(job):
                    filled(act, jobs, job + tag, i)
                    return bank[jobs.bank(job + tag)]

                def freeing(job):
                    return free[jobs.bank(job + tag)]

                for stage, what in DELTA_ORDER:
                    if part is not None and what not in part:
                        continue
                    if stage == "inverse" and inverse is not None:
                        if what[0] in ("U", "V") and what != "Uv":
                            (w, k, t), job = what, f"{what[0]}{what[1]}{what[2]}"
                            act.activation(XX[:, HD * t:HD * t + HD, 0 if w == "U" else 1, :],
                                           out_of(job)[:, :].rearrange("p (h t) -> p h t", h=HD), ACT.Copy).then_inc(freeing(job), 1)
                        elif what == "WT":
                            act.activation(WT[:, :], out_of("WT")[:, 0:L], ACT.Copy).then_inc(freeing("WT"), 1)
                        elif what == "Uv":
                            act.activation(Uv[:, :, :].rearrange("p n m -> p (n m)"), out_of("Uv")[:, 0:L], ACT.Copy).then_inc(freeing("Uv"), 1)
                    elif stage == "scan" and scan is not None:
                        if what == "out":
                            for t in range(NT):
                                act.activation(o_sb[:, t, :], out_of(f"o{t}")[:, 0:P], ACT.Copy).then_inc(freeing(f"o{t}"), 1)
                        elif what == "turn":
                            act.activation(yT_d[:, :], out_of("yT")[:, 0:L], ACT.Copy).then_inc(freeing("yT"), 1)
                    elif stage == "front" and front is not None:
                        if what == "xT":
                            act.activation(xpad[:, 3:3 + L], out_of("xT")[:, 0:L], ACT.Copy).then_inc(freeing("xT"), 1)
                        elif what == "conv0":
                            act.wait_ge(conv_ready, front + 1)
                            act.activation(hexp[:, :], hacc[:, :], ACT.Exp, scale=-1.0).then_inc(hexp_ready, 1)
                        elif what == "proj":
                            for t in range(NT):
                                act.activation(pr[:, t, :], out_of(f"proj{t}")[:, 0:NPR], ACT.Copy).then_inc(freeing(f"proj{t}"), 1)
                            moved(act, jobs, f"proj0{tag}", i)
                            moved(act, jobs, f"proj1{tag}", i)
                            act.activation(sg[:, :, :], pr[:, :, NPR - HD * DV - HD:NPR], ACT.Exp, scale=-1.0).then_inc(gexp_ready, 1)
                        elif what == "tq":
                            for t in range(NT):
                                act.activation(qkT[:, t, :, :].rearrange("p w t -> p (w t)"), out_of(f"tq{t}")[:, 0:3 * P],
                                               ACT.Copy).then_inc(freeing(f"tq{t}"), 1)

            layer(act, (ffn_turn(0), ffn_turn(1)), delta_turn, None, setup_first, setup_rest)

        @block.tensor
        def _(pe):
            pe.wait_ge(ident_ready, 1)

            def weights_turned(job, source, at, n, rows=P):
                turn(pe, setup, job, 0)
                b = setup.bank(job)
                for k in range(n):
                    last = pe.transpose(bank[b][0:rows, P * k:P * k + P], source[:, at + k, :], ident[:, :])
                last.then_inc(full[b], 1)

            def setup_first():
                pe.wait_ge(Wg_in, 2 * 16)
                weights_turned("Wg", wst, 20, 2)
                pe.wait_ge(Wv_in, 16)
                weights_turned("Wv", wst, 16, 4)
                pe.wait_ge(const_done, CONSTS)

            def setup_rest():
                pe.wait_ge(Wqk_in, 2 * 16)
                for j in (0, 2, 1, 3):
                    weights_turned(f"Wqk{j}", wst, 4 * j, 4)
                pe.wait_ge(Wo_in, 16)
                for j in range(2):
                    weights_turned(f"Wo{j}", wost, 4 * j, 4, DH)
                moved(pe, setup, "Wqk1", 0)
                moved(pe, setup, "Wqk3", 0)

            def ffn_turn(phase):
                def turn_of(jobs, i, norm, front, attend, output, part=None):
                    def out_of(name):
                        turn(pe, jobs, name, i)
                        return bank[jobs.bank(name)]

                    def done(last, name):
                        last.then_inc(full[jobs.bank(name)], 1)

                    def inputs_turned():
                        o = out_of("xT")
                        pe.wait_ge(xn_ready, 2 * front + (4 * phase * B + 2))
                        for t in range(NT):
                            last = pe.transpose(o[:, P * t:P * t + P], xn[:, t, :], ident[:, :])
                        done(last, "xT")

                    def gates():
                        moved(pe, jobs, "xT", i)
                        o = out_of("gate")
                        for t in range(NT):
                            last = pe.matmul(o[:, 2 * P * t:2 * P * t + 2 * P], xT[:, P * t:P * t + P], WgT[:, :], start=True, stop=True)
                        done(last, "gate")

                    def expert_values(t):
                        o = out_of(f"pv{t}")
                        done(pe.matmul(o[:, :], xT[:, P * t:P * t + P], WvT[:, :], start=True, stop=True), f"pv{t}")

                    def project(c):
                        o = out_of(f"qk{c}")
                        for a in range(2):
                            w, oa = NPAIR * a + c, o[:, L * a:L * a + L]
                            pe.matmul(oa, WTh[:, w, :], xTh[:, :], start=True, stop=False)
                            pe.matmul(oa, WTh[:, w, :], xTl[:, :], start=False, stop=False)
                            last = pe.matmul(oa, WTl[:, w, :], xTh[:, :], start=False, stop=True)
                        done(last, f"qk{c}")

                    def shift_scores(h):
                        o, r, c = out_of(f"S{h}"), heads(h), h // 2
                        for t in range(NT):
                            last = pe.matmul(o[:, L * t:L * t + L], qkh[r, c, 0, P * t:P * t + P], qkh[r, c, 1, :], start=True, stop=True)
                        done(last, f"S{h}")

                    def scores(h):
                        o, r, c = out_of(f"ST{h}"), heads(h), h // 2
                        for t in range(NT):
                            ot, tj = o[:, L * t:L * t + L], slice(P * t, P * t + P)
                            pe.matmul(ot, qkh[r, c, 1, tj], qkh[r, c, 0, :], start=True, stop=False)
                            pe.matmul(ot, qkh[r, c, 1, tj], qkl[r, c, 0, :], start=False, stop=False)
                            pe.matmul(ot, qkl[r, c, 1, tj], qkh[r, c, 0, :], start=False, stop=False)
                            last = pe.matmul(ot, sel[:, h, :], nmT[:, :], start=False, stop=True)
                        done(last, f"ST{h}")

                    def attended(h):
                        g = h // 2
                        o = out_of(f"at{g}") if h % 2 == 0 else bank[jobs.bank(f"at{g}")]
                        moved(pe, jobs, f"ST{h}", i)
                        for t in range(NT):
                            ot = o[:, (2 * (h % 2) + t) * DV1:(2 * (h % 2) + t + 1) * DV1]
                            for tj in range(NT):
                                last = pe.matmul(ot, PT[:, h % 4, tj, P * t:P * t + P], v[:, H * tj + h, :],
                                                 start=(tj == 0), stop=(tj == NT - 1))
                        if h % 2:
                            done(last, f"at{g}")

                    def front_step(what):
                        name, c = what if isinstance(what, tuple) else (what, None)
                        if what == "xT":
                            inputs_turned()
                        elif what == "gate":
                            gates()
                        elif what in ("pv0", "pv1"):
                            expert_values(int(what[2]))
                        elif name == "qk":
                            if c == 0:
                                pe.wait_ge(xlo_ready, front + (phase * B + 1))
                            project(c)
                        elif name == "shift":
                            pe.wait_ge(qkhi_ready, NPAIR * front + (NPAIR * phase * B + c + 1))
                            shift_scores(2 * c)
                            shift_scores(2 * c + 1)
                        elif name[0:4] == "vmix":
                            j = int(name[4])
                            if j == 0:
                                pe.wait_ge(pvT_ready, front + (phase * B + 1))
                            pe.wait_ge(bdv_ready, 4 * front + (4 * phase * B + j + 1))
                            o = out_of(name)
                            for k in range(8):
                                last = pe.matmul(o[:, DH * k:DH * k + DH], bdv[:, 8 * j + k, :, :].rearrange("p m h -> p (m h)"),
                                                 pvT[:, 8 * j + k, :], start=True, stop=True)
                            done(last, name)
                        elif what == "mT":
                            o = out_of("mT")
                            all_moved(pe, jobs, [f"S{h}" for h in range(H)], i, but=jobs.bank("mT"))
                            for t in range(NT):
                                last = pe.transpose(o[0:H, P * t:P * t + P], negm[:, t, :], ident[:, :])
                            done(last, "mT")

                    def output_step(what):
                        if what[0:4] == "omix":
                            j = int(what[4])
                            if j == 0:
                                pe.wait_ge(aT_ready, output + (phase * B + 1))
                            pe.wait_ge(bdo_ready, 4 * output + (4 * phase * B + j + 1))
                            o = out_of(what)
                            for k in range(8):
                                last = pe.matmul(o[0:DH, DH * k:DH * k + DH], aT[:, 8 * j + k, :],
                                                 bdo[:, 8 * j + k, :, :].rearrange("p m e -> p (m e)"), start=True, stop=True)
                            done(last, what)
                        elif what == "res":
                            o = out_of("res")
                            all_moved(pe, jobs, [f"omix{j}" for j in range(4)], i, but=jobs.bank("res"))
                            for t in range(NT):
                                for e in range(E):
                                    last = pe.matmul(o[:, C * t:C * t + C], yT[:, t, e, :, :].rearrange("d q l -> d (q l)"), WoT[:, e, :],
                                                     start=(e == 0), stop=(e == E - 1))
                            done(last, "res")

                    for stage, what in FFN_ORDER:
                        if part is not None and what not in part:
                            continue
                        name, c = what if isinstance(what, tuple) else (what, None)
                        if stage == "front" and front is not None:
                            front_step(what)
                        elif stage == "output" and output is not None:
                            output_step(what)
                        elif stage == "attend" and attend is not None:
                            if name == "scores":
                                scores(2 * c)
                                scores(2 * c + 1)
                            elif name == "values":
                                if c == 0:
                                    pe.wait_ge(v_ready, attend + (phase * B + 1))
                                attended(2 * c)
                                attended(2 * c + 1)
                    if front is not None and (part is None or "mT" in part):
                        all_moved(pe, jobs, [f"qk{c}" for c in range(NPAIR)] + ["mT"], i)
                return turn_of

            def delta_turn(jobs, i, tag, inverse, scan, front, s, part=None):
                def out_of(job):
                    turn(pe, jobs, job + tag, i)
                    return bank[jobs.bank(job + tag)]

                def done(last, job):
                    last.then_inc(full[jobs.bank(job + tag)], 1)

                def wait_moved(job):
                    moved(pe, jobs, job + tag, i)

                def inverse_step(what):
                    AA, XX, qkp, vb = AA_of[s], XX_of[s], qkp_of[s], vb_of[s]
                    if what == "WT":
                        wait_moved(f"V{LEVELS - 1}0")
                        wait_moved(f"V{LEVELS - 1}1")
                        o = out_of("WT")
                        for t in range(NT):
                            for h in range(HD):
                                last = pe.matmul(o[DP * h:DP * h + DP, P * t:P * t + P], qkp[:, t, 1, h, :], XX[:, HD * t + h, 1, :],
                                                 start=True, stop=True)
                        done(last, "WT")
                    elif what == "Uv":
                        o = out_of("Uv")
                        for t in range(NT):
                            for h in range(HD):
                                last = pe.matmul(o[:, P * t + DV * h:P * t + DV * h + DV], XX[:, HD * t + h, 1, :],
                                                 vb[:, t, DV * h:DV * h + DV], start=True, stop=True)
                        done(last, "Uv")
                    else:
                        w, k, t = what
                        if w == "T":
                            if k == 1:
                                pe.wait_ge(X0_ready, 2 * inverse + (t + 1))
                            else:
                                wait_moved(f"U{k - 1}{t}")
                                wait_moved(f"V{k - 1}{t}")
                        elif w == "U" or k == LEVELS - 1:
                            wait_moved(f"T{k}{t}")
                        o = out_of(f"{w}{k}{t}")
                        for h in range(HD):
                            a, xx, n = AA[:, HD * t + h, 0, :], XX[:, HD * t + h, :, :], TT[:, t, h, :]
                            left, right = {"T": (a, xx[:, 0, :]), "U": (xx[:, 1, :], n), "V": (n, xx[:, 1, :])}[w]
                            last = pe.matmul(o[:, P * h:P * h + P], left, right, start=True, stop=True)
                        done(last, f"{w}{k}{t}")

                def scan_step(what):
                    AA, qkp, qkT = AA_of[1 - s], qkp_of[1 - s], qkT_of[1 - s]
                    if what[0] == "S":
                        c = int(what[1])
                        t, r = (c - 1) // 2, slice(CH * ((c - 1) % 2), CH * ((c - 1) % 2) + CH)
                        pe.wait_ge(U_ready, 4 * scan + c)
                        o = out_of(what)
                        done(pe.matmul(o[:, 0:P], qkp[r, t, 0, :, :].rearrange("p h d -> p (h d)"), U[r, t, :],
                                       start=(c == 1), stop=(c == 2 * NT - 1), skip_group_check=True), what)
                    elif what[0:2] == "ws":
                        c = int(what[2])
                        wait_moved(f"S{c}")
                        o, r = out_of(what), slice(CH * (c % 2), CH * (c % 2) + CH)
                        done(pe.matmul(o[r, 0:P], WT[:, CH * c:CH * c + CH], St[:, c, :], start=True, stop=True), what)
                    elif what == "out":
                        pe.wait_ge(U_ready, 4 * scan + 4)
                        for t in range(NT):
                            o = out_of(f"o{t}")
                            for half in range(2):
                                pe.matmul(o[CH * half:CH * half + CH, 0:P], qkT[:, t, 2, CH * half:CH * half + CH], St[:, 2 * t + half, :],
                                          start=True, stop=False, skip_group_check=True)
                            for h in range(HD):
                                last = pe.matmul(o[:, DV * h:DV * h + DV], AA[:, HD * t + h, 1, :], U[:, t, DV * h:DV * h + DV],
                                                 start=False, stop=True, skip_group_check=True)
                            done(last, f"o{t}")
                    elif what == "turn":
                        pe.wait_ge(y_ready, scan + 1)
                        o = out_of("yT")
                        for t in range(NT):
                            last = pe.transpose(o[:, P * t:P * t + P], y[:, t, :], ident[:, :])
                        done(last, "yT")
                    elif what == "residual":
                        wait_moved("yT")
                        o = out_of("fin")
                        for t in range(NT):
                            last = pe.matmul(o[:, C * t:C * t + C], yT_d[:, P * t:P * t + P], dWo_sb[:, :], start=True, stop=True)
                        done(last, "fin")

                def front_step(what):
                    qkp, qkT = qkp_of[1 - s], qkT_of[1 - s]
                    if what == "xT":
                        pe.wait_ge(xn_ready, 2 * front + (2 * B + 2))
                        o = out_of("xT")
                        for t in range(NT):
                            last = pe.transpose(o[:, P * t:P * t + P], xn[:, t, :], ident[:, :])
                        done(last, "xT")
                    elif what == "proj":
                        pe.wait_ge(hT_ready, front + 1)
                        for t in range(NT):
                            o = out_of(f"proj{t}")
                            done(pe.matmul(o[:, 0:NPR], hT[:, P * t:P * t + P], dW[:, :], start=True, stop=True), f"proj{t}")
                    elif what == "tq":
                        pe.wait_ge(qkp_ready, front + 1)
                        for t in range(NT):
                            o = out_of(f"tq{t}")
                            for w in range(3):
                                last = pe.transpose(o[:, P * w:P * w + P], qkp[:, t, w, :, :].rearrange("p h d -> p (h d)"), ident[:, :])
                            done(last, f"tq{t}")
                    elif what.startswith("gram"):
                        t, h = int(what[4]), int(what[5])
                        if h == 0:
                            wait_moved(f"tq{t}")
                        o, r = out_of(what), slice(DP * h, DP * h + DP)
                        done(pe.matmul(o[:, 0:2 * P], qkT[r, t, 0, :], qkT[r, t, 1:3, :].rearrange("p w t -> p (w t)"),
                                       start=True, stop=True), what)

                for stage, what in DELTA_ORDER:
                    if part is not None and what not in part:
                        continue
                    if stage == "inverse" and inverse is not None:
                        inverse_step(what)
                    elif stage == "scan" and scan is not None:
                        scan_step(what)
                    elif stage == "front" and front is not None:
                        front_step(what)
                if inverse is not None and (part is None or "WT" in part):
                    wait_moved("WT")

            layer(pe, (ffn_turn(0), ffn_turn(1)), delta_turn, None, setup_first, setup_rest)


_INS = ["L0_attn_hidden_states", "L0_attn_conv_w", "L0_attn_Wq", "L0_attn_Wk", "L0_attn_Wv", "L0_attn_Wb", "L0_attn_Wg",
        "L0_attn_norm_w", "L0_attn_Wo", "L0_ffn_Wq", "L0_ffn_Wk", "L0_ffn_Wv", "L0_ffn_Ws", "L0_ffn_Wd", "L0_ffn_Wo"]


def kernel(**inputs):
    import numpy as np
    import concourse.bacc as bacc
    from concourse.bass_utils import run_bass_kernel_spmd as run

    nc = bacc.Bacc("TRN2", target_bir_lowering=False, num_devices=1)
    arrays, args = {}, []
    for name in _INS:
        a = np.ascontiguousarray(inputs[name])
        arrays[name] = a
        args.append(nc.dram_tensor(name, a.shape, mybir.dt.from_np(a.dtype), kind="ExternalInput").ap())
    args.append(nc.dram_tensor("out", (B, L, C), F32, kind="ExternalOutput").ap())
    build(nc, *args)
    r = run(nc, [arrays], core_ids=[0])
    return r.results[0]["out"]
```
